# Optimizing a Trainium2 kernel written in Bass

```python
import numpy as np
import jax
import jax.numpy as jnp

def _softmax(x, axis=-1):
    return jax.nn.softmax(x, axis=axis)

def _gelu(x):
    return jax.nn.gelu(x, approximate=True)

def _silu(x):
    return jax.nn.silu(x)

def _sigmoid(x):
    return jax.nn.sigmoid(x)

def _layernorm(x, axis=-1, eps=1e-05):
    m = jnp.mean(x, axis=axis, keepdims=True)
    v = jnp.var(x, axis=axis, keepdims=True)
    return (x - m) / jnp.sqrt(v + eps)

def _scatter_add(tgt, idx, src, axis=0):
    return tgt.at[idx].add(src)

def _segment_sum(src, seg, n):
    return jax.ops.segment_sum(src, seg, n)
kernel_name = 'mk_gnn_preln_d4_gnn_r32_7c934a'

def setup_inputs(seed: int=0):
    np.random.seed(seed)
    _w = jnp.asarray

    def _rec_inputs():
        import jax
        import jax.numpy as jnp
        _gk = jax.random.key(seed)
        x = -0.000202 + 1 * jax.random.normal(jax.random.fold_in(_gk, 1), (3125, 64), jnp.float32)
        _s = jax.random.randint(jax.random.fold_in(_gk, 2), (25000,), 0, 3125, jnp.int32)
        _d = jax.random.randint(jax.random.fold_in(_gk, 3), (25000,), 0, 3125, jnp.int32)
        _loop = jnp.arange(3125, dtype=jnp.int32)
        src = jnp.concatenate([_s, _d, _loop])
        dst = jnp.concatenate([_d, _s, _loop])
        _o = jnp.argsort(dst, stable=True)
        src = src[_o]
        dst = dst[_o]
        edge_attr_32 = 0.000196303 + 1.00016 * jax.random.normal(jax.random.fold_in(_gk, 12), (53125, 32), jnp.float32)
        return (x, src, dst, edge_attr_32)
    x, src, dst, edge_attr_32 = _rec_inputs()

    def _L0_gnn_setup():
        import jax, jax.numpy as jnp
        import numpy as np
        N_NODES = 3125
        N_EDGES = 50000
        D = 64

        def _sage_layer(h, src, dst, W_self, W_neigh, b, n_nodes):
            msg = h[src]
            agg = jax.ops.segment_sum(msg, dst, num_segments=n_nodes)
            deg = jax.ops.segment_sum(jnp.ones((src.shape[0], 1), h.dtype), dst, num_segments=n_nodes)
            h_neigh = agg / jnp.maximum(deg, 1.0)
            return h @ W_self + h_neigh @ W_neigh + b
        key = jax.random.key(seed)
        ks = jax.random.split(key, 9)
        x = jax.random.normal(ks[0], (N_NODES, D), dtype=jnp.float32)
        src = jax.random.randint(ks[1], (N_EDGES,), 0, N_NODES, dtype=jnp.int64)
        dst = jax.random.randint(ks[2], (N_EDGES,), 0, N_NODES, dtype=jnp.int64)
        s = 1.0 / np.sqrt(D)
        W_self1 = jax.random.normal(ks[3], (D, D), dtype=jnp.float32) * s
        W_neigh1 = jax.random.normal(ks[4], (D, D), dtype=jnp.float32) * s
        b1 = jnp.zeros((D,), dtype=jnp.float32)
        W_self2 = jax.random.normal(ks[5], (D, D), dtype=jnp.float32) * s
        W_neigh2 = jax.random.normal(ks[6], (D, D), dtype=jnp.float32) * s
        b2 = jnp.zeros((D,), dtype=jnp.float32)
        return {'x': x, 'src': src, 'dst': dst, 'W_self1': W_self1, 'W_neigh1': W_neigh1, 'b1': b1, 'W_self2': W_self2, 'W_neigh2': W_neigh2, 'b2': b2}
    _L0_gnn_all = _L0_gnn_setup()
    _L0_gnn_in = {k: v for k, v in _L0_gnn_all.items() if k in ('W_self1', 'W_neigh1', 'b1', 'W_self2', 'W_neigh2', 'b2')}
    del _L0_gnn_all

    def _L1_gnn_setup():
        import jax, jax.numpy as jnp
        import numpy as np
        N_NODES = 3125
        N_EDGES = 50000
        D_IN = 64
        D_HID = 64
        key = jax.random.key(seed)
        k_x, k_e, k_wl, k_wr, k_b = jax.random.split(key, 5)
        x = jax.random.normal(k_x, (N_NODES, D_IN), dtype=jnp.float32)
        edge_index = jax.random.randint(k_e, (2, N_EDGES), 0, N_NODES, dtype=jnp.int64)
        scale = 1.0 / np.sqrt(D_IN)
        W_l = jax.random.uniform(k_wl, (D_IN, D_HID), jnp.float32, -scale, scale)
        W_r = jax.random.uniform(k_wr, (D_IN, D_HID), jnp.float32, -scale, scale)
        b = jax.random.uniform(k_b, (D_HID,), jnp.float32, -scale, scale)
        return {'x': x, 'edge_index': edge_index, 'W_l': W_l, 'W_r': W_r, 'b': b}
    _L1_gnn_all = _L1_gnn_setup()
    _L1_gnn_in = {k: v for k, v in _L1_gnn_all.items() if k in ('W_l', 'W_r', 'b')}
    del _L1_gnn_all

    def _L2_gnn_setup():
        import jax, jax.numpy as jnp
        import numpy as np
        EPS = 0.001

        def _cheb_edge_weights(edge_index, n_nodes):
            row, col = (edge_index[0], edge_index[1])
            mask = (row != col).astype(jnp.float32)
            deg = jax.ops.segment_sum(mask, row, num_segments=n_nodes)
            dinv = jnp.where(deg > 0, jax.lax.rsqrt(jnp.maximum(deg, 1.0)), 0.0)
            return -dinv[row] * dinv[col] * mask

        def _instance_norm(x, gamma, beta):
            m = jnp.mean(x)
            v = jnp.mean(jnp.square(x - m))
            return (x - m) * jax.lax.rsqrt(v + EPS) * gamma + beta
        key = jax.random.key(seed)
        ks = jax.random.split(key, 4)
        N, E, C, D = (50000, 25000, 64, 3)
        x = jax.random.normal(ks[0], (N, C), jnp.float32)
        edge_index = jax.random.randint(ks[1], (2, E), 0, N, jnp.int32)
        W0 = jax.random.normal(ks[2], (D, C, C), jnp.float32) * 0.05
        W1 = jax.random.normal(ks[3], (D, C, C), jnp.float32) * 0.05
        b = jnp.zeros((D, C), jnp.float32)
        gamma = jnp.ones((D,), jnp.float32)
        beta = jnp.zeros((D,), jnp.float32)
        return {'x': x, 'edge_index': edge_index, 'W0': W0, 'W1': W1, 'b': b, 'gamma': gamma, 'beta': beta}
    _L2_gnn_all = _L2_gnn_setup()
    _L2_gnn_in = {k: v for k, v in _L2_gnn_all.items() if k in ('W0', 'W1', 'b', 'gamma', 'beta')}
    del _L2_gnn_all

    def _L3_gnn_setup():
        import jax, jax.numpy as jnp
        import numpy as np
        N, D, E, ED, L = (3125, 64, 25000, 32, 5)
        LN_EPS = 1e-05

        def _leaky(x):
            return jax.nn.leaky_relu(x, negative_slope=0.1)
        key = jax.random.key(seed)
        ks = jax.random.split(key, 16)
        s = 0.05
        return {'x': jax.random.normal(ks[0], (N, D), dtype=jnp.float32), 'edge_index': jax.random.randint(ks[1], (2, E), 0, N, dtype=jnp.int64), 'edge_attr': jax.random.normal(ks[2], (E, ED), dtype=jnp.float32), 'W1': jax.random.normal(ks[3], (L, D, 2 * D), dtype=jnp.float32) * s, 'b1': jnp.zeros((L, 2 * D), dtype=jnp.float32), 'W2': jax.random.normal(ks[4], (L, 2 * D, D), dtype=jnp.float32) * s, 'b2': jnp.zeros((L, D), dtype=jnp.float32), 'We1': jax.random.normal(ks[5], (L, ED, D), dtype=jnp.float32) * s, 'be1': jnp.zeros((L, D), dtype=jnp.float32), 'We2': jax.random.normal(ks[6], (L, D, D), dtype=jnp.float32) * s, 'be2': jnp.zeros((L, D), dtype=jnp.float32), 'res_w': jnp.ones((L,), dtype=jnp.float32), 'dot_scale': jnp.ones((L,), dtype=jnp.float32), 'ln_g': jnp.ones((L, D), dtype=jnp.float32), 'ln_b': jnp.zeros((L, D), dtype=jnp.float32)}
    _L3_gnn_all = _L3_gnn_setup()
    _L3_gnn_in = {k: v for k, v in _L3_gnn_all.items() if k in ('W1', 'b1', 'W2', 'b2', 'We1', 'be1', 'We2', 'be2', 'res_w', 'dot_scale', 'ln_g', 'ln_b')}
    del _L3_gnn_all
    return {'x': x, 'src': src, 'dst': dst, 'edge_attr_32': edge_attr_32, 'L0_gnn_W_self1': _L0_gnn_in['W_self1'], 'L0_gnn_W_neigh1': _L0_gnn_in['W_neigh1'], 'L0_gnn_b1': _L0_gnn_in['b1'], 'L0_gnn_W_self2': _L0_gnn_in['W_self2'], 'L0_gnn_W_neigh2': _L0_gnn_in['W_neigh2'], 'L0_gnn_b2': _L0_gnn_in['b2'], 'L1_gnn_W_l': _L1_gnn_in['W_l'], 'L1_gnn_W_r': _L1_gnn_in['W_r'], 'L1_gnn_b': _L1_gnn_in['b'], 'L2_gnn_W0': _L2_gnn_in['W0'], 'L2_gnn_W1': _L2_gnn_in['W1'], 'L2_gnn_b': _L2_gnn_in['b'], 'L2_gnn_gamma': _L2_gnn_in['gamma'], 'L2_gnn_beta': _L2_gnn_in['beta'], 'L3_gnn_W1': _L3_gnn_in['W1'], 'L3_gnn_b1': _L3_gnn_in['b1'], 'L3_gnn_W2': _L3_gnn_in['W2'], 'L3_gnn_b2': _L3_gnn_in['b2'], 'L3_gnn_We1': _L3_gnn_in['We1'], 'L3_gnn_be1': _L3_gnn_in['be1'], 'L3_gnn_We2': _L3_gnn_in['We2'], 'L3_gnn_be2': _L3_gnn_in['be2'], 'L3_gnn_res_w': _L3_gnn_in['res_w'], 'L3_gnn_dot_scale': _L3_gnn_in['dot_scale'], 'L3_gnn_ln_g': _L3_gnn_in['ln_g'], 'L3_gnn_ln_b': _L3_gnn_in['ln_b']}

def reference(x, src, dst, edge_attr_32, L0_gnn_W_self1, L0_gnn_W_neigh1, L0_gnn_b1, L0_gnn_W_self2, L0_gnn_W_neigh2, L0_gnn_b2, L1_gnn_W_l, L1_gnn_W_r, L1_gnn_b, L2_gnn_W0, L2_gnn_W1, L2_gnn_b, L2_gnn_gamma, L2_gnn_beta, L3_gnn_W1, L3_gnn_b1, L3_gnn_W2, L3_gnn_b2, L3_gnn_We1, L3_gnn_be1, L3_gnn_We2, L3_gnn_be2, L3_gnn_res_w, L3_gnn_dot_scale, L3_gnn_ln_g, L3_gnn_ln_b):
    import jax
    import jax.numpy as jnp

    def _L0_gnn_ref(x, src, dst, W_self1, W_neigh1, b1, W_self2, W_neigh2, b2):
        import jax, jax.numpy as jnp
        import numpy as np
        N_NODES = 3125
        N_EDGES = 50000
        D = 64

        def _sage_layer(h, src, dst, W_self, W_neigh, b, n_nodes):
            msg = h[src]
            agg = jax.ops.segment_sum(msg, dst, num_segments=n_nodes)
            deg = jax.ops.segment_sum(jnp.ones((src.shape[0], 1), h.dtype), dst, num_segments=n_nodes)
            h_neigh = agg / jnp.maximum(deg, 1.0)
            return h @ W_self + h_neigh @ W_neigh + b
        n = x.shape[0]
        h = _sage_layer(x, src, dst, W_self1, W_neigh1, b1, n)
        h = _sage_layer(h, src, dst, W_self2, W_neigh2, b2, n)
        return h

    def _L1_gnn_ref(x, edge_index, W_l, W_r, b):
        import jax, jax.numpy as jnp
        import numpy as np
        N_NODES = 3125
        N_EDGES = 50000
        D_IN = 64
        D_HID = 64
        src = edge_index[0]
        dst = edge_index[1]
        n = x.shape[0]
        msg = x[src]
        s = jax.ops.segment_sum(msg, dst, num_segments=n)
        cnt = jax.ops.segment_sum(jnp.ones((src.shape[0],), x.dtype), dst, num_segments=n)
        agg = s / jnp.maximum(cnt, 1.0)[:, None]
        out = agg @ W_l + x @ W_r + b
        return jax.nn.relu(out)

    def _L2_gnn_ref(x, edge_index, W0, W1, b, gamma, beta):
        import jax, jax.numpy as jnp
        import numpy as np
        EPS = 0.001

        def _cheb_edge_weights(edge_index, n_nodes):
            row, col = (edge_index[0], edge_index[1])
            mask = (row != col).astype(jnp.float32)
            deg = jax.ops.segment_sum(mask, row, num_segments=n_nodes)
            dinv = jnp.where(deg > 0, jax.lax.rsqrt(jnp.maximum(deg, 1.0)), 0.0)
            return -dinv[row] * dinv[col] * mask

        def _instance_norm(x, gamma, beta):
            m = jnp.mean(x)
            v = jnp.mean(jnp.square(x - m))
            return (x - m) * jax.lax.rsqrt(v + EPS) * gamma + beta
        n = x.shape[0]
        row, col = (edge_index[0], edge_index[1])
        w = _cheb_edge_weights(edge_index, n)
        depth = W0.shape[0]
        x1 = None
        for i in range(depth):
            Tx1 = jax.ops.segment_sum(w[:, None] * x[row], col, num_segments=n)
            x = x @ W0[i].T + Tx1 @ W1[i].T + b[i]
            x = _instance_norm(x, gamma[i], beta[i])
            if i == 0:
                x1 = x
            elif i < depth - 1:
                x = jax.nn.relu(x)
        return jax.nn.relu((x + x1) / 2)

    def _L3_gnn_ref(x, edge_index, edge_attr, W1, b1, W2, b2, We1, be1, We2, be2, res_w, dot_scale, ln_g, ln_b):
        import jax, jax.numpy as jnp
        import numpy as np
        N, D, E, ED, L = (3125, 64, 25000, 32, 5)
        LN_EPS = 1e-05

        def _leaky(x):
            return jax.nn.leaky_relu(x, negative_slope=0.1)
        src, dst = (edge_index[0], edge_index[1])
        n = x.shape[0]
        for l in range(W1.shape[0]):
            h = _leaky(x @ W1[l] + b1[l]) @ W2[l] + b2[l]
            e = _leaky(edge_attr @ We1[l] + be1[l]) @ We2[l] + be2[l]
            msg = h[src] * e * dot_scale[l]
            agg = jax.ops.segment_sum(msg, dst, num_segments=n)
            out = x + agg * res_w[l]
            mu = jnp.mean(out, axis=-1, keepdims=True)
            var = jnp.mean(jnp.square(out - mu), axis=-1, keepdims=True)
            x = (out - mu) * jax.lax.rsqrt(var + LN_EPS) * ln_g[l] + ln_b[l]
        return x
    edge_index = jnp.stack([src, dst])
    h = jnp.maximum(_layernorm(x, axis=-1), 0.0)
    x = x + _L0_gnn_ref(h, src, dst, L0_gnn_W_self1, L0_gnn_W_neigh1, L0_gnn_b1, L0_gnn_W_self2, L0_gnn_W_neigh2, L0_gnn_b2)
    h = jnp.maximum(_layernorm(x, axis=-1), 0.0)
    x = x + _L1_gnn_ref(h, edge_index, L1_gnn_W_l, L1_gnn_W_r, L1_gnn_b)
    h = jnp.maximum(_layernorm(x, axis=-1), 0.0)
    x = x + _L2_gnn_ref(h, edge_index, L2_gnn_W0, L2_gnn_W1, L2_gnn_b, L2_gnn_gamma, L2_gnn_beta)
    h = jnp.maximum(_layernorm(x, axis=-1), 0.0)
    x = x + _L3_gnn_ref(h, edge_index, edge_attr_32, L3_gnn_W1, L3_gnn_b1, L3_gnn_W2, L3_gnn_b2, L3_gnn_We1, L3_gnn_be1, L3_gnn_We2, L3_gnn_be2, L3_gnn_res_w, L3_gnn_dot_scale, L3_gnn_ln_g, L3_gnn_ln_b)
    return x

_drawn_inputs = setup_inputs


def setup_inputs(seed=0):
    import zlib

    import numpy as np

    out = dict(_drawn_inputs(seed))
    spreads = {'L0_gnn_b1': (0.0, 0.1),
     'L0_gnn_b2': (0.0, 0.1),
     'L2_gnn_b': (0.0, 0.1),
     'L2_gnn_gamma': (1.0, 0.2),
     'L2_gnn_beta': (0.0, 0.355),
     'L3_gnn_b1': (0.0, 0.1),
     'L3_gnn_b2': (0.0, 0.1),
     'L3_gnn_be1': (0.0, 0.1),
     'L3_gnn_be2': (0.0, 0.1),
     'L3_gnn_res_w': (1.0, 0.2),
     'L3_gnn_dot_scale': (1.0, 0.2),
     'L3_gnn_ln_g': (1.0, 0.2),
     'L3_gnn_ln_b': (0.0, 0.1)}
    factors = {}
    for name, (base, spread) in spreads.items():
        noise = np.random.default_rng([zlib.crc32(name.encode()), seed]).standard_normal(out[name].shape)
        drawn = base * np.exp(spread * noise) if base else spread * noise
        out[name] = jnp.asarray(drawn.astype(out[name].dtype))
    for name, factor in factors.items():
        out[name] = (out[name] * factor).astype(out[name].dtype)
    return out
```

```python
import concourse.bass as bass
from concourse import mybir
from contextlib import ExitStack

NODES, D, EDGES, ED, LAYERS = 3125, 64, 53125, 32, 5
P = 128
NB = -(-NODES // P)
NPAD = NB * P
TILES = -(-EDGES // P)
EPAD = TILES * P
QUAD = 4
QUADS = TILES // QUAD
SLOTS = 4
ROUNDS = QUADS // SLOTS
BANK = 512
STAGES = 2 + 1 + 3 + LAYERS
LAST_BLOCK = NODES - (NB - 1) * P
ROWS = TILES // 4
PAIRS = (NB + 1) // 2
assert TILES % (QUAD * SLOTS) == 0


def gnn_program(nc, x, src_t, dst_t, dst_r, attr_t, w_self1, w_neigh1, b_1, w_self2, w_neigh2, b_2,
                w_l, w_r, b_m, w0_t, w1_t, b_c, gamma, beta, w1, b1_t, w2, b2, we1, be1_t, we2, be2,
                res_w, dot_scale, ln_g, ln_b, out):
    f32, i32, bf16 = mybir.dt.float32, mybir.dt.int32, mybir.dt.bfloat16
    ALU, ACT, AX = mybir.AluOpType, mybir.ActivationFunctionType, mybir.AxisListType
    ctx = ExitStack()
    with ctx:
        def sb(name, shape, dt=f32):
            return ctx.enter_context(nc.sbuf_tensor(name, shape, dt))

        def sem(name):
            return ctx.enter_context(nc.semaphore(name))

        def bc(ap, axis, n):
            a = ap.unsqueeze(axis)
            shape = list(a.shape)
            shape[axis] = n
            return a.to_broadcast(shape)

        table = nc.dram_tensor("table", (NPAD, D), f32, kind="Internal").ap()
        tile_range = nc.dram_tensor("tile_range", (2, TILES), f32, kind="Internal").ap()

        idx_all = sb("idx_all", [P, TILES], i32)
        src_i = sb("src_i", [P, TILES], i32)
        dst_i = sb("dst_i", [P, TILES], i32)
        tmp_i = sb("tmp_i", [P, TILES], i32)
        src_f = sb("src_f", [P, TILES])
        dst_f = sb("dst_f", [P, TILES])
        not_loop = sb("not_loop", [P, TILES])
        dst_lo = sb("dst_lo", [P, TILES])
        dst_hi = sb("dst_hi", [P, TILES])
        src_lo = sb("src_lo", [P, TILES])
        src_hi = sb("src_hi", [P, TILES])
        out_hi = sb("out_hi", [P, TILES])
        dstr_i = sb("dstr_i", [ROWS, 4, P], i32)
        dstr_b = sb("dstr_b", [ROWS, 4, P], i32)
        dstr_f = sb("dstr_f", [ROWS, 4, P])
        low_r = sb("low_r", [ROWS, 4])
        high_r = sb("high_r", [ROWS, 4])
        first_block = sb("first_block", [P, TILES])
        last_block = sb("last_block", [P, TILES])
        bank_of = sb("bank_of", [P, TILES])
        cmp = sb("cmp", [P, TILES])
        window_f = sb("window_f", [P, TILES])
        window_at = sb("window_at", [P, TILES], i32)
        spread = sb("spread", [P, 1])
        spread_i = sb("spread_i", [P, 1], i32)
        MASKS = 2 * PAIRS
        masks = sb("masks", [P, TILES, MASKS])
        iota_lo = sb("iota_lo", [P, P])
        iota_hi = sb("iota_hi", [P, MASKS])
        idx_slot = sb("idx_slot", [P, SLOTS * QUAD], i32)
        rows = sb("rows", [P, SLOTS, QUAD, D])
        onehot = sb("onehot", [P, 2, QUAD, P])
        onehot_src = sb("onehot_src", [P, 2, QUAD, P])
        hot_hi = sb("hot_hi", [P, 2, 2, QUAD, MASKS])
        masked = sb("masked", [P, 2, QUAD, 2, D])
        msg = sb("msg", [P, 2, QUAD, 2, D])
        attr = sb("attr", [ED, SLOTS, QUAD * P])
        act_e = sb("act_e", [P, 2, QUAD * P])

        X = sb("X", [P, NB, D])
        H = sb("H", [P, NB, D])
        S0 = sb("S0", [P, NB, D])
        X1 = sb("X1", [P, NB, D])
        cat = sb("cat", [P, NB, 2 * D])
        XT = sb("XT", [P, NPAD])
        hid_z = sb("hid_z", [P, 2, BANK])
        hid = sb("hid", [P, 2, BANK])
        stat = sb("stat", [P, 8, NB])
        real = sb("real", [P, NB])
        rdeg = sb("rdeg", [P, NB])
        dinv = sb("dinv", [P, NB])
        ndinv = sb("ndinv", [P, NB])
        ident = sb("ident", [P, P])
        ones = sb("ones", [P, P])
        part = sb("part", [P, 8])
        eps5 = sb("eps5", [P, 1])
        eps3 = sb("eps3", [P, 1])
        zero = sb("zero", [P, 1])

        Wp = sb("Wp", [P, 6, D])
        Bp = sb("Bp", [P, 6, D])
        gam = sb("gam", [P, 3])
        bet = sb("bet", [P, 3])
        W1 = sb("W1", [D, LAYERS, 2 * D])
        B1 = sb("B1", [P, LAYERS])
        W2 = sb("W2", [P, LAYERS, D])
        B2 = sb("B2", [P, LAYERS, D])
        WE1 = sb("WE1", [ED, LAYERS, 2, D])
        BE1 = sb("BE1", [P, LAYERS])
        WE2 = sb("WE2", [P, LAYERS, 2, D])
        BE2 = sb("BE2", [P, LAYERS, D])
        BE2r = sb("BE2r", [P, LAYERS, D])
        BE2p = sb("BE2p", [P, 3, LAYERS, D], bf16)
        BE2s = sb("BE2s", [P, LAYERS, D], bf16)
        pick = sb("pick", [P, P], bf16)
        RW = sb("RW", [P, LAYERS])
        DS = sb("DS", [P, LAYERS])
        LG = sb("LG", [P, LAYERS, D])
        LB = sb("LB", [P, LAYERS, D])

        agg_ps = ctx.enter_context(nc.psum_tensor("agg_ps", [P, 4 * BANK], f32))
        z_ps = ctx.enter_context(nc.psum_tensor("z_ps", [P, 2, BANK], f32))
        e_ps = ctx.enter_context(nc.psum_tensor("e_ps", [P, 2, BANK], f32))

        loaded = sem("loaded")
        range_out = sem("range_out")
        range_in = sem("range_in")
        consts = sem("consts")
        flag_ready = sem("flag_ready")
        dve = sem("dve")
        hist_hot = sem("hist_hot")
        hist_done = sem("hist_done")
        table_due = sem("table_due")
        table_in = sem("table_in")
        idx_ready = sem("idx_ready")
        idx_seen = sem("idx_seen")
        gathered = [sem(f"gathered{j}") for j in range(SLOTS)]
        masked_ready = sem("masked_ready")
        hot_ready = sem("hot_ready")
        msg_ready = sem("msg_ready")
        scattered = sem("scattered")
        cleared = sem("cleared")
        attr_in = [sem(f"attr_in{j}") for j in range(SLOTS)]
        z_ready = sem("z_ready")
        acted = sem("acted")
        e_ready = sem("e_ready")
        node_in = sem("node_in")
        turned = sem("turned")
        xt_ready = sem("xt_ready")
        hid_ps_ready = sem("hid_ps_ready")
        hid_z_ready = sem("hid_z_ready")
        hid_ready = sem("hid_ready")
        projected = sem("projected")
        sum_in = sem("sum_in")
        summed = sem("summed")
        root_in = sem("root_in")
        rooted = sem("rooted")
        out_due = sem("out_due")
        written = sem("written")

        NQ = -(-NB // QUAD)
        dims = lambda g: (g * QUAD, min(QUAD, NB - g * QUAD))
        weights = [
            (Wp[0:D, 0, :], w_self1), (Wp[D:P, 0, :], w_neigh1), (Wp[0:D, 1, :], w_self2), (Wp[D:P, 1, :], w_neigh2),
            (Wp[0:D, 2, :], w_r), (Wp[D:P, 2, :], w_l),
            (Wp[0:D, 3:6, :], w0_t.rearrange("i a b -> a i b")), (Wp[D:P, 3:6, :], w1_t.rearrange("i a b -> a i b")),
            (Bp[:, 0, :], b_1.partition_broadcast(P)), (Bp[:, 1, :], b_2.partition_broadcast(P)),
            (Bp[:, 2, :], b_m.partition_broadcast(P)),
            (Bp[:, 3:6, :], b_c.partition_broadcast(P)),
            (gam[:, :], gamma.partition_broadcast(P)), (bet[:, :], beta.partition_broadcast(P)),
            (W1[:, :, :], w1.rearrange("l a b -> a l b")), (B1[:, :], b1_t),
            (W2[:, :, :], w2.rearrange("l a b -> a l b")), (B2[:, :, :], b2.partition_broadcast(P)),
            (WE1[:, :, 0, :], we1.rearrange("l a b -> a l b")), (WE1[:, :, 1, :], we1.rearrange("l a b -> a l b")),
            (BE1[0:D, :], be1_t), (BE1[D:P, :], be1_t),
            (WE2[0:D, :, 0, :], we2.rearrange("l a b -> a l b")), (WE2[0:D, :, 1, :], we2.rearrange("l a b -> a l b")),
            (WE2[D:P, :, 0, :], we2.rearrange("l a b -> a l b")), (WE2[D:P, :, 1, :], we2.rearrange("l a b -> a l b")),
            (BE2[:, :, :], be2.partition_broadcast(P)),
            (RW[:, :], res_w.partition_broadcast(P)), (DS[:, :], dot_scale.partition_broadcast(P)),
            (LG[:, :, :], ln_g.partition_broadcast(P)), (LB[:, :, :], ln_b.partition_broadcast(P)),
        ]
        nodes = [
            (X[:, 0:NB - 1, :], x[0:(NB - 1) * P, :].rearrange("(b p) d -> p b d", p=P)),
            (X[0:LAST_BLOCK, NB - 1, :], x[(NB - 1) * P:NODES, :]),
            (src_i[:, :], src_t), (dst_i[:, :], dst_t), (dstr_i[:, :, :], dst_r.rearrange("p (g e) -> p g e", g=4)),
        ]
        ALL_IN = 16 * (len(weights) + len(nodes))

        block = ctx.enter_context(nc.Block())

        def wait(eng, semaphore, value):
            if not isinstance(value, int) or value > 0:
                eng.wait_ge(semaphore, value)

        def rounds(eng, body, peel, end=ROUNDS):
            if peel:
                body(0)
            with eng.Fori(1 if peel else 0, end) as i:
                body(i)

        def branch(eng, program):
            eng.wait_ge(flag_ready, 1)
            flag = eng.value_load(spread_i[0:1, 0:1], min_val=0, max_val=1)
            with eng.If(flag == 0):
                program(1)
            with eng.Else():
                program(PAIRS)

        @block.sync
        def _(sp):
            sp.wait_ge(consts, 1)
            for to, of in nodes + weights:
                sp.dma_start(to, of).then_inc(loaded, 16)
            sp.wait_ge(dve, 8)
            sp.dma_start(tile_range[0].rearrange("(p g) -> p g", g=4), low_r[:, :]).then_inc(range_out, 16)
            sp.dma_start(tile_range[1].rearrange("(p g) -> p g", g=4), high_r[:, :]).then_inc(range_out, 16)
            sp.wait_ge(range_out, 32)
            sp.dma_start(first_block[:, :], tile_range[0].partition_broadcast(P)).then_inc(range_in, 16)
            sp.dma_start(last_block[:, :], tile_range[1].partition_broadcast(P)).then_inc(range_in, 16)

            def program(wide):
                for s in range(STAGES):
                    sp.wait_ge(table_due, s + 1)
                    sp.dma_start(table.rearrange("(p b) d -> p (b d)", b=NB),
                                 H[:, :, :].rearrange("p b d -> p (b d)")).then_inc(table_in, 16)
                    if s >= STAGES - LAYERS:
                        l = s - STAGES + LAYERS

                        def load_attr(i):
                            for j in range(SLOTS):
                                wait(sp, z_ready, i * SLOTS + (QUADS * l + j - SLOTS + 1))
                                sp.dma_start(attr[:, j, :], attr_t[:, bass.ds((i * SLOTS + j) * (QUAD * P), QUAD * P)])\
                                  .then_inc(attr_in[j], 16)

                        rounds(sp, load_attr, l == 0)
                sp.wait_ge(out_due, 1)
                sp.dma_start(out[0:(NB - 1) * P, :].rearrange("(b p) d -> p b d", p=P),
                             X[:, 0:NB - 1, :]).then_inc(written, 16)
                sp.dma_start(out[(NB - 1) * P:NODES, :], X[0:LAST_BLOCK, NB - 1, :]).then_inc(written, 16)
                sp.wait_ge(written, 32)

            branch(sp, program)

        @block.gpsimd
        def _(pool):
            nc.gpsimd.memset(X[:, NB - 1, :], 0.0).then_inc(consts, 1)
            nc.gpsimd.iota(iota_lo[:, :], [[1, P]], base=0, channel_multiplier=0,
                           allow_small_or_imprecise_dtypes=True).then_inc(consts, 1)
            nc.gpsimd.iota(iota_hi[:, :], [[1, MASKS]], base=0, channel_multiplier=0,
                           allow_small_or_imprecise_dtypes=True).then_inc(consts, 1)
            nc.gpsimd.memset(ident[:, :], 0.0).then_inc(consts, 1)
            nc.gpsimd.memset(ones[:, :], 1.0).then_inc(consts, 1)
            nc.gpsimd.memset(real[:, :], 1.0).then_inc(consts, 1)
            nc.gpsimd.memset(eps5[:, :], 1e-5).then_inc(consts, 1)
            nc.gpsimd.memset(eps3[:, :], 1e-3).then_inc(consts, 1)
            nc.gpsimd.memset(zero[:, :], 0.0).then_inc(consts, 1)
            nc.gpsimd.memset(pick[:, :], 0.0).then_inc(consts, 1)
            nc.gpsimd.memset(BE2s[:, :, :], 0.0).then_inc(consts, 1)
            pool.wait_ge(consts, 11)
            nc.gpsimd.affine_select(out=ident[:, :], in_=ident[:, :], compare_op=ALU.not_equal, fill=1.0, base=0,
                                    pattern=[[-1, P]], channel_multiplier=1).then_inc(consts, 1)
            nc.gpsimd.affine_select(out=real[:, NB - 1:NB], in_=real[:, NB - 1:NB], compare_op=ALU.is_gt, fill=0.0,
                                    base=LAST_BLOCK, pattern=[[0, 1]], channel_multiplier=-1).then_inc(consts, 1)
            for r in range(3):
                pool.wait_ge(consts, 13 + r)
                nc.gpsimd.memset(pick[32 * r:32 * r + 1, :], 1.0).then_inc(consts, 1)

            def program(wide):
                for s in range(STAGES):
                    pool.wait_ge(table_in, 16 * (s + 1))

                    def gathers(i):
                        for j in range(SLOTS):
                            wait(pool, masked_ready, i * (SLOTS * wide) + wide * (QUADS * s + j - SLOTS + 1))
                            c = slice(j * QUAD, (j + 1) * QUAD)
                            nc.gpsimd.tensor_copy(idx_slot[:, c], idx_all[:, bass.ds((i * SLOTS + j) * QUAD, QUAD)])\
                              .then_inc(idx_ready, 1)
                            pool.wait_ge(idx_ready, i * SLOTS + (QUADS * s + j + 1))
                            pool.sem_inc(idx_seen, 1)
                            for k in range(QUAD):
                                at = j * QUAD + k
                                nc.gpsimd.indirect_dma_start(
                                    out=rows[:, j, k, :], out_offset=None, in_=table,
                                    in_offset=bass.IndirectOffsetOnAxis(ap=idx_slot[:, at:at + 1], axis=0),
                                ).then_inc(gathered[j], 16)

                    rounds(pool, gathers, s == 0)

            branch(pool, program)

        @block.scalar
        def _(act):
            def program(wide):
                def copy_turned(k):
                    for g in range(NQ):
                        b0, n = dims(g)
                        act.wait_ge(turned, NQ * k + g + 1)
                        nc.scalar.activation(XT[:, b0 * P:(b0 + n) * P], z_ps[:, g % 2, 0:n * P], ACT.Copy)\
                          .then_inc(xt_ready, 1)

                roots = [0]

                def root(eps, cols, row):
                    act.wait_ge(root_in, roots[0] + 1)
                    roots[0] += 1
                    t = stat[:, row, 0:cols]
                    nc.scalar.activation(t, t, ACT.Sqrt, bias=eps[:, :]).then_inc(rooted, 1)

                root(zero_bias, NB, 6)
                root(eps5, NB, 1)
                copy_turned(0)
                copy_turned(1)
                root(eps5, NB, 1)
                copy_turned(2)
                root(eps5, NB, 1)
                for i in range(3):
                    copy_turned(3 + i)
                    act.wait_ge(root_in, roots[0] + 1)
                    roots[0] += 1
                    nc.scalar.activation(part[:, 4:5], part[:, 4:5], ACT.Sqrt, bias=eps3[:, :]).then_inc(rooted, 1)
                root(eps5, NB, 1)
                for l in range(LAYERS):
                    for g in range(NQ):
                        b0, n = dims(g)
                        act.wait_ge(turned, NQ * (6 + l) + g + 1)
                        nc.scalar.activation(XT[0:D, b0 * P:(b0 + n) * P], z_ps[0:D, g % 2, 0:n * P], ACT.Copy)\
                          .then_inc(xt_ready, 1)
                    for g in range(NQ):
                        _, n = dims(g)
                        act.wait_ge(hid_ps_ready, NQ * l + g + 1)
                        wait(act, hid_ready, NQ * l + g - 1)
                        nc.scalar.activation(hid_z[:, g % 2, 0:n * P], e_ps[:, g % 2, 0:n * P], ACT.Identity,
                                             bias=B1[:, l:l + 1]).then_inc(hid_z_ready, 1)

                    def activate(i):
                        for j in range(SLOTS):
                            act.wait_ge(z_ready, i * SLOTS + (QUADS * l + j + 1))
                            wait(act, e_ready, i * SLOTS + (QUADS * l + j - 1))
                            nc.scalar.activation(act_e[:, j % 2, :], z_ps[:, j % 2, :], ACT.Relu,
                                                 bias=BE1[:, l:l + 1]).then_inc(acted, 1)

                    rounds(act, activate, l == 0)
                    root(eps5, NB, 1)

            zero_bias = zero
            branch(act, program)

        @block.tensor
        def _(pe):
            def program(wide):
                with pe.Fori(0, QUADS // 2) as i:
                    for j in range(2):
                        pe.wait_ge(hist_hot, i * 2 + (j + 1))
                        for k in range(QUAD):
                            nc.tensor.matmul(z_ps[:, 0, 0:MASKS], onehot[:, j, k, :], hot_hi[:, j, 0, k, :],
                                             start=False, stop=True, skip_group_check=True)
                            last = nc.tensor.matmul(z_ps[:, 1, 0:MASKS], onehot_src[:, j, k, :], hot_hi[:, j, 1, k, :],
                                                    start=False, stop=True, skip_group_check=True)
                        last.then_inc(hist_done, 1)

                def turn(k, rows_of, width):
                    pe.wait_ge(node_in, k + 1)
                    for g in range(NQ):
                        b0, n = dims(g)
                        if g >= 2:
                            pe.wait_ge(xt_ready, NQ * k + g - 1)
                        for b in range(n):
                            last = nc.tensor.transpose(z_ps[0:width, g % 2, b * P:(b + 1) * P],
                                                       rows_of(b0 + b), ident[:, :])
                        last.then_inc(turned, 1)

                def scatter(s, i, j, at):
                    ready, before = (masked_ready, 0) if s < 6 else (msg_ready, QUADS * 6)
                    pe.wait_ge(hot_ready, i * SLOTS + (QUADS * s + j + 1))
                    if wide == 1:
                        pe.wait_ge(ready, i * SLOTS + (QUADS * s - before + j + 1))
                        for k in range(QUAD):
                            last = nc.tensor.matmul(agg_ps[:, bass.ds(at[j * QUAD + k], 2 * D)],
                                                    onehot[:, j % 2, k, :], source[:, j % 2, k, :, :],
                                                    start=False, stop=True, skip_group_check=True)
                        last.then_inc(scattered, 1)
                    else:
                        for w in range(wide):
                            pe.wait_ge(ready, i * (SLOTS * wide) + (wide * (QUADS * s - before + j) + w + 1))
                            for k in range(QUAD):
                                last = nc.tensor.matmul(agg_ps[:, w * 2 * D:(w + 1) * 2 * D],
                                                        onehot[:, j % 2, k, :],
                                                        source[:, (j * wide + w) % 2, k, :, :],
                                                        start=False, stop=True, skip_group_check=True)
                            last.then_inc(scattered, 1)

                def windows(i):
                    if wide > 1:
                        return None
                    _, at = nc.values_load_multi_w_load_instructions(
                        window_at[0:1, bass.ds(i * SLOTS * QUAD, SLOTS * QUAD)], engines=[pe.engine],
                        min_val=0, max_val=4 * BANK - 2 * D, bass_reorder=False,
                        skip_runtime_bounds_check_because="it comes from a block, and no block lies further")
                    return at

                def project(k, lhs, weight, ready):
                    for g in range(NQ):
                        b0, n = dims(g)
                        ready(g)
                        for b in range(n):
                            last = nc.tensor.matmul(agg_ps[:, (b0 + b) * D:(b0 + b + 1) * D],
                                                    lhs(g, b), weight, start=False, stop=True, skip_group_check=True)
                    last.then_inc(projected, 1)

                for s in range(6):
                    source = masked
                    pe.wait_ge(cleared, 2 * s + 1)
                    with pe.Fori(0, ROUNDS) as i:
                        at = windows(i)
                        for j in range(SLOTS):
                            scatter(s, i, j, at)
                    turn(s, lambda b: cat[:, b, :], P)
                    pe.wait_ge(cleared, 2 * s + 2)
                    project(s, lambda g, b: XT[:, (g * QUAD + b) * P:(g * QUAD + b + 1) * P], Wp[:, s, :],
                            lambda g: pe.wait_ge(xt_ready, NQ * s + g + 1))
                    if s >= 3:
                        for r in range(2):
                            pe.wait_ge(sum_in, 2 * (s - 3) + r + 1)
                            nc.tensor.matmul(z_ps[:, 0, 0:1], ones[:, :], part[:, r:r + 1], start=True, stop=True)\
                              .then_inc(summed, 1)

                for l in range(LAYERS):
                    s = 6 + l
                    turn(s, lambda b: X1[:, b, :], D)
                    for g in range(NQ):
                        b0, n = dims(g)
                        pe.wait_ge(xt_ready, NQ * s + g + 1)
                        if g >= 2:
                            pe.wait_ge(hid_z_ready, NQ * l + g - 1)
                        nc.tensor.matmul(e_ps[:, g % 2, 0:n * P], W1[:, l, :], XT[0:D, b0 * P:(b0 + n) * P],
                                         start=True, stop=True).then_inc(hid_ps_ready, 1)
                        if g == 0:
                            pe.wait_ge(cleared, 12 + 2 * l + 1)
                        if g >= 1:
                            second(pe, l, g - 1, dims)
                    second(pe, l, NQ - 1, dims).then_inc(projected, 1)

                    source = msg
                    base = QUADS * l
                    pe.wait_ge(cleared, 12 + 2 * l + 2)

                    def first_product(i, j):
                        i, j = i + j // SLOTS, j % SLOTS
                        pe.wait_ge(attr_in[j], 16 * (ROUNDS * l + i + 1))
                        wait(pe, acted, i * SLOTS + (base + j - 1))
                        nc.tensor.matmul(z_ps[:, j % 2, :], WE1[:, l, :, :], attr[:, j, :], start=True, stop=True)\
                          .then_inc(z_ready, 1)

                    def second_product(i, j):
                        i, j = i + j // SLOTS, j % SLOTS
                        pe.wait_ge(acted, i * SLOTS + (base + j + 1))
                        wait(pe, msg_ready, i * (SLOTS * wide) + wide * (base + j - 1))
                        nc.tensor.matmul(e_ps[:, j % 2, :], pick[:, :], bc(BE2s[:, l, :], 1, 2 * QUAD),
                                         start=True, stop=False, skip_group_check=True)
                        for k in range(QUAD):
                            last = nc.tensor.matmul(e_ps[:, j % 2, k * 2 * D:(k + 1) * 2 * D],
                                                    act_e[:, j % 2, k * P:(k + 1) * P], WE2[:, l, :, :],
                                                    start=False, stop=True, skip_group_check=True)
                        last.then_inc(e_ready, 1)

                    first_product(0, 0)
                    first_product(0, 1)
                    second_product(0, 0)

                    def products(i):
                        at = windows(i)
                        for j in range(SLOTS):
                            first_product(i, j + 2)
                            second_product(i, j + 1)
                            scatter(s, i, j, at)

                    rounds(pe, products, l == 0, ROUNDS - 1)
                    at = windows(ROUNDS - 1)
                    for j in range(SLOTS):
                        if j + 2 < SLOTS:
                            first_product(ROUNDS - 1, j + 2)
                        if j + 1 < SLOTS:
                            second_product(ROUNDS - 1, j + 1)
                        scatter(s, ROUNDS - 1, j, at)

            def second(pe, l, g, dims):
                b0, n = dims(g)
                pe.wait_ge(hid_ready, NQ * l + g + 1)
                for b in range(n):
                    last = nc.tensor.matmul(agg_ps[:, (b0 + b) * D:(b0 + b + 1) * D], hid[:, g % 2, b * P:(b + 1) * P],
                                            W2[:, l, :], start=False, stop=True, skip_group_check=True)
                return last

            branch(pe, program)

        @block.vector
        def _(v):
            steps = [0]

            def link(ins):
                steps[0] += 1
                ins.then_inc(dve, 1)
                v.wait_ge(dve, steps[0])

            V = nc.vector
            v.wait_ge(consts, 16)
            v.wait_ge(loaded, ALL_IN)
            link(V.memset(agg_ps[:, :], 0.0))
            link(V.memset(z_ps[:, :, :], 0.0))
            link(V.memset(part[:, :], 0.0))
            link(V.tensor_scalar(dstr_b[:, :, :], dstr_i[:, :, :], 7, None, ALU.arith_shift_right))
            link(V.tensor_copy(dstr_f[:, :, :], dstr_b[:, :, :]))
            link(V.tensor_reduce(low_r[:, :], dstr_f[:, :, :], AX.X, ALU.min))
            link(V.tensor_reduce(high_r[:, :], dstr_f[:, :, :], AX.X, ALU.max))
            link(V.memset(masks[:, :, :], 0.0))
            for i_t, f_t, lo, hi in ((src_i, src_f, src_lo, src_hi), (dst_i, dst_f, dst_lo, dst_hi)):
                link(V.tensor_copy(f_t[:, :], i_t[:, :]))
                link(V.tensor_scalar(tmp_i[:, :], i_t[:, :], 7, None, ALU.arith_shift_right))
                link(V.tensor_copy(hi[:, :], tmp_i[:, :]))
                link(V.scalar_tensor_tensor(lo[:, :], hi[:, :], -float(P), f_t[:, :], ALU.mult, ALU.add))
            link(V.tensor_tensor(not_loop[:, :], src_f[:, :], dst_f[:, :], ALU.not_equal))
            link(V.tensor_scalar(cmp[:, :], src_hi[:, :], 1.0, None, ALU.add))
            link(V.tensor_tensor(cmp[:, :], cmp[:, :], not_loop[:, :], ALU.mult))
            link(V.tensor_scalar(out_hi[:, :], cmp[:, :], -1.0, None, ALU.add))
            link(V.scalar_tensor_tensor(cmp[:, :], src_lo[:, :], float(NB), src_hi[:, :], ALU.mult, ALU.add))
            link(V.tensor_copy(idx_all[:, :], cmp[:, :]))
            v.wait_ge(range_in, 32)
            link(V.tensor_scalar(bank_of[:, :], first_block[:, :], 7.0, None, ALU.is_ge))
            for edge in (14.0, 21.0):
                link(V.tensor_scalar(cmp[:, :], first_block[:, :], edge, None, ALU.is_ge))
                link(V.tensor_tensor(bank_of[:, :], bank_of[:, :], cmp[:, :], ALU.add))
            link(V.tensor_tensor(window_f[:, :], first_block[:, :], bank_of[:, :], ALU.add))
            link(V.tensor_scalar(window_f[:, :], window_f[:, :], float(D), None, ALU.mult))
            link(V.tensor_copy(window_at[:, :], window_f[:, :]))
            link(V.tensor_tensor(cmp[:, :], last_block[:, :], first_block[:, :], ALU.subtract))
            link(V.tensor_reduce(spread[:, :], cmp[:, :], AX.X, ALU.max))
            link(V.tensor_scalar(spread[:, :], spread[:, :], 2.0, None, ALU.is_ge))
            link(V.tensor_scalar(WE1[:, :, 1, :], WE1[:, :, 1, :], -1.0, None, ALU.mult))
            link(V.tensor_scalar(BE1[D:P, :], BE1[D:P, :], -1.0, None, ALU.mult))
            link(V.tensor_scalar(WE2[D:P, :, :, :], WE2[D:P, :, :, :], -0.1, None, ALU.mult))
            link(V.tensor_copy(BE2p[:, 0, :, :], BE2[:, :, :]))
            link(V.tensor_tensor(BE2r[:, :, :], BE2[:, :, :], BE2p[:, 0, :, :], ALU.subtract))
            link(V.tensor_copy(BE2p[:, 1, :, :], BE2r[:, :, :]))
            link(V.tensor_tensor(BE2r[:, :, :], BE2r[:, :, :], BE2p[:, 1, :, :], ALU.subtract))
            link(V.tensor_copy(BE2p[:, 2, :, :], BE2r[:, :, :]))
            for r in range(3):
                link(V.tensor_copy(BE2s[32 * r:32 * r + 1, :, :], BE2p[32 * r:32 * r + 1, r, :, :]))
            link(V.tensor_tensor(RW[:, :], RW[:, :], DS[:, :], ALU.mult))
            V.tensor_copy(spread_i[:, :], spread[:, :]).then_inc(flag_ready, 1)

            began = steps[0]

            def program(wide):
                steps[0] = began
                if wide == 1:
                    for w in range(2):
                        if w:
                            link(V.tensor_scalar(first_block[:, :], first_block[:, :], 1.0, None, ALU.add))
                        link(V.tensor_tensor(masks[:, :, w], dst_hi[:, :], first_block[:, :], ALU.is_equal))
                else:
                    for w in range(2 * wide):
                        link(V.tensor_scalar(masks[:, :, w], dst_hi[:, :], float(w), None, ALU.is_equal))

                def hist(i):
                    for j in range(2):
                        wait(v, hist_done, i * 2 + (j - 1))
                        t = bass.ds((i * 2 + j) * QUAD, QUAD)
                        for hot, lo in ((onehot, dst_lo), (onehot_src, src_lo)):
                            V.tensor_tensor(hot[:, j, :, :], bc(iota_lo[:, :], 1, QUAD), bc(lo[:, t], 2, P), ALU.is_equal)
                        V.tensor_tensor(hot_hi[:, j, 0, :, :], bc(iota_hi[:, :], 1, QUAD), bc(dst_hi[:, t], 2, MASKS),
                                        ALU.is_equal)
                        V.tensor_tensor(hot_hi[:, j, 1, :, :], bc(iota_hi[:, :], 1, QUAD), bc(out_hi[:, t], 2, MASKS),
                                        ALU.is_equal).then_inc(hist_hot, 1)

                rounds(v, hist, True, QUADS // 2)
                v.wait_ge(hist_done, QUADS)
                link(V.tensor_scalar(stat[:, 0, :], z_ps[:, 0, 0:NB], 1.0, None, ALU.max))
                link(V.reciprocal(rdeg[:, :], stat[:, 0, :]))
                link(V.tensor_scalar(stat[:, 7, :], z_ps[:, 1, 0:NB], 0.0, None, ALU.is_gt))
                roots = [0]

                def root(ins):
                    roots[0] += 1
                    ins.then_inc(root_in, 1)
                    v.wait_ge(rooted, roots[0])

                given = {}

                def give(ins, semaphore):
                    given[semaphore.name] = given.get(semaphore.name, 0) + 1
                    ins.then_inc(semaphore, 1)
                    v.wait_ge(semaphore, given[semaphore.name])

                root(V.tensor_scalar(stat[:, 6, :], z_ps[:, 1, 0:NB], 1.0, None, ALU.max))
                link(V.reciprocal(stat[:, 6, :], stat[:, 6, :]))
                link(V.tensor_tensor(dinv[:, :], stat[:, 6, :], stat[:, 7, :], ALU.mult))
                link(V.tensor_scalar(ndinv[:, :], dinv[:, :], -1.0, None, ALU.mult))

                def per_node(t):
                    return bc(t, 2, D)

                def norm(to, of, relu, last=None):
                    link(V.tensor_reduce(stat[:, 0, :], of, AX.X, ALU.add))
                    link(V.tensor_scalar(stat[:, 0, :], stat[:, 0, :], 1.0 / D, None, ALU.mult))
                    link(V.tensor_tensor(S0[:, :, :], of, per_node(stat[:, 0, :]), ALU.subtract))
                    link(V.tensor_tensor(to, S0[:, :, :], S0[:, :, :], ALU.mult))
                    link(V.tensor_reduce(stat[:, 1, :], to, AX.X, ALU.add))
                    root(V.tensor_scalar(stat[:, 1, :], stat[:, 1, :], 1.0 / D, None, ALU.mult))
                    link(V.reciprocal(stat[:, 1, :], stat[:, 1, :]))
                    if relu:
                        link(V.tensor_scalar(S0[:, :, :], S0[:, :, :], 0.0, None, ALU.max))
                    ins = V.tensor_tensor(to, S0[:, :, :], per_node(stat[:, 1, :]), ALU.mult)
                    give(ins, last) if last is not None else link(ins)

                def agg_view():
                    if wide > 1:
                        return [(0, NB, agg_ps[:, 0:NB * D].rearrange("p (b d) -> p b d", d=D))]
                    got = []
                    for k in range(4):
                        n = min(7, NB - 7 * k)
                        got.append((7 * k, n, agg_ps[:, k * BANK:k * BANK + n * D].rearrange("p (b d) -> p b d", d=D)))
                    return got

                def edges(s, edge_layer):
                    l = s - 6

                    def quads(i):
                        for j in range(SLOTS):
                            t = bass.ds((i * SLOTS + j) * QUAD, QUAD)
                            wait(v, scattered, i * (SLOTS * wide) + wide * (QUADS * s + j - 1))
                            V.tensor_tensor(onehot[:, j % 2, :, :], bc(iota_lo[:, :], 1, QUAD), bc(dst_lo[:, t], 2, P),
                                            ALU.is_equal).then_inc(hot_ready, 1)
                            v.wait_ge(gathered[j], i * (16 * QUAD) + 16 * QUAD * (ROUNDS * s + 1))
                            for w in range(wide):
                                at = (j * wide + w) % 2
                                units = i * (SLOTS * wide)
                                u = wide * (QUADS * s + j) + w
                                ue = wide * (QUADS * l + j) + w
                                if l < 0:
                                    wait(v, scattered, units + (u - 1))
                                else:
                                    wait(v, msg_ready, units + (ue - 1))
                                V.tensor_tensor(masked[:, at, :, :, :], bc(rows[:, j, :, :], 2, 2),
                                                bc(masks[:, t, 2 * w:2 * w + 2], 3, D), ALU.mult)\
                                 .then_inc(masked_ready, 1)
                                if l < 0:
                                    continue
                                if w == 0:
                                    v.wait_ge(e_ready, i * SLOTS + (QUADS * l + j + 1))
                                v.wait_ge(masked_ready, units + (u + 1))
                                v.wait_ge(scattered, units + (u - 1))
                                V.tensor_tensor(msg[:, at, :, :, :], masked[:, at, :, :, :],
                                                e_ps[:, j % 2, :].rearrange("p (k w d) -> p k w d", k=QUAD, w=2),
                                                ALU.mult).then_inc(msg_ready, 1)

                    rounds(v, quads, s == 0 or l == 0)
                    v.wait_ge(scattered, wide * QUADS * (s + 1))

                def clear():
                    give(V.memset(agg_ps[:, :], 0.0), cleared)

                def take_agg(to):
                    for b0, n, view in agg_view():
                        link(V.tensor_copy(to[:, b0:b0 + n, :], view))
                    if wide == 1:
                        for k in range(3):
                            b = 7 * (k + 1)
                            link(V.tensor_tensor(to[:, b, :], to[:, b, :],
                                                 agg_ps[:, k * BANK + 7 * D:k * BANK + 8 * D], ALU.add))

                def projection(s):
                    v.wait_ge(projected, s + 1)
                    return agg_ps[:, 0:NB * D].rearrange("p (b d) -> p b d", d=D)

                norm(H[:, :, :], X[:, :, :], True, table_due)
                for s in range(3):
                    clear()
                    edges(s, False)
                    link(V.tensor_copy(cat[:, :, 0:D], H[:, :, :]))
                    take_agg(S0)
                    give(V.tensor_tensor(cat[:, :, D:2 * D], S0[:, :, :], per_node(rdeg[:, :]), ALU.mult), node_in)
                    clear()
                    y = projection(s)
                    ins = V.tensor_tensor(H[:, :, :], y, bc(Bp[:, s, :], 1, NB), ALU.add)
                    give(ins, table_due) if s == 0 else link(ins)
                    if s == 2:
                        link(V.tensor_scalar(H[:, :, :], H[:, :, :], 0.0, None, ALU.max))
                    if s:
                        link(V.tensor_tensor(X[:, :, :], X[:, :, :], H[:, :, :], ALU.add))
                        norm(H[:, :, :], X[:, :, :], True, table_due if s == 1 else None)

                for w in range(2 * wide):
                    link(V.tensor_copy(cmp[:, :], masks[:, :, w]))
                    link(V.tensor_tensor(masks[:, :, w], cmp[:, :], not_loop[:, :], ALU.mult))
                link(V.tensor_copy(cat[:, :, 0:D], H[:, :, :]))
                for i in range(3):
                    s = 3 + i
                    give(V.tensor_tensor(H[:, :, :], cat[:, :, 0:D], per_node(dinv[:, :]), ALU.mult), table_due)
                    clear()
                    edges(s, False)
                    take_agg(S0)
                    give(V.tensor_tensor(cat[:, :, D:2 * D], S0[:, :, :], per_node(ndinv[:, :]), ALU.mult), node_in)
                    clear()
                    y = projection(s)
                    link(V.tensor_tensor(S0[:, :, :], y, bc(Bp[:, s, :], 1, NB), ALU.add))
                    link(V.tensor_tensor(S0[:, :, :], S0[:, :, :], per_node(real[:, :]), ALU.mult))
                    give(V.tensor_reduce(part[:, 0:1], S0[:, :, :].rearrange("p b d -> p (b d)"), AX.X, ALU.add), sum_in)
                    v.wait_ge(summed, 2 * i + 1)
                    link(V.tensor_scalar(part[:, 2:3], z_ps[:, 0, 0:1], 1.0 / (NODES * D), None, ALU.mult))
                    link(V.tensor_scalar(S0[:, :, :], S0[:, :, :], part[:, 2:3], None, ALU.subtract))
                    link(V.tensor_tensor(S0[:, :, :], S0[:, :, :], per_node(real[:, :]), ALU.mult))
                    link(V.tensor_tensor(H[:, :, :], S0[:, :, :], S0[:, :, :], ALU.mult))
                    give(V.tensor_reduce(part[:, 1:2], H[:, :, :].rearrange("p b d -> p (b d)"), AX.X, ALU.add), sum_in)
                    v.wait_ge(summed, 2 * i + 2)
                    root(V.tensor_scalar(part[:, 4:5], z_ps[:, 0, 0:1], 1.0 / (NODES * D), None, ALU.mult))
                    link(V.reciprocal(part[:, 3:4], part[:, 4:5]))
                    link(V.tensor_tensor(part[:, 3:4], part[:, 3:4], gam[:, i:i + 1], ALU.mult))
                    link(V.tensor_scalar(cat[:, :, 0:D], S0[:, :, :], part[:, 3:4], bet[:, i:i + 1], ALU.mult, ALU.add))
                    if i == 0:
                        link(V.tensor_copy(X1[:, :, :], cat[:, :, 0:D]))
                    if i == 1:
                        link(V.tensor_scalar(cat[:, :, 0:D], cat[:, :, 0:D], 0.0, None, ALU.max))
                link(V.tensor_tensor(S0[:, :, :], X1[:, :, :], cat[:, :, 0:D], ALU.add))
                link(V.tensor_scalar(S0[:, :, :], S0[:, :, :], 0.5, 0.0, ALU.mult, ALU.max))
                link(V.tensor_tensor(X[:, :, :], X[:, :, :], S0[:, :, :], ALU.add))
                norm(X1[:, :, :], X[:, :, :], True, node_in)

                for l in range(LAYERS):
                    s = 6 + l
                    clear()
                    for g in range(NQ):
                        _, n = dims(g)
                        v.wait_ge(hid_z_ready, NQ * l + g + 1)
                        V.scalar_tensor_tensor(hid[:, g % 2, 0:n * P], hid_z[:, g % 2, 0:n * P], 0.1,
                                               hid_z[:, g % 2, 0:n * P], ALU.mult, ALU.max).then_inc(hid_ready, 1)
                    v.wait_ge(projected, s + 1)
                    give(V.tensor_tensor(H[:, :, :], agg_ps[:, 0:NB * D].rearrange("p (b d) -> p b d", d=D),
                                         bc(B2[:, l, :], 1, NB), ALU.add), table_due)
                    if l == 0:
                        if wide == 1:
                            link(V.tensor_tensor(masks[:, :, 1], dst_hi[:, :], first_block[:, :], ALU.is_equal))
                            link(V.tensor_scalar(cmp[:, :], first_block[:, :], -1.0, None, ALU.add))
                            link(V.tensor_tensor(masks[:, :, 0], dst_hi[:, :], cmp[:, :], ALU.is_equal))
                        else:
                            for w in range(2 * wide):
                                link(V.tensor_scalar(masks[:, :, w], dst_hi[:, :], float(w), None, ALU.is_equal))
                    clear()
                    edges(s, True)
                    take_agg(H)
                    link(V.tensor_scalar(H[:, :, :], H[:, :, :], RW[:, l:l + 1], None, ALU.mult))
                    link(V.tensor_tensor(H[:, :, :], H[:, :, :], X1[:, :, :], ALU.add))
                    norm(X1[:, :, :], H[:, :, :], False)
                    link(V.tensor_tensor(H[:, :, :], X1[:, :, :], bc(LG[:, l, :], 1, NB), ALU.mult))
                    ins = V.tensor_tensor(X1[:, :, :], H[:, :, :], bc(LB[:, l, :], 1, NB), ALU.add)
                    give(ins, node_in) if l < LAYERS - 1 else link(ins)
                V.tensor_tensor(X[:, :, :], X[:, :, :], X1[:, :, :], ALU.add).then_inc(out_due, 1)

            branch(v, program)


_OUTS = [((3125, 64), "float32")]


def kernel(**inputs):
    import numpy as np
    import concourse.bacc as bacc
    from concourse import mybir as mb
    from concourse.bass_utils import run_bass_kernel_spmd as run

    a = {k: np.asarray(v) for k, v in inputs.items()}
    pad = EPAD - EDGES
    src = np.concatenate([a["src"].astype(np.int32), np.full(pad, NPAD - 1, np.int32)])
    dst = np.concatenate([a["dst"].astype(np.int32), np.full(pad, NPAD - 1, np.int32)])
    attr_t = np.zeros((ED, EPAD), np.float32)
    attr_t[:, :EDGES] = a["edge_attr_32"].T
    arrays = {
        "x": a["x"], "src_t": src.reshape(TILES, P).T, "dst_t": dst.reshape(TILES, P).T,
        "dst_r": dst.reshape(ROWS, 4 * P), "attr_t": attr_t,
        "w_self1": a["L0_gnn_W_self1"], "w_neigh1": a["L0_gnn_W_neigh1"], "b_1": a["L0_gnn_b1"],
        "w_self2": a["L0_gnn_W_self2"], "w_neigh2": a["L0_gnn_W_neigh2"], "b_2": a["L0_gnn_b2"],
        "w_l": a["L1_gnn_W_l"], "w_r": a["L1_gnn_W_r"], "b_m": a["L1_gnn_b"],
        "w0_t": a["L2_gnn_W0"].transpose(0, 2, 1), "w1_t": a["L2_gnn_W1"].transpose(0, 2, 1),
        "b_c": a["L2_gnn_b"], "gamma": a["L2_gnn_gamma"], "beta": a["L2_gnn_beta"],
        "w1": a["L3_gnn_W1"], "b1_t": a["L3_gnn_b1"].T, "w2": a["L3_gnn_W2"], "b2": a["L3_gnn_b2"],
        "we1": a["L3_gnn_We1"], "be1_t": a["L3_gnn_be1"].T, "we2": a["L3_gnn_We2"], "be2": a["L3_gnn_be2"],
        "res_w": a["L3_gnn_res_w"], "dot_scale": a["L3_gnn_dot_scale"], "ln_g": a["L3_gnn_ln_g"],
        "ln_b": a["L3_gnn_ln_b"],
    }
    nc = bacc.Bacc("TRN2", target_bir_lowering=False, num_devices=1)
    args = []
    for name, v in arrays.items():
        arrays[name] = v = np.ascontiguousarray(v)
        args.append(nc.dram_tensor(name, v.shape, mb.dt.from_np(v.dtype), kind="ExternalInput").ap())
    for i, (shape, dtype) in enumerate(_OUTS):
        args.append(nc.dram_tensor(f"out_{i}", shape, mb.dt.from_np(np.dtype(dtype)), kind="ExternalOutput").ap())
    gnn_program(nc, *args)
    got = run(nc, [arrays], core_ids=[0])
    return got.results[0]["out_0"]
```

```python
import concourse.bass as bass
from concourse import mybir
from contextlib import ExitStack

NODES, D, EDGES, ED, LAYERS = 3125, 64, 53125, 32, 5
P = 128
NB = -(-NODES // P)
NPAD = NB * P
TILES = -(-EDGES // P)
EPAD = TILES * P
QUAD = 4
QUADS = TILES // QUAD
SLOTS = 4
ROUNDS = QUADS // SLOTS
BANK = 512
STAGES = 2 + 1 + 3 + LAYERS
LAST_BLOCK = NODES - (NB - 1) * P
ROWS = TILES // 4
PAIRS = (NB + 1) // 2
MASKS = 2 * PAIRS
DENSE = STAGES - LAYERS
SPAN = 16
KEYS = NB * SPAN
ACOLS = NODES + SPAN - 1
PW = 3 * D + 2
OUTS = 8
HALF = (NB + 1) // 2
CHUNKS = ((0, 8), (8, 16), (16, NB))
UNITS = -(-NB // QUAD)
ZEROED = 15
assert TILES % (QUAD * SLOTS) == 0


def gnn_program(nc, x, src_t, dst_t, dst_r, attr_t, w_self1, w_neigh1, b_1, w_self2, w_neigh2, b_2,
                w_l, w_r, b_m, w0_t, w1_t, b_c, gamma, beta, w1, b1_t, w2, b2, we1, be1_t, we2, be2,
                res_w, dot_scale, ln_g, ln_b, ln_g_t, ln_b_t, out):
    f32, i32, bf16 = mybir.dt.float32, mybir.dt.int32, mybir.dt.bfloat16
    ALU, ACT, AX = mybir.AluOpType, mybir.ActivationFunctionType, mybir.AxisListType
    ctx = ExitStack()
    with ctx:
        def sb(name, shape, dt=f32):
            return ctx.enter_context(nc.sbuf_tensor(name, shape, dt))

        def sem(name):
            return ctx.enter_context(nc.semaphore(name))

        def bc(ap, axis, n):
            a = ap.unsqueeze(axis)
            shape = list(a.shape)
            shape[axis] = n
            return a.to_broadcast(shape)

        table = nc.dram_tensor("table", (NPAD, D), f32, kind="Internal").ap()
        saved_tables = nc.dram_tensor("saved_tables", (P, 5 * TILES), f32, kind="Internal").ap()
        tile_range = nc.dram_tensor("tile_range", (2, TILES), f32, kind="Internal").ap()

        adj = sb("adj", [P, NB, ACOLS], bf16)
        flat = adj[:, :, :].rearrange("p c n -> p (c n)")
        taken = [0]

        def carve(shape, dt=f32, at=None):
            size = 1
            for n in shape[1:]:
                size *= n
            if at is not None:
                taken[0] = at
            halves = size * (1 if dt == bf16 else 2)
            lo = taken[0]
            taken[0] = lo + halves + halves % 2
            assert taken[0] <= NB * ACOLS, "adj's memory is full"
            t = flat[0:shape[0], lo:lo + halves]
            if dt != bf16:
                t = t.bitcast(dt)
            names = "abcd"[:len(shape) - 1]
            if len(names) > 1:
                t = t.rearrange(f"p ({' '.join(names)}) -> p {' '.join(names)}", **dict(zip(names, shape[1:])))
            return t

        tables = carve([P, 5, TILES])
        idx_all = tables[:, 0, :].bitcast(i32)
        window_at = tables[:, 1, :].bitcast(i32)
        dst_lo = tables[:, 2, :]
        near = tables[:, 3:5, :].rearrange("p w t -> p t w")
        rows = carve([P, SLOTS, QUAD, D])
        onehot = carve([P, 2, QUAD, P])
        masked = carve([P, 2, QUAD, 2, D])
        msg = carve([P, 2, QUAD, 2, D])
        attr = carve([P, SLOTS, QUAD * P])[0:ED]
        act_e = carve([P, 2, QUAD * P])
        XT = carve([P, NPAD])
        hid_z = carve([P, 2, BANK])
        hid = carve([P, 2, BANK])
        rows_buf = carve([P, NB * D])
        S0 = carve([P, NB, D])
        H = carve([P, NB, D])
        W1 = carve([P, LAYERS, 2, 2 * D])
        B1 = carve([P, LAYERS])
        W2 = carve([P, LAYERS, D])
        B2 = carve([P, LAYERS, D])
        WE1 = carve([P, LAYERS, 2, D])[0:ED]
        BE1 = carve([P, LAYERS])
        WE2 = carve([P, LAYERS, 2, D])
        BE2 = carve([P, LAYERS, D])
        BE2r = carve([P, LAYERS, D])
        BE2p = carve([P, 3, LAYERS, D], bf16)
        BE2s = carve([P, LAYERS, D], bf16)
        RW = carve([P, LAYERS])
        DS = carve([P, LAYERS])
        LGT = carve([P, LAYERS])
        LBT = carve([P, LAYERS])
        LG = carve([P, LAYERS, D])
        LB = carve([P, LAYERS, D])
        onehot_src = carve([P, 2, QUAD, P])
        hot_hi = carve([P, 2, 2, QUAD, MASKS])
        dst_hi = carve([P, TILES])
        src_lo = carve([P, TILES])
        out_hi = carve([P, TILES])
        cmp = carve([P, TILES])
        masks = carve([P, TILES, MASKS])
        taken[0] -= 2 * TILES * MASKS
        src_i = carve([P, TILES], i32)
        dst_i = carve([P, TILES], i32)
        tmp_i = carve([P, TILES], i32)
        src_f = carve([P, TILES])
        dst_f = carve([P, TILES])
        src_hi = carve([P, TILES])
        dstr_i = carve([P, 4, P], i32)[0:ROWS]
        dstr_f = carve([P, 4, P])[0:ROWS]
        low_r = carve([P, 4])[0:ROWS]
        high_r = carve([P, 4])[0:ROWS]
        first_node = carve([P, TILES])
        last_node = carve([P, TILES])
        first_block = carve([P, TILES])
        bank_of = carve([P, TILES])
        window_f = carve([P, TILES])
        spread = carve([P, 4])

        not_loop = sb("not_loop", [P, TILES])
        spread_i = sb("spread_i", [P, 1], i32)
        iota_lo = sb("iota_lo", [P, P])
        iota_hi = sb("iota_hi", [P, MASKS])
        idx_slot = sb("idx_slot", [P, SLOTS * QUAD], i32)
        low_slot = sb("low_slot", [P, SLOTS * QUAD])

        X = sb("X", [P, NB, D])
        X1 = sb("X1", [P, NB, D])
        cat = sb("cat", [P, NB, 2 * D])
        turned_rows = sb("turned_rows", [P, 2, BANK])
        parts = sb("parts", [P, NB, PW], bf16)
        stat = sb("stat", [P, 8, NB])
        real = sb("real", [P, NB])
        rdeg = sb("rdeg", [P, NB])
        dinv = sb("dinv", [P, NB])
        ndinv = sb("ndinv", [P, NB])
        ident = sb("ident", [P, P])
        ones = sb("ones", [P, P])
        part = sb("part", [P, 8])
        loops = sb("loops", [P, NB])
        eps5 = sb("eps5", [P, 1])
        eps3 = sb("eps3", [P, 1])
        zero = sb("zero", [P, 1])
        pick = sb("pick", [P, P], bf16)
        Wp = sb("Wp", [P, 6, D])
        Bp = sb("Bp", [P, 6, D])
        gam = sb("gam", [P, 3])
        bet = sb("bet", [P, 3])
        iota_key = sb("iota_key", [P, KEYS], mybir.dt.float16)
        iota_low = sb("iota_low", [P, P], mybir.dt.float16)
        both = X1[:, :, :].rearrange("p b d -> p (b d)").bitcast(bf16)
        hot_key = both[:, 0:4 * KEYS].rearrange("p (s k) -> p s k", s=4)
        counts = both[:, 4 * KEYS:8 * KEYS].rearrange("p (s k) -> p s k", s=4)
        hot_low = turned_rows[:, :, :].rearrange("p a b -> p (a b)").bitcast(bf16).rearrange("p (s k) -> p s k", k=P)
        hot_out = cat[:, :, :].rearrange("p b d -> p (b d)").bitcast(bf16)[:, 0:2 * OUTS * 2 * NB]            .rearrange("p (s t w b) -> p s t w b", s=2, t=OUTS, w=2)
        edge_keys = parts[:, :, :].rearrange("p b d -> p (b d)")[:, 0:10 * TILES].bitcast(f32)            .rearrange("p (k t) -> p k t", k=5)
        key = edge_keys[:, 0, :]
        src_low = edge_keys[:, 1, :]
        first_i = edge_keys[:, 2, :].bitcast(i32)
        out_blocks = edge_keys[:, 3:5, :]

        agg_ps = ctx.enter_context(nc.psum_tensor("agg_ps", [P, 4 * BANK], f32))
        z_ps = ctx.enter_context(nc.psum_tensor("z_ps", [P, 2, BANK], f32))
        e_ps = ctx.enter_context(nc.psum_tensor("e_ps", [P, 2, BANK], f32))

        loaded = sem("loaded")
        range_out = sem("range_out")
        range_in = sem("range_in")
        consts = sem("consts")
        flag_ready = sem("flag_ready")
        dve = sem("dve")
        hist_hot = sem("hist_hot")
        hist_done = sem("hist_done")
        table_due = sem("table_due")
        table_in = sem("table_in")
        idx_in = [sem(f"idx_in{j}") for j in range(SLOTS)]
        idx_seen = sem("idx_seen")
        gathered = [sem(f"gathered{j}") for j in range(SLOTS)]
        masked_ready = sem("masked_ready")
        hot_ready = sem("hot_ready")
        msg_ready = sem("msg_ready")
        scattered = sem("scattered")
        cleared = sem("cleared")
        attr_in = [sem(f"attr_in{j}") for j in range(SLOTS)]
        z_ready = sem("z_ready")
        acted = sem("acted")
        e_ready = sem("e_ready")
        node_in = sem("node_in")
        turned = sem("turned")
        xt_ready = sem("xt_ready")
        square_in = sem("square_in")
        squared = sem("squared")
        power_in = sem("power_in")
        power_rooted = sem("power_rooted")
        rows_in = sem("rows_in")
        rows_turned = sem("rows_turned")
        rows_copied = sem("rows_copied")
        hid_ps_ready = sem("hid_ps_ready")
        hid_z_ready = sem("hid_z_ready")
        hid_ready = sem("hid_ready")
        rows_projected = sem("rows_projected")
        projected = sem("projected")
        sum_in = sem("sum_in")
        summed = sem("summed")
        root_in = sem("root_in")
        rooted = sem("rooted")
        out_due = sem("out_due")
        late = sem("late")
        kept = sem("kept")
        adj_free = sem("adj_free")
        adj_zero = sem("adj_zero")
        low_in = sem("low_in")
        lows_seen = sem("lows_seen")
        low_ready = sem("low_ready")
        out_ready = sem("out_ready")
        key_ready = sem("key_ready")
        counted = sem("counted")
        counts_ready = sem("counts_ready")
        added = sem("added")
        parts_ready = sem("parts_ready")
        nb_ready = sem("nb_ready")
        nb_taken = sem("nb_taken")
        cat_ready = sem("cat_ready")
        cat_turned = sem("cat_turned")
        cat_copied = sem("cat_copied")
        cat_out = sem("cat_out")
        cat_taken = sem("cat_taken")
        dense_root_in = sem("dense_root_in")
        dense_rooted = sem("dense_rooted")
        written = sem("written")

        NQ = -(-NB // QUAD)
        dims = lambda g: (g * QUAD, min(QUAD, NB - g * QUAD))
        weights = [
            (Wp[0:D, 0, :], w_self1), (Wp[D:P, 0, :], w_neigh1), (Wp[0:D, 1, :], w_self2), (Wp[D:P, 1, :], w_neigh2),
            (Wp[0:D, 2, :], w_r), (Wp[D:P, 2, :], w_l),
            (Wp[0:D, 3:6, :], w0_t.rearrange("i a b -> a i b")), (Wp[D:P, 3:6, :], w1_t.rearrange("i a b -> a i b")),
            (Bp[:, 0, :], b_1.partition_broadcast(P)), (Bp[:, 1, :], b_2.partition_broadcast(P)),
            (Bp[:, 2, :], b_m.partition_broadcast(P)),
            (Bp[:, 3:6, :], b_c.partition_broadcast(P)),
            (gam[:, :], gamma.partition_broadcast(P)), (bet[:, :], beta.partition_broadcast(P)),
        ]
        late_weights = [
            (W1[0:D, :, 0, :], w1.rearrange("l a b -> a l b")), (W1[D:P, :, 1, :], w1.rearrange("l a b -> a l b")),
            (B1[:, :], b1_t), (LGT[0:D, :], ln_g_t), (LGT[D:P, :], ln_g_t), (LBT[0:D, :], ln_b_t), (LBT[D:P, :], ln_b_t),
            (W2[:, :, :], w2.rearrange("l a b -> a l b")), (B2[:, :, :], b2.partition_broadcast(P)),
            (WE1[:, :, 0, :], we1.rearrange("l a b -> a l b")), (WE1[:, :, 1, :], we1.rearrange("l a b -> a l b")),
            (BE1[0:D, :], be1_t), (BE1[D:P, :], be1_t),
            (WE2[0:D, :, 0, :], we2.rearrange("l a b -> a l b")), (WE2[0:D, :, 1, :], we2.rearrange("l a b -> a l b")),
            (WE2[D:P, :, 0, :], we2.rearrange("l a b -> a l b")), (WE2[D:P, :, 1, :], we2.rearrange("l a b -> a l b")),
            (BE2[:, :, :], be2.partition_broadcast(P)),
            (RW[:, :], res_w.partition_broadcast(P)), (DS[:, :], dot_scale.partition_broadcast(P)),
            (LG[:, :, :], ln_g.partition_broadcast(P)), (LB[:, :, :], ln_b.partition_broadcast(P)),
        ]
        nodes = [
            (X[:, 0:NB - 1, :], x[0:(NB - 1) * P, :].rearrange("(b p) d -> p b d", p=P)),
            (X[0:LAST_BLOCK, NB - 1, :], x[(NB - 1) * P:NODES, :]),
            (src_i[:, :], src_t), (dst_i[:, :], dst_t), (dstr_i[:, :, :], dst_r.rearrange("p (g e) -> p g e", g=4)),
        ]
        ALL_IN = 16 * (len(weights) + len(nodes))

        block = ctx.enter_context(nc.Block())

        def wait(eng, semaphore, value):
            if not isinstance(value, int) or value > 0:
                eng.wait_ge(semaphore, value)

        def rounds(eng, body, peel, end=ROUNDS):
            if peel:
                body(0)
            with eng.Fori(1 if peel else 0, end) as i:
                body(i)

        def branch(eng, program):
            eng.wait_ge(flag_ready, 1)
            flag = eng.value_load(spread_i[0:1, 0:1], min_val=0, max_val=1)
            with eng.If(flag == 0):
                program(1)
            with eng.Else():
                program(PAIRS)

        @block.sync
        def _(sp):
            sp.wait_ge(consts, 1)
            for to, of in nodes + weights:
                sp.dma_start(to, of).then_inc(loaded, 16)
            sp.wait_ge(dve, 6)
            sp.dma_start(tile_range[0].rearrange("(p g) -> p g", g=4), low_r).then_inc(range_out, 16)
            sp.dma_start(tile_range[1].rearrange("(p g) -> p g", g=4), high_r).then_inc(range_out, 16)
            sp.wait_ge(range_out, 32)
            sp.dma_start(first_node, tile_range[0].partition_broadcast(P)).then_inc(range_in, 16)
            sp.dma_start(last_node, tile_range[1].partition_broadcast(P)).then_inc(range_in, 16)

            def program(wide):
                edge_tables = tables.rearrange("p k t -> p (k t)")
                if wide == 1:
                    sp.dma_start(saved_tables, edge_tables).then_inc(kept, 16)
                    sp.wait_ge(kept, 16)
                    sp.wait_ge(adj_free, 1)
                    sp.dma_start(edge_tables, saved_tables).then_inc(late, 16)
                for to, of in late_weights:
                    sp.dma_start(to, of).then_inc(late, 16)
                if wide == 1:
                    sp.wait_ge(late, 16 * (len(late_weights) + 1))
                skipped = DENSE if wide == 1 else 0

                def load_round(s, i):
                    l = s - DENSE + skipped
                    for j in range(SLOTS):
                        wait(sp, gathered[j], i * (16 * QUAD) + 16 * QUAD * ROUNDS * s)
                        sp.dma_start(idx_slot[:, j * QUAD:(j + 1) * QUAD],
                                     idx_all[:, bass.ds((i * SLOTS + j) * QUAD, QUAD)]).then_inc(idx_in[j], 16)
                        if l >= 0:
                            wait(sp, z_ready, i * SLOTS + (QUADS * l + j - SLOTS + 1))
                            sp.dma_start(attr[:, j, :], attr_t[:, bass.ds((i * SLOTS + j) * (QUAD * P), QUAD * P)])\
                              .then_inc(attr_in[j], 16)

                for s in range(STAGES - skipped):
                    load_round(s, 0)
                    sp.wait_ge(table_due, s + 1)
                    sp.dma_start(table.rearrange("(p b) d -> p (b d)", b=NB),
                                 H[:, :, :].rearrange("p b d -> p (b d)")).then_inc(table_in, 16)
                    with sp.Fori(1, ROUNDS) as i:
                        load_round(s, i)
                sp.wait_ge(out_due, 1)
                sp.dma_start(out[0:(NB - 1) * P, :].rearrange("(b p) d -> p b d", p=P),
                             X[:, 0:NB - 1, :]).then_inc(written, 16)
                sp.dma_start(out[(NB - 1) * P:NODES, :], X[0:LAST_BLOCK, NB - 1, :]).then_inc(written, 16)
                sp.wait_ge(written, 32)

            branch(sp, program)

        @block.gpsimd
        def _(pool):
            nc.gpsimd.memset(X[:, NB - 1, :], 0.0).then_inc(consts, 1)
            nc.gpsimd.iota(iota_lo[:, :], [[1, P]], base=0, channel_multiplier=0,
                           allow_small_or_imprecise_dtypes=True).then_inc(consts, 1)
            nc.gpsimd.iota(iota_hi[:, :], [[1, MASKS]], base=0, channel_multiplier=0,
                           allow_small_or_imprecise_dtypes=True).then_inc(consts, 1)
            nc.gpsimd.memset(ident[:, :], 0.0).then_inc(consts, 1)
            nc.gpsimd.memset(ones[:, :], 1.0).then_inc(consts, 1)
            nc.gpsimd.memset(real[:, :], 1.0).then_inc(consts, 1)
            nc.gpsimd.memset(eps5[:, :], 1e-5).then_inc(consts, 1)
            nc.gpsimd.memset(eps3[:, :], 1e-3).then_inc(consts, 1)
            nc.gpsimd.memset(zero[:, :], 0.0).then_inc(consts, 1)
            nc.gpsimd.memset(pick[:, :], 0.0).then_inc(consts, 1)
            nc.gpsimd.iota(iota_low[:, :], [[1, P]], base=0, channel_multiplier=0,
                           allow_small_or_imprecise_dtypes=True).then_inc(consts, 1)
            nc.gpsimd.iota(iota_key[:, :], [[1, KEYS]], base=0, channel_multiplier=0,
                           allow_small_or_imprecise_dtypes=True).then_inc(consts, 1)
            pool.wait_ge(consts, 12)
            nc.gpsimd.affine_select(out=ident[:, :], in_=ident[:, :], compare_op=ALU.not_equal, fill=1.0, base=0,
                                    pattern=[[-1, P]], channel_multiplier=1).then_inc(consts, 1)
            nc.gpsimd.affine_select(out=real[:, NB - 1:NB], in_=real[:, NB - 1:NB], compare_op=ALU.is_gt, fill=0.0,
                                    base=LAST_BLOCK, pattern=[[0, 1]], channel_multiplier=-1).then_inc(consts, 1)
            for r in range(3):
                pool.wait_ge(consts, 14 + r)
                nc.gpsimd.memset(pick[32 * r:32 * r + 1, :], 1.0).then_inc(consts, 1)

            def program(wide):
                if wide == 1:
                    ring = SLOTS * QUAD

                    def lows(i):
                        wait(pool, low_ready, i * ring)
                        nc.gpsimd.tensor_copy(low_slot[:, :], src_low[:, bass.ds(i * ring, ring)]).then_inc(low_in, 1)
                        pool.wait_ge(low_in, i + 1)
                        for j in range(ring):
                            if j % OUTS == 0:
                                wait(pool, counted, i * ring + (j - ring + OUTS))
                                pool.sem_inc(lows_seen, 1)
                            nc.gpsimd.tensor_scalar(hot_low[:, j, :], iota_low[:, :],
                                                    low_slot[:, j:j + 1], None, ALU.is_equal)\
                              .then_inc(low_ready, 1)

                    rounds(pool, lows, True)
                for s in range(STAGES - (DENSE if wide == 1 else 0)):
                    pool.wait_ge(table_in, 16 * (s + 1))

                    def gathers(i):
                        for j in range(SLOTS):
                            wait(pool, masked_ready, i * (SLOTS * wide) + wide * (QUADS * s + j - SLOTS + 1))
                            pool.wait_ge(idx_in[j], i * 16 + 16 * (ROUNDS * s + 1))
                            pool.sem_inc(idx_seen, 1)
                            for k in range(QUAD):
                                at = j * QUAD + k
                                nc.gpsimd.indirect_dma_start(
                                    out=rows[:, j, k, :], out_offset=None, in_=table,
                                    in_offset=bass.IndirectOffsetOnAxis(ap=idx_slot[:, at:at + 1], axis=0),
                                ).then_inc(gathered[j], 16)

                    rounds(pool, gathers, s == 0)

            branch(pool, program)

        @block.scalar
        def _(act):
            def program(wide):
                def copy_turned(k):
                    for g in range(NQ):
                        b0, n = dims(g)
                        act.wait_ge(turned, NQ * k + g + 1)
                        nc.scalar.activation(XT[:, b0 * P:(b0 + n) * P], z_ps[:, g % 2, 0:n * P], ACT.Copy)\
                          .then_inc(xt_ready, 1)

                roots = [0]

                def root(eps, cols, row):
                    act.wait_ge(root_in, roots[0] + 1)
                    roots[0] += 1
                    t = stat[:, row, 0:cols]
                    nc.scalar.activation(t, t, ACT.Sqrt, bias=eps[:, :]).then_inc(rooted, 1)

                if wide == 1:
                    dense_blocks()
                else:
                    root(zero_bias, NB, 6)
                    root(eps5, NB, 1)
                    copy_turned(0)
                    copy_turned(1)
                    root(eps5, NB, 1)
                    copy_turned(2)
                    root(eps5, NB, 1)
                    for i in range(3):
                        copy_turned(3 + i)
                        act.wait_ge(root_in, roots[0] + 1)
                        roots[0] += 1
                        nc.scalar.activation(part[:, 4:5], part[:, 4:5], ACT.Sqrt, bias=eps3[:, :]).then_inc(rooted, 1)

                def norm_rows(k):
                    for c, (b0, b1) in enumerate(CHUNKS):
                        act.wait_ge(square_in, len(CHUNKS) * k + c + 1)
                        nc.scalar.activation(cat[:, b0:b1, 0:D], cat[:, b0:b1, D:2 * D], ACT.Square).then_inc(squared, 1)
                    for c, (b0, b1) in enumerate(CHUNKS):
                        act.wait_ge(power_in, len(CHUNKS) * k + c + 1)
                        nc.scalar.activation(stat[:, 1, b0:b1], stat[:, 1, b0:b1], ACT.Sqrt, bias=eps5[:, :],
                                             scale=1.0 / D).then_inc(power_rooted, 1)

                for l in range(LAYERS):
                    norm_rows(l)
                    for u in range(UNITS):
                        _, n = dims(u)
                        if u % 2 == 0:
                            k, high = u // 2, (P if n > 1 else D)
                            to, of = XT[0:high, k * BANK:k * BANK + n * P], z_ps[0:high, k % 2, 0:n * P]
                            act.wait_ge(rows_turned, (UNITS + 1) // 2 * l + k + 1)
                            if l == 0:
                                nc.scalar.activation(to, of, ACT.Copy).then_inc(rows_copied, 1)
                            else:
                                nc.scalar.activation(to, of, ACT.Identity, bias=LBT[0:high, l - 1:l],
                                                     scale=LGT[0:high, l - 1:l]).then_inc(rows_copied, 1)
                        act.wait_ge(hid_ps_ready, UNITS * l + u + 1)
                        wait(act, hid_ready, UNITS * l + u - 1)
                        nc.scalar.activation(hid_z[:, u % 2, 0:n * P], e_ps[:, u % 2, 0:n * P], ACT.Identity,
                                             bias=B1[:, l:l + 1]).then_inc(hid_z_ready, 1)

                    def activate(i):
                        for j in range(SLOTS):
                            act.wait_ge(z_ready, i * SLOTS + (QUADS * l + j + 1))
                            wait(act, e_ready, i * SLOTS + (QUADS * l + j - 1))
                            nc.scalar.activation(act_e[:, j % 2, :], z_ps[:, j % 2, :], ACT.Relu,
                                                 bias=BE1[:, l:l + 1]).then_inc(acted, 1)

                    rounds(act, activate, l == 0)
                norm_rows(LAYERS)

            zero_bias = zero

            def dense_blocks():
                act.wait_ge(kept, 16)
                for c in range(ZEROED, NB):
                    nc.scalar.activation(adj[:, c, :], zero[:, 0:1].to_broadcast([P, ACOLS]), ACT.Copy).then_inc(adj_zero, 1)

                def copy_counts(i):
                    for j in range(SLOTS):
                        act.wait_ge(counted, i * SLOTS + (j + 1))
                        wait(act, added, i * SLOTS + (j - SLOTS + 1))
                        nc.scalar.activation(counts[:, j, :], agg_ps[:, j * BANK:j * BANK + KEYS], ACT.Copy)                          .then_inc(counts_ready, 1)

                rounds(act, copy_counts, True, TILES // SLOTS)
                taken_roots = [0]

                def root(t, eps):
                    taken_roots[0] += 1
                    act.wait_ge(dense_root_in, taken_roots[0])
                    nc.scalar.activation(t, t, ACT.Sqrt, bias=eps[:, :]).then_inc(dense_rooted, 1)

                def copy_cat(s, g):
                    _, n = dims(g)
                    act.wait_ge(cat_turned, NQ * s + g + 1)
                    wait(act, cat_out, NQ * s + max(0, g - 1))
                    nc.scalar.activation(turned_rows[:, g % 2, 0:n * P], z_ps[:, g % 2, 0:n * P], ACT.Copy)                      .then_inc(cat_copied, 1)

                root(stat[:, 6, :], zero)
                root(stat[:, 1, :], eps5)
                for s in range(DENSE):
                    for it in range(1, NQ + 2):
                        if it <= NQ:
                            copy_cat(s, it - 1)
                        if s in (1, 2) and it >= 2:
                            root(stat[:, 1, 0:dims(it - 2)[1]], eps5)
                    if s >= 3:
                        root(part[:, 4:5], eps3)

            branch(act, program)

        @block.tensor
        def _(pe):
            def program(wide):
                def gathered_degrees():
                    with pe.Fori(0, QUADS // 2) as i:
                        for j in range(2):
                            pe.wait_ge(hist_hot, i * 2 + (j + 1))
                            for k in range(QUAD):
                                nc.tensor.matmul(z_ps[:, 0, 0:MASKS], onehot[:, j, k, :], hot_hi[:, j, 0, k, :],
                                                 start=False, stop=True, skip_group_check=True)
                                last = nc.tensor.matmul(z_ps[:, 1, 0:MASKS], onehot_src[:, j, k, :],
                                                        hot_hi[:, j, 1, k, :],
                                                        start=False, stop=True, skip_group_check=True)
                            last.then_inc(hist_done, 1)

                def count_edges(i):
                    ring = SLOTS * QUAD
                    for j in range(ring):
                        pe.wait_ge(low_ready, i * ring + (j + 1))
                        if j % OUTS == 0:
                            pe.wait_ge(out_ready, i * (ring // OUTS) + (j // OUTS + 1))
                        nc.tensor.matmul(z_ps[:, 0, 0:2 * NB], hot_low[:, j, :], hot_out[:, j // OUTS, j % OUTS, :, :],
                                         start=False, stop=True, skip_group_check=True)
                        pe.wait_ge(key_ready, i * ring + (j + 1))
                        wait(pe, counts_ready, i * ring + (j - SLOTS + 1))
                        nc.tensor.matmul(agg_ps[:, j % SLOTS * BANK:j % SLOTS * BANK + KEYS], hot_low[:, j, :],
                                         hot_key[:, j % 4, :], start=True, stop=True).then_inc(counted, 1)

                def dense_stage(s):
                    for g in range(NQ + 2):
                        if g < NQ:
                            b0, n = dims(g)
                            wait(pe, nb_taken, s * NQ + max(0, g - 1))
                            for b in range(n):
                                lo = (b0 + b) * P
                                m = min(P, ACOLS - lo)
                                for c in range(NB):
                                    if g == 0 and b == 0 and c in (0, HALF):
                                        pe.wait_ge(parts_ready, s * 2 + (1 if c == 0 else 2))
                                    at = g % 2 * 2 * BANK + b * (BANK // 2)
                                    last = nc.tensor.matmul(agg_ps[0:m, at:at + PW], adj[:, c, lo:lo + m],
                                                            parts[:, c, :], start=c == 0, stop=c == NB - 1)
                            last.then_inc(nb_ready, 1)
                        if 1 <= g <= NQ:
                            b0, n = dims(g - 1)
                            pe.wait_ge(cat_ready, s * NQ + g)
                            wait(pe, cat_copied, s * NQ + max(0, g - 2))
                            for b in range(n):
                                last = nc.tensor.transpose(z_ps[:, (g - 1) % 2, b * P:(b + 1) * P], cat[:, b0 + b, :],
                                                           ident[:, :])
                            last.then_inc(cat_turned, 1)
                        if g >= 2:
                            _, n = dims(g - 2)
                            pe.wait_ge(cat_copied, s * NQ + (g - 1))
                            wait(pe, cat_taken, s * NQ + max(0, g - 3))
                            for b in range(n):
                                last = nc.tensor.matmul(e_ps[:, g % 2, b * D:(b + 1) * D],
                                                        turned_rows[:, g % 2, b * P:(b + 1) * P], weight_of(s),
                                                        start=True, stop=True)
                            last.then_inc(cat_out, 1)

                def weight_of(s):
                    return Wp[:, bass.ds(s, 1), :].rearrange("p a d -> p (a d)")

                def mean_sums(first):
                    for r in range(2):
                        pe.wait_ge(sum_in, first + (r + 1))
                        nc.tensor.matmul(z_ps[:, 0, 0:1], ones[:, :], part[:, r:r + 1], start=True, stop=True)\
                          .then_inc(summed, 1)

                def turn(k, rows_of, width):
                    pe.wait_ge(node_in, k + 1)
                    for g in range(NQ):
                        b0, n = dims(g)
                        if g >= 2:
                            pe.wait_ge(xt_ready, NQ * k + g - 1)
                        for b in range(n):
                            last = nc.tensor.transpose(z_ps[0:width, g % 2, b * P:(b + 1) * P],
                                                       rows_of(b0 + b), ident[:, :])
                        last.then_inc(turned, 1)

                def scatter(s, i, j, at, source, ready, before):
                    pe.wait_ge(hot_ready, i * SLOTS + (QUADS * s + j + 1))
                    if wide == 1:
                        pe.wait_ge(ready, i * SLOTS + (before + j + 1))
                        for k in range(QUAD):
                            last = nc.tensor.matmul(agg_ps[:, bass.ds(at[j * QUAD + k], 2 * D)],
                                                    onehot[:, j % 2, k, :], source[:, j % 2, k, :, :],
                                                    start=False, stop=True, skip_group_check=True)
                        last.then_inc(scattered, 1)
                    else:
                        for w in range(wide):
                            pe.wait_ge(ready, i * (SLOTS * wide) + (wide * (before + j) + w + 1))
                            for k in range(QUAD):
                                last = nc.tensor.matmul(agg_ps[:, w * 2 * D:(w + 1) * 2 * D],
                                                        onehot[:, j % 2, k, :],
                                                        source[:, (j * wide + w) % 2, k, :, :],
                                                        start=False, stop=True, skip_group_check=True)
                            last.then_inc(scattered, 1)

                def windows(i):
                    if wide > 1:
                        return None
                    _, at = nc.values_load_multi_w_load_instructions(
                        window_at[0:1, bass.ds(i * SLOTS * QUAD, SLOTS * QUAD)], engines=[pe.engine],
                        min_val=0, max_val=4 * BANK - 2 * D, bass_reorder=False,
                        skip_runtime_bounds_check_because="it comes from a block, and no block lies further")
                    return at

                def project(k, lhs, weight, ready):
                    for g in range(NQ):
                        b0, n = dims(g)
                        ready(g)
                        for b in range(n):
                            last = nc.tensor.matmul(agg_ps[:, (b0 + b) * D:(b0 + b + 1) * D],
                                                    lhs(g, b), weight, start=False, stop=True, skip_group_check=True)
                    last.then_inc(projected, 1)

                def gathered_stages():
                    for s in range(DENSE):
                        pe.wait_ge(cleared, 2 * s + 1)
                        with pe.Fori(0, ROUNDS) as i:
                            at = windows(i)
                            for j in range(SLOTS):
                                scatter(s, i, j, at, masked, masked_ready, QUADS * s)
                        turn(s, lambda b: cat[:, b, :], P)
                        pe.wait_ge(cleared, 2 * s + 2)
                        project(s, lambda g, b: XT[:, (g * QUAD + b) * P:(g * QUAD + b + 1) * P], Wp[:, s, :],
                                lambda g: pe.wait_ge(xt_ready, NQ * s + g + 1))
                        if s >= 3:
                            mean_sums(2 * (s - 3))

                if wide == 1:
                    rounds(pe, count_edges, True)
                    dense_stage(0)
                    with pe.Fori(1, 3) as s:
                        dense_stage(s)
                    with pe.Fori(3, DENSE) as s:
                        dense_stage(s)
                        mean_sums(s * 2 - 6)
                else:
                    gathered_degrees()
                    gathered_stages()
                s0 = 0 if wide == 1 else DENSE
                for l in range(LAYERS):
                    s = s0 + l
                    def turn_rows(k):
                        wait(pe, rows_copied, (UNITS + 1) // 2 * l + k - 1)
                        pe.wait_ge(rows_in, len(CHUNKS) * l + min(k + 1, len(CHUNKS)))
                        for b in range(8 * k, min(8 * k + 8, NB), 2):
                            width = min(2, NB - b) * D
                            last = nc.tensor.transpose(z_ps[0:width, k % 2, (b // 2 - 4 * k) * P:(b // 2 - 4 * k + 1) * P],
                                                       rows_buf[:, b * D:b * D + width], ident[:, :])
                        last.then_inc(rows_turned, 1)

                    def hidden(u):
                        _, n = dims(u)
                        k, high = u // 2, (P if n > 1 else D)
                        pe.wait_ge(rows_copied, (UNITS + 1) // 2 * l + k + 1)
                        if u >= 2:
                            pe.wait_ge(hid_z_ready, UNITS * l + u - 1)
                        nc.tensor.matmul(e_ps[:, u % 2, 0:n * P], W1[0:high, l, u % 2, :],
                                         XT[0:high, k * BANK:k * BANK + n * P], start=True, stop=True)\
                          .then_inc(hid_ps_ready, 1)

                    def rows_out(u):
                        _, n = dims(u)
                        pe.wait_ge(hid_ready, UNITS * l + u + 1)
                        for k in range(n):
                            b = 8 * (u // 2) + u % 2 + 2 * k
                            last = nc.tensor.matmul(agg_ps[:, b * D:(b + 1) * D], hid[:, u % 2, k * P:(k + 1) * P],
                                                    W2[:, l, :], start=True, stop=True)
                        if u % 2 == 1 or u == UNITS - 1:
                            last.then_inc(rows_projected, 1)

                    turn_rows(0)
                    for u in range(UNITS):
                        if u % 2 == 0 and u + 2 < UNITS + 1:
                            turn_rows(u // 2 + 1)
                        if u >= 2:
                            rows_out(u - 2)
                        hidden(u)
                    rows_out(UNITS - 2)
                    rows_out(UNITS - 1)

                    base = QUADS * l
                    pe.wait_ge(cleared, s0 * 2 + l + 1)

                    def first_product(i, j):
                        i, j = i + j // SLOTS, j % SLOTS
                        pe.wait_ge(attr_in[j], 16 * (ROUNDS * l + i + 1))
                        wait(pe, acted, i * SLOTS + (base + j - 1))
                        nc.tensor.matmul(z_ps[:, j % 2, :], WE1[:, l, :, :], attr[:, j, :], start=True, stop=True)\
                          .then_inc(z_ready, 1)

                    def second_product(i, j):
                        i, j = i + j // SLOTS, j % SLOTS
                        pe.wait_ge(acted, i * SLOTS + (base + j + 1))
                        wait(pe, msg_ready, i * (SLOTS * wide) + wide * (base + j - 1))
                        nc.tensor.matmul(e_ps[:, j % 2, :], pick[:, :], bc(BE2s[:, l, :], 1, 2 * QUAD),
                                         start=True, stop=False, skip_group_check=True)
                        for k in range(QUAD):
                            last = nc.tensor.matmul(e_ps[:, j % 2, k * 2 * D:(k + 1) * 2 * D],
                                                    act_e[:, j % 2, k * P:(k + 1) * P], WE2[:, l, :, :],
                                                    start=False, stop=True, skip_group_check=True)
                        last.then_inc(e_ready, 1)

                    first_product(0, 0)
                    first_product(0, 1)
                    second_product(0, 0)

                    def products(i):
                        at = windows(i)
                        for j in range(SLOTS):
                            first_product(i, j + 2)
                            second_product(i, j + 1)
                            scatter(s, i, j, at, msg, msg_ready, base)

                    rounds(pe, products, l == 0, ROUNDS - 1)
                    at = windows(ROUNDS - 1)
                    for j in range(SLOTS):
                        if j + 2 < SLOTS:
                            first_product(ROUNDS - 1, j + 2)
                        if j + 1 < SLOTS:
                            second_product(ROUNDS - 1, j + 1)
                        scatter(s, ROUNDS - 1, j, at, msg, msg_ready, base)

            branch(pe, program)

        @block.vector
        def _(v):
            steps = [0]

            def link(ins):
                steps[0] += 1
                ins.then_inc(dve, 1)
                v.wait_ge(dve, steps[0])

            V = nc.vector
            v.wait_ge(consts, 17)
            v.wait_ge(loaded, ALL_IN)
            link(V.memset(agg_ps[:, :], 0.0))
            link(V.memset(z_ps[:, :, :], 0.0))
            link(V.memset(part[:, :], 0.0))
            link(V.tensor_copy(dstr_f[:, :, :], dstr_i[:, :, :]))
            link(V.tensor_reduce(low_r[:, :], dstr_f[:, :, :], AX.X, ALU.min))
            link(V.tensor_reduce(high_r[:, :], dstr_f[:, :, :], AX.X, ALU.max))
            for i_t, f_t, lo, hi in ((src_i, src_f, src_lo, src_hi), (dst_i, dst_f, dst_lo, dst_hi)):
                link(V.tensor_copy(f_t[:, :], i_t[:, :]))
                link(V.tensor_scalar(tmp_i[:, :], i_t[:, :], 7, None, ALU.arith_shift_right))
                link(V.tensor_copy(hi[:, :], tmp_i[:, :]))
                link(V.scalar_tensor_tensor(lo[:, :], hi[:, :], -float(P), f_t[:, :], ALU.mult, ALU.add))
            link(V.tensor_tensor(not_loop[:, :], src_f[:, :], dst_f[:, :], ALU.not_equal))
            link(V.tensor_scalar(cmp[:, :], src_hi[:, :], 1.0, None, ALU.add))
            link(V.tensor_tensor(cmp[:, :], cmp[:, :], not_loop[:, :], ALU.mult))
            link(V.tensor_scalar(out_hi[:, :], cmp[:, :], -1.0, None, ALU.add))
            link(V.tensor_copy(out_blocks[:, 0, :], out_hi[:, :]))
            link(V.tensor_tensor(out_blocks[:, 1, :], src_hi[:, :], cmp[:, :], ALU.subtract))
            link(V.tensor_copy(src_low[:, :], src_lo[:, :]))
            link(V.scalar_tensor_tensor(cmp[:, :], src_lo[:, :], float(NB), src_hi[:, :], ALU.mult, ALU.add))
            link(V.tensor_copy(idx_all[:, :], cmp[:, :]))
            v.wait_ge(range_in, 32)
            link(V.tensor_copy(first_i[:, :], first_node[:, :]))
            link(V.tensor_scalar(tmp_i[:, :], first_i[:, :], 7, None, ALU.arith_shift_right))
            link(V.tensor_copy(first_block[:, :], tmp_i[:, :]))
            link(V.scalar_tensor_tensor(key[:, :], src_hi[:, :], float(SPAN), dst_f[:, :], ALU.mult, ALU.add))
            link(V.tensor_tensor(key[:, :], key[:, :], first_node[:, :], ALU.subtract))
            link(V.tensor_tensor(near[:, :, 0], dst_hi[:, :], first_block[:, :], ALU.is_equal))
            link(V.tensor_scalar(cmp[:, :], first_block[:, :], 1.0, None, ALU.add))
            link(V.tensor_tensor(near[:, :, 1], dst_hi[:, :], cmp[:, :], ALU.is_equal))
            link(V.tensor_scalar(bank_of[:, :], first_block[:, :], 7.0, None, ALU.is_ge))
            for edge in (14.0, 21.0):
                link(V.tensor_scalar(cmp[:, :], first_block[:, :], edge, None, ALU.is_ge))
                link(V.tensor_tensor(bank_of[:, :], bank_of[:, :], cmp[:, :], ALU.add))
            link(V.tensor_tensor(window_f[:, :], first_block[:, :], bank_of[:, :], ALU.add))
            link(V.tensor_scalar(window_f[:, :], window_f[:, :], float(D), None, ALU.mult))
            link(V.tensor_copy(window_at[:, :], window_f[:, :]))
            link(V.tensor_tensor(cmp[:, :], last_node[:, :], first_node[:, :], ALU.subtract))
            link(V.tensor_scalar(window_f[:, :], cmp[:, :], float(SPAN), None, ALU.is_ge))
            link(V.tensor_reduce(spread[:, 0:1], window_f[:, :], AX.X, ALU.max))
            link(V.tensor_scalar(window_f[:, :], cmp[:, :], 1.0, None, ALU.is_lt))
            link(V.tensor_reduce(spread[:, 1:2], window_f[:, :], AX.X, ALU.max))
            link(V.tensor_tensor(window_f[:, 0:TILES - 1], last_node[:, 0:TILES - 1], first_node[:, 1:TILES], ALU.is_gt))
            link(V.tensor_reduce(spread[:, 2:3], window_f[:, 0:TILES - 1], AX.X, ALU.max))
            link(V.tensor_reduce(spread[:, 3:4], spread[:, 0:3], AX.X, ALU.max))
            V.tensor_copy(spread_i[:, :], spread[:, 3:4]).then_inc(flag_ready, 1)

            began = steps[0]

            def program(wide):
                steps[0] = began
                roots = [0]
                dense = [wide == 1]

                def root(ins):
                    roots[0] += 1
                    ins.then_inc(dense_root_in if dense[0] else root_in, 1)
                    v.wait_ge(dense_rooted if dense[0] else rooted, roots[0])

                given = {}

                def give(ins, semaphore):
                    given[semaphore.name] = given.get(semaphore.name, 0) + 1
                    ins.then_inc(semaphore, 1)
                    v.wait_ge(semaphore, given[semaphore.name])

                def late_weights_ready():
                    v.wait_ge(late, 16 * (len(late_weights) + (1 if wide == 1 else 0)))
                    link(V.memset(W1[0:D, :, 1, :], 0.0))
                    link(V.memset(W1[D:P, :, 0, :], 0.0))
                    link(V.tensor_scalar(WE1[:, :, 1, :], WE1[:, :, 1, :], -1.0, None, ALU.mult))
                    link(V.tensor_scalar(BE1[D:P, :], BE1[D:P, :], -1.0, None, ALU.mult))
                    link(V.tensor_scalar(WE2[D:P, :, :, :], WE2[D:P, :, :, :], -0.1, None, ALU.mult))
                    link(V.memset(BE2s[:, :, :], 0.0))
                    link(V.tensor_copy(BE2p[:, 0, :, :], BE2[:, :, :]))
                    link(V.tensor_tensor(BE2r[:, :, :], BE2[:, :, :], BE2p[:, 0, :, :], ALU.subtract))
                    link(V.tensor_copy(BE2p[:, 1, :, :], BE2r[:, :, :]))
                    link(V.tensor_tensor(BE2r[:, :, :], BE2r[:, :, :], BE2p[:, 1, :, :], ALU.subtract))
                    link(V.tensor_copy(BE2p[:, 2, :, :], BE2r[:, :, :]))
                    for r in range(3):
                        link(V.tensor_copy(BE2s[32 * r:32 * r + 1, :, :], BE2p[32 * r:32 * r + 1, r, :, :]))
                    link(V.tensor_tensor(RW[:, :], RW[:, :], DS[:, :], ALU.mult))

                def out_degrees(counted_out):
                    link(V.tensor_scalar(stat[:, 7, :], counted_out, 0.0, None, ALU.is_gt))
                    root(V.tensor_scalar(stat[:, 6, :], counted_out, 1.0, None, ALU.max))
                    link(V.reciprocal(stat[:, 6, :], stat[:, 6, :]))
                    link(V.tensor_tensor(dinv[:, :], stat[:, 6, :], stat[:, 7, :], ALU.mult))
                    link(V.tensor_scalar(ndinv[:, :], dinv[:, :], -1.0, None, ALU.mult))

                def gathered_degrees():
                    for w in range(2 * wide):
                        link(V.tensor_scalar(masks[:, :, w], dst_hi[:, :], float(w), None, ALU.is_equal))

                    def hist(i):
                        for j in range(2):
                            wait(v, hist_done, i * 2 + (j - 1))
                            t = bass.ds((i * 2 + j) * QUAD, QUAD)
                            for hot, lo in ((onehot, dst_lo), (onehot_src, src_lo)):
                                V.tensor_tensor(hot[:, j, :, :], bc(iota_lo[:, :], 1, QUAD), bc(lo[:, t], 2, P),
                                                ALU.is_equal)
                            V.tensor_tensor(hot_hi[:, j, 0, :, :], bc(iota_hi[:, :], 1, QUAD), bc(dst_hi[:, t], 2, MASKS),
                                            ALU.is_equal)
                            V.tensor_tensor(hot_hi[:, j, 1, :, :], bc(iota_hi[:, :], 1, QUAD), bc(out_hi[:, t], 2, MASKS),
                                            ALU.is_equal).then_inc(hist_hot, 1)

                    rounds(v, hist, True, QUADS // 2)
                    v.wait_ge(hist_done, QUADS)
                    link(V.tensor_scalar(stat[:, 0, :], z_ps[:, 0, 0:NB], 1.0, None, ALU.max))
                    link(V.reciprocal(rdeg[:, :], stat[:, 0, :]))
                    out_degrees(z_ps[:, 1, 0:NB])

                def count_edges():
                    ring = SLOTS * QUAD
                    v.wait_ge(kept, 16)
                    for c in range(ZEROED):
                        V.memset(adj[:, c, :], 0.0).then_inc(adj_zero, 1)

                    def hot_keys(i, j):
                        V.tensor_scalar(hot_key[:, j % 4, :], iota_key[:, :], key[:, bass.ds(i * ring + j, 1)], None,
                                        ALU.is_equal).then_inc(key_ready, 1)

                    def hot_outs(i, j):
                        of = bass.ds(i * ring + j, OUTS)
                        V.tensor_tensor(hot_out[:, j // OUTS % 2, :, :, :],
                                        iota_hi[:, 0:NB].unsqueeze(1).unsqueeze(1).to_broadcast([P, OUTS, 2, NB]),
                                        bc(out_blocks[:, :, of].rearrange("p w t -> p t w"), 3, NB),
                                        ALU.is_equal).then_inc(out_ready, 1)

                    hot_keys(0, 0)
                    hot_keys(0, 1)
                    hot_outs(0, 0)
                    v.wait_ge(adj_zero, NB)

                    def tiles(i, last=False):
                        _, first = nc.values_load_multi_w_load_instructions(
                            first_i[0:1, bass.ds(i * ring, ring)], engines=[v.engine], min_val=0, max_val=NODES - 1,
                            bass_reorder=False,
                            skip_runtime_bounds_check_because="the narrow program's tiles begin at real nodes")
                        for j in range(ring):
                            if not last or j + 2 < ring:
                                wait(v, counted, i * ring + (j - 1))
                                hot_keys(i, j + 2)
                                if (j + 2) % OUTS == 0:
                                    hot_outs(i, j + 2)
                            v.wait_ge(counts_ready, i * ring + (j + 1))
                            wait(v, added, i * ring + j)
                            to = adj[:, :, bass.ds(first[j], SPAN)]
                            V.tensor_tensor(to, to, counts[:, j % SLOTS, :].rearrange("p (c n) -> p c n", n=SPAN),
                                            ALU.add).then_inc(added, 1)

                    rounds(v, tiles, True, ROUNDS - 1)
                    tiles(ROUNDS - 1, last=True)
                    v.wait_ge(added, TILES)
                    link(V.tensor_scalar(loops[:, :], z_ps[:, 0, NB:2 * NB], -1.0, None, ALU.mult))
                    out_degrees(z_ps[:, 0, 0:NB])
                    link(V.memset(parts[:, :, 3 * D:PW], 1.0))

                def per_node(t):
                    return bc(t, 2, D)

                def norm(to, of, centred, relu, last=None):
                    n = to.shape[1]
                    mean, power = stat[:, 0, 0:n], stat[:, 1, 0:n]
                    link(V.tensor_reduce(mean, of, AX.X, ALU.add))
                    link(V.tensor_scalar(mean, mean, 1.0 / D, None, ALU.mult))
                    link(V.tensor_tensor(centred, of, per_node(mean), ALU.subtract))
                    link(V.tensor_tensor(to, centred, centred, ALU.mult))
                    link(V.tensor_reduce(power, to, AX.X, ALU.add))
                    root(V.tensor_scalar(power, power, 1.0 / D, None, ALU.mult))
                    link(V.reciprocal(power, power))
                    if relu:
                        link(V.tensor_scalar(centred, centred, 0.0, None, ALU.max))
                    ins = V.tensor_tensor(to, centred, per_node(power), ALU.mult)
                    give(ins, last) if last is not None else link(ins)

                own, neighbours = cat[:, :, 0:D], cat[:, :, D:2 * D]

                def split(half, scaled):
                    b = slice(0, HALF) if half == 0 else slice(HALF, NB)
                    of, rest = own[:, b, :], neighbours[:, b, :]
                    if scaled:
                        link(V.tensor_tensor(rest, of, per_node(dinv[:, b]), ALU.mult))
                        of = rest
                    for k in range(3):
                        ins = V.tensor_copy(parts[:, b, k * D:(k + 1) * D], of)
                        if k == 2:
                            give(ins, parts_ready)
                        else:
                            link(ins)
                            link(V.tensor_tensor(rest, of, parts[:, b, k * D:(k + 1) * D], ALU.subtract))
                            of = rest

                def dense_stages():
                    norm(own, X[:, :, :], neighbours, True)
                    split(0, False)
                    split(1, False)
                    for s in range(DENSE):
                        for it in range(NQ + 2):
                            if it < NQ:
                                neighbours_sum(s, it)
                            if it == NQ and s == DENSE - 1:
                                v.wait_ge(nb_ready, NQ * DENSE)
                                v.sem_inc(adj_free, 1)
                            if it >= 2:
                                after_projection(s, it - 2)
                        if s >= 3:
                            norm_all(s - 3, own, neighbours)
                            if s == 3:
                                link(V.tensor_copy(X1[:, :, :], own))
                            if s == 4:
                                link(V.tensor_scalar(own, own, 0.0, None, ALU.max))
                        if s == 2:
                            for c in range(NB):
                                n = min(P, ACOLS - c * P)
                                at = adj[:, c, c * P:c * P + n]
                                V.scalar_tensor_tensor(at, ident[:, 0:n], loops[:, c:c + 1], at, ALU.mult, ALU.add)
                        if s < DENSE - 1:
                            split(0, s >= 2)
                            split(1, s >= 2)

                def neighbours_sum(s, g):
                    b0, n = dims(g)
                    b = slice(b0, b0 + n)
                    at = g % 2 * 2 * BANK
                    sums = agg_ps[:, at:at + n * (BANK // 2)].rearrange("p (b w) -> p b w", w=BANK // 2)
                    v.wait_ge(nb_ready, NQ * s + g + 1)
                    if s == 0:
                        link(V.tensor_scalar(stat[:, 0, b], sums[:, :, 3 * D], 1.0, None, ALU.max))
                        link(V.reciprocal(rdeg[:, b], stat[:, 0, b]))
                    give(V.tensor_reduce(neighbours[:, b, :],
                                         sums[:, :, 0:3 * D].rearrange("p b (k d) -> p b d k", k=3), AX.X, ALU.add),
                         nb_taken)
                    give(V.tensor_tensor(neighbours[:, b, :], neighbours[:, b, :],
                                         per_node((rdeg if s < 3 else ndinv)[:, b]), ALU.mult), cat_ready)

                def after_projection(s, g):
                    b0, n = dims(g)
                    b = slice(b0, b0 + n)
                    h, scratch = own[:, b, :], neighbours[:, b, :]
                    v.wait_ge(cat_out, NQ * s + g + 1)
                    give(V.tensor_tensor(h if s in (0, 3, 4, 5) else scratch,
                                         e_ps[:, g % 2, 0:n * D].rearrange("p (b d) -> p b d", d=D),
                                         bc(Bp[:, s, :], 1, n), ALU.add), cat_taken)
                    if s in (1, 2):
                        if s == 2:
                            link(V.tensor_scalar(scratch, scratch, 0.0, None, ALU.max))
                        link(V.tensor_tensor(X[:, b, :], X[:, b, :], scratch, ALU.add))
                        norm(h, X[:, b, :], scratch, True)
                    if s >= 3:
                        if g == NQ - 1:
                            link(V.tensor_tensor(own[:, NB - 1:NB, :], own[:, NB - 1:NB, :],
                                                 per_node(real[:, NB - 1:NB]), ALU.mult))
                        link(V.tensor_reduce(stat[:, 2, b], h, AX.X, ALU.add))

                def norm_all(i, to, scratch):
                    give(V.tensor_reduce(part[:, 0:1], stat[:, 2, :], AX.X, ALU.add), sum_in)
                    v.wait_ge(summed, 2 * i + 1)
                    link(V.tensor_scalar(part[:, 2:3], z_ps[:, 0, 0:1], 1.0 / (NODES * D), None, ALU.mult))
                    link(V.tensor_scalar(to, to, part[:, 2:3], None, ALU.subtract))
                    link(V.tensor_tensor(to[:, NB - 1:NB, :], to[:, NB - 1:NB, :], per_node(real[:, NB - 1:NB]), ALU.mult))
                    link(V.tensor_tensor(scratch, to, to, ALU.mult))
                    link(V.tensor_reduce(stat[:, 2, :], scratch, AX.X, ALU.add))
                    give(V.tensor_reduce(part[:, 1:2], stat[:, 2, :], AX.X, ALU.add), sum_in)
                    v.wait_ge(summed, 2 * i + 2)
                    root(V.tensor_scalar(part[:, 4:5], z_ps[:, 0, 0:1], 1.0 / (NODES * D), None, ALU.mult))
                    link(V.reciprocal(part[:, 3:4], part[:, 4:5]))
                    link(V.tensor_tensor(part[:, 3:4], part[:, 3:4], gam[:, i:i + 1], ALU.mult))
                    link(V.tensor_scalar(to, to, part[:, 3:4], bet[:, i:i + 1], ALU.mult, ALU.add))

                def agg_view():
                    if wide > 1:
                        return [(0, NB, agg_ps[:, 0:NB * D].rearrange("p (b d) -> p b d", d=D))]
                    got = []
                    for k in range(4):
                        n = min(7, NB - 7 * k)
                        got.append((7 * k, n, agg_ps[:, k * BANK:k * BANK + n * D].rearrange("p (b d) -> p b d", d=D)))
                    return got

                def edges(s, l):

                    def quads(i):
                        for j in range(SLOTS):
                            t = bass.ds((i * SLOTS + j) * QUAD, QUAD)
                            wait(v, scattered, i * (SLOTS * wide) + wide * (QUADS * s + j - 1))
                            V.tensor_tensor(onehot[:, j % 2, :, :], bc(iota_lo[:, :], 1, QUAD), bc(dst_lo[:, t], 2, P),
                                            ALU.is_equal).then_inc(hot_ready, 1)
                            v.wait_ge(gathered[j], i * (16 * QUAD) + 16 * QUAD * (ROUNDS * s + 1))
                            for w in range(wide):
                                at = (j * wide + w) % 2
                                units = i * (SLOTS * wide)
                                u = wide * (QUADS * s + j) + w
                                ue = wide * (QUADS * l + j) + w
                                if l < 0:
                                    wait(v, scattered, units + (u - 1))
                                else:
                                    wait(v, msg_ready, units + (ue - 1))
                                V.tensor_tensor(masked[:, at, :, :, :], bc(rows[:, j, :, :], 2, 2),
                                                bc(by_block[:, t, 2 * w:2 * w + 2], 3, D), ALU.mult)\
                                 .then_inc(masked_ready, 1)
                                if l < 0:
                                    continue
                                if w == 0:
                                    v.wait_ge(e_ready, i * SLOTS + (QUADS * l + j + 1))
                                v.wait_ge(masked_ready, units + (u + 1))
                                wait(v, scattered, units + (u - 1))
                                V.tensor_tensor(msg[:, at, :, :, :], masked[:, at, :, :, :],
                                                e_ps[:, j % 2, :].rearrange("p (k w d) -> p k w d", k=QUAD, w=2),
                                                ALU.mult).then_inc(msg_ready, 1)

                    rounds(v, quads, s == 0 or l == 0)
                    v.wait_ge(scattered, wide * QUADS * (s + 1))

                by_block = near if wide == 1 else masks

                def clear():
                    give(V.memset(agg_ps[:, :], 0.0), cleared)

                def take_agg(to):
                    for b0, n, view in agg_view():
                        link(V.tensor_copy(to[:, b0:b0 + n, :], view))
                    if wide == 1:
                        for k in range(3):
                            b = 7 * (k + 1)
                            link(V.tensor_tensor(to[:, b, :], to[:, b, :],
                                                 agg_ps[:, k * BANK + 7 * D:k * BANK + 8 * D], ALU.add))

                def projection(s):
                    v.wait_ge(projected, s + 1)
                    return agg_ps[:, 0:NB * D].rearrange("p (b d) -> p b d", d=D)

                def gathered_stages():
                    norm(H[:, :, :], X[:, :, :], S0[:, :, :], True, table_due)
                    for s in range(3):
                        clear()
                        edges(s, -1)
                        link(V.tensor_copy(cat[:, :, 0:D], H[:, :, :]))
                        take_agg(S0)
                        give(V.tensor_tensor(cat[:, :, D:2 * D], S0[:, :, :], per_node(rdeg[:, :]), ALU.mult), node_in)
                        clear()
                        y = projection(s)
                        ins = V.tensor_tensor(H[:, :, :], y, bc(Bp[:, s, :], 1, NB), ALU.add)
                        give(ins, table_due) if s == 0 else link(ins)
                        if s == 2:
                            link(V.tensor_scalar(H[:, :, :], H[:, :, :], 0.0, None, ALU.max))
                        if s:
                            link(V.tensor_tensor(X[:, :, :], X[:, :, :], H[:, :, :], ALU.add))
                            norm(H[:, :, :], X[:, :, :], S0[:, :, :], True, table_due if s == 1 else None)

                    for w in range(2 * wide):
                        link(V.tensor_copy(cmp[:, :], masks[:, :, w]))
                        link(V.tensor_tensor(masks[:, :, w], cmp[:, :], not_loop[:, :], ALU.mult))
                    link(V.tensor_copy(cat[:, :, 0:D], H[:, :, :]))
                    for i in range(3):
                        s = 3 + i
                        give(V.tensor_tensor(H[:, :, :], cat[:, :, 0:D], per_node(dinv[:, :]), ALU.mult), table_due)
                        clear()
                        edges(s, -1)
                        take_agg(S0)
                        give(V.tensor_tensor(cat[:, :, D:2 * D], S0[:, :, :], per_node(ndinv[:, :]), ALU.mult), node_in)
                        clear()
                        y = projection(s)
                        link(V.tensor_tensor(own, y, bc(Bp[:, s, :], 1, NB), ALU.add))
                        link(V.tensor_tensor(own, own, per_node(real[:, :]), ALU.mult))
                        link(V.tensor_reduce(stat[:, 2, :], own, AX.X, ALU.add))
                        norm_all(i, own, neighbours)
                        if i == 0:
                            link(V.tensor_copy(X1[:, :, :], cat[:, :, 0:D]))
                        if i == 1:
                            link(V.tensor_scalar(cat[:, :, 0:D], cat[:, :, 0:D], 0.0, None, ALU.max))

                if wide == 1:
                    count_edges()
                    dense_stages()
                else:
                    late_weights_ready()
                    gathered_degrees()
                    gathered_stages()
                link(V.tensor_tensor(neighbours, X1[:, :, :], own, ALU.add))
                link(V.tensor_scalar(neighbours, neighbours, 0.5, 0.0, ALU.mult, ALU.max))
                link(V.tensor_tensor(X[:, :, :], X[:, :, :], neighbours, ALU.add))
                if wide == 1:
                    late_weights_ready()

                def mark(ins):
                    steps[0] += 1
                    ins.then_inc(dve, 1)
                    return steps[0]

                def norm_rows(k, of, relu):
                    cut = [slice(b0, b1) for b0, b1 in CHUNKS]
                    made = [mark(V.tensor_reduce(stat[:, 0, c], of[:, c, :], AX.X, ALU.add)) for c in cut]
                    for c, summed_up in zip(cut, made):
                        v.wait_ge(dve, summed_up)
                        V.scalar_tensor_tensor(neighbours[:, c, :], per_node(stat[:, 0, c]), -1.0 / D, of[:, c, :],
                                               ALU.mult, ALU.add).then_inc(square_in, 1)
                    for j, c in enumerate(cut):
                        v.wait_ge(squared, len(cut) * k + j + 1)
                        V.tensor_reduce(stat[:, 1, c], own[:, c, :], AX.X, ALU.add).then_inc(power_in, 1)
                    if relu:
                        for c in cut:
                            link(V.tensor_scalar(neighbours[:, c, :], neighbours[:, c, :], 0.0, None, ALU.max))
                    for j, c in enumerate(cut):
                        v.wait_ge(power_rooted, len(cut) * k + j + 1)
                        link(V.reciprocal(stat[:, 1, c], stat[:, 1, c]))
                        V.tensor_tensor(rows_buf[:, :].rearrange("p (b d) -> p b d", d=D)[:, c, :], neighbours[:, c, :],
                                        per_node(stat[:, 1, c]), ALU.mult).then_inc(rows_in, 1)

                norm_rows(0, X[:, :, :], True)

                normed = rows_buf[:, :].rearrange("p (b d) -> p b d", d=D)

                def rows_done(l, k):
                    b = slice(8 * k, min(8 * k + 8, NB))
                    v.wait_ge(rows_projected, (UNITS + 1) // 2 * l + k + 1)
                    return V.tensor_tensor(H[:, b, :], agg_ps[:, b.start * D:b.stop * D].rearrange("p (b d) -> p b d", d=D),
                                           bc(B2[:, l, :], 1, b.stop - b.start), ALU.add)

                for l in range(LAYERS):
                    s = l if wide == 1 else DENSE + l
                    for u in range(UNITS):
                        _, n = dims(u)
                        v.wait_ge(hid_z_ready, UNITS * l + u + 1)
                        V.scalar_tensor_tensor(hid[:, u % 2, 0:n * P], hid_z[:, u % 2, 0:n * P], 0.1,
                                               hid_z[:, u % 2, 0:n * P], ALU.mult, ALU.max).then_inc(hid_ready, 1)
                        if u in (3, 5):
                            rows_done(l, u // 2 - 1)
                    rows_done(l, 2)
                    give(rows_done(l, 3), table_due)
                    clear()
                    v.wait_ge(rows_in, len(CHUNKS) * (l + 1))
                    if l == 0:
                        link(V.tensor_copy(X1[:, :, :], normed))
                    else:
                        link(V.tensor_tensor(X1[:, :, :], normed, bc(LG[:, l - 1, :], 1, NB), ALU.mult))
                        link(V.tensor_tensor(X1[:, :, :], X1[:, :, :], bc(LB[:, l - 1, :], 1, NB), ALU.add))
                    if l == 0 and wide > 1:
                        for w in range(2 * wide):
                            link(V.tensor_scalar(masks[:, :, w], dst_hi[:, :], float(w), None, ALU.is_equal))
                    edges(s, l)
                    for b0, n, view in agg_view():
                        link(V.scalar_tensor_tensor(H[:, b0:b0 + n, :], view, RW[:, l:l + 1], X1[:, b0:b0 + n, :],
                                                    ALU.mult, ALU.add))
                    if wide == 1:
                        for k in range(3):
                            b = 7 * (k + 1)
                            link(V.scalar_tensor_tensor(H[:, b, :], agg_ps[:, k * BANK + 7 * D:k * BANK + 8 * D],
                                                        RW[:, l:l + 1], H[:, b, :], ALU.mult, ALU.add))
                    norm_rows(l + 1, H[:, :, :], False)
                v.wait_ge(rows_in, len(CHUNKS) * (LAYERS + 1))
                link(V.tensor_tensor(X1[:, :, :], normed, bc(LG[:, LAYERS - 1, :], 1, NB), ALU.mult))
                link(V.tensor_tensor(X1[:, :, :], X1[:, :, :], bc(LB[:, LAYERS - 1, :], 1, NB), ALU.add))
                V.tensor_tensor(X[:, :, :], X[:, :, :], X1[:, :, :], ALU.add).then_inc(out_due, 1)

            branch(v, program)


_OUTS = [((3125, 64), "float32")]


def kernel(**inputs):
    import numpy as np
    import concourse.bacc as bacc
    from concourse import mybir as mb
    from concourse.bass_utils import run_bass_kernel_spmd as run

    a = {k: np.asarray(v) for k, v in inputs.items()}
    pad = EPAD - EDGES
    src = np.concatenate([a["src"].astype(np.int32), np.full(pad, NODES, np.int32)])
    dst = np.concatenate([a["dst"].astype(np.int32), np.full(pad, NODES, np.int32)])
    attr_t = np.zeros((ED, EPAD), np.float32)
    attr_t[:, :EDGES] = a["edge_attr_32"].T
    arrays = {
        "x": a["x"], "src_t": src.reshape(TILES, P).T, "dst_t": dst.reshape(TILES, P).T,
        "dst_r": dst.reshape(ROWS, 4 * P), "attr_t": attr_t,
        "w_self1": a["L0_gnn_W_self1"], "w_neigh1": a["L0_gnn_W_neigh1"], "b_1": a["L0_gnn_b1"],
        "w_self2": a["L0_gnn_W_self2"], "w_neigh2": a["L0_gnn_W_neigh2"], "b_2": a["L0_gnn_b2"],
        "w_l": a["L1_gnn_W_l"], "w_r": a["L1_gnn_W_r"], "b_m": a["L1_gnn_b"],
        "w0_t": a["L2_gnn_W0"].transpose(0, 2, 1), "w1_t": a["L2_gnn_W1"].transpose(0, 2, 1),
        "b_c": a["L2_gnn_b"], "gamma": a["L2_gnn_gamma"], "beta": a["L2_gnn_beta"],
        "w1": a["L3_gnn_W1"], "b1_t": a["L3_gnn_b1"].T, "w2": a["L3_gnn_W2"], "b2": a["L3_gnn_b2"],
        "we1": a["L3_gnn_We1"], "be1_t": a["L3_gnn_be1"].T, "we2": a["L3_gnn_We2"], "be2": a["L3_gnn_be2"],
        "res_w": a["L3_gnn_res_w"], "dot_scale": a["L3_gnn_dot_scale"], "ln_g": a["L3_gnn_ln_g"],
        "ln_b": a["L3_gnn_ln_b"], "ln_g_t": a["L3_gnn_ln_g"].T, "ln_b_t": a["L3_gnn_ln_b"].T,
    }
    nc = bacc.Bacc("TRN2", target_bir_lowering=False, num_devices=1)
    args = []
    for name, v in arrays.items():
        arrays[name] = v = np.ascontiguousarray(v)
        args.append(nc.dram_tensor(name, v.shape, mb.dt.from_np(v.dtype), kind="ExternalInput").ap())
    for i, (shape, dtype) in enumerate(_OUTS):
        args.append(nc.dram_tensor(f"out_{i}", shape, mb.dt.from_np(np.dtype(dtype)), kind="ExternalOutput").ap())
    gnn_program(nc, *args)
    got = run(nc, [arrays], core_ids=[0])
    return got.results[0]["out_0"]
```

```python
import concourse.bass as bass
from concourse import mybir
from contextlib import ExitStack

NODES, D, EDGES, ED, LAYERS = 3125, 64, 53125, 32, 5
P = 128
NB = -(-NODES // P)
NPAD = NB * P
TILES = -(-EDGES // P)
EPAD = TILES * P
QUAD = 4
QUADS = TILES // QUAD
SLOTS = 4
ROUNDS = QUADS // SLOTS
BANK = 512
STAGES = 2 + 1 + 3 + LAYERS
LAST_BLOCK = NODES - (NB - 1) * P
ROWS = TILES // 4
PAIRS = (NB + 1) // 2
MASKS = 2 * PAIRS
DENSE = STAGES - LAYERS
SPAN = 12
KEYS = NB * SPAN
ACOLS = NODES + SPAN - 1
PW = 3 * D + 2
OUTS = 8
HALF = (NB + 1) // 2
HALVES = (slice(0, HALF), slice(HALF, NB))
CHUNKS = ((0, 8), (8, 16), (16, NB))
COUNTED = 6
EARLY = 16
UNITS = -(-NB // QUAD)
ZEROED = 5
SHARE = 8
assert TILES % (QUAD * SLOTS) == 0


def gnn_program(nc, x, src_t, dst_t, dst_r, attr_t, w_self1, w_neigh1, b_1, w_self2, w_neigh2, b_2,
                w_l, w_r, b_m, w0_t, w1_t, b_c, gamma, beta, w1, b1_t, w2, b2, we1, be1_t, we2, be2,
                res_w, dot_scale, ln_g, ln_b, ln_g_t, ln_b_t, out):
    f32, i32, bf16 = mybir.dt.float32, mybir.dt.int32, mybir.dt.bfloat16
    ALU, ACT, AX = mybir.AluOpType, mybir.ActivationFunctionType, mybir.AxisListType
    ctx = ExitStack()
    with ctx:
        def sb(name, shape, dt=f32):
            return ctx.enter_context(nc.sbuf_tensor(name, shape, dt))

        def sem(name):
            return ctx.enter_context(nc.semaphore(name))

        def bc(ap, axis, n):
            a = ap.unsqueeze(axis)
            shape = list(a.shape)
            shape[axis] = n
            return a.to_broadcast(shape)

        table = nc.dram_tensor("table", (NPAD, D), f32, kind="Internal").ap()
        saved_tables = nc.dram_tensor("saved_tables", (P, 5 * TILES), f32, kind="Internal").ap()
        tile_range = nc.dram_tensor("tile_range", (2, TILES), f32, kind="Internal").ap()

        adj = sb("adj", [P, NB, ACOLS], bf16)
        flat = adj[:, :, :].rearrange("p c n -> p (c n)")
        taken = [0]

        def carve(shape, dt=f32):
            size = 1
            for n in shape[1:]:
                size *= n
            halves = size * (1 if dt == bf16 else 2)
            lo = taken[0]
            taken[0] = lo + halves + halves % 2
            assert taken[0] <= NB * ACOLS, "adj's memory is full"
            t = flat[0:shape[0], lo:lo + halves]
            if dt != bf16:
                t = t.bitcast(dt)
            names = "abcd"[:len(shape) - 1]
            if len(names) > 1:
                t = t.rearrange(f"p ({' '.join(names)}) -> p {' '.join(names)}", **dict(zip(names, shape[1:])))
            return t

        tables = carve([P, 5, TILES])
        idx_all = tables[:, 0, :].bitcast(i32)
        window_at = tables[:, 1, :].bitcast(i32)
        dst_lo = tables[:, 2, :]
        near = tables[:, 3:5, :].rearrange("p w t -> p t w")
        rows = carve([P, SLOTS, QUAD, D])
        onehot = carve([P, 2, QUAD, P])
        masked = carve([P, 2, QUAD, 2, D])
        msg = carve([P, 2, QUAD, 2, D])
        attr = carve([P, SLOTS, QUAD * P])[0:ED]
        act_e = carve([P, 2, QUAD * P])
        XT = carve([P, NPAD])
        hid_z = carve([P, 2, BANK])
        hid = carve([P, QUAD, BANK])
        S0 = carve([P, NB, D])
        rows_buf = S0.rearrange("p b d -> p (b d)")
        H = carve([P, NB, D])
        W1 = carve([P, LAYERS, 2, 2 * D])
        B1 = carve([P, LAYERS])
        W2 = carve([P, LAYERS, D])
        B2 = carve([P, LAYERS, D])
        WE1 = carve([P, LAYERS, 2, D])[0:ED]
        BE1 = carve([P, LAYERS])
        WE2 = carve([P, LAYERS, 2, D])
        BE2 = carve([P, LAYERS, D])
        BE2r = carve([P, LAYERS, D])
        BE2p = carve([P, 3, LAYERS, D], bf16)
        BE2s = carve([P, LAYERS, D], bf16)
        RW = carve([P, LAYERS])
        DS = carve([P, LAYERS])
        LGT = carve([P, LAYERS])
        LBT = carve([P, LAYERS])
        LG = carve([P, LAYERS, D])
        LB = carve([P, LAYERS, D])
        onehot_src = carve([P, 2, QUAD, P])
        hot_hi = carve([P, 2, 2, QUAD, MASKS])
        set_up_from = taken[0]
        dst_hi = carve([P, TILES])
        src_lo = carve([P, TILES])
        out_hi = carve([P, TILES])
        cmp = carve([P, TILES])
        masks = carve([P, TILES, MASKS])
        taken[0] -= 2 * TILES * MASKS
        src_i = carve([P, TILES], i32)
        dst_i = carve([P, TILES], i32)
        tmp_i = carve([P, TILES], i32)
        src_f = carve([P, TILES])
        dst_f = carve([P, TILES])
        src_hi = carve([P, TILES])
        dstr_i = carve([P, 4, P], i32)[0:ROWS]
        dstr_f = carve([P, 4, P])[0:ROWS]
        low_r = carve([P, 4])[0:ROWS]
        high_r = carve([P, 4])[0:ROWS]
        first_node = carve([P, TILES])
        last_node = carve([P, TILES])
        first_block = carve([P, TILES])
        bank_of = carve([P, TILES])
        window_f = carve([P, TILES])
        spread = carve([P, 4])

        early_zero = [c for c in range(NB) if c * ACOLS >= 10 * TILES and (c + 1) * ACOLS <= set_up_from]
        late_zero = [c for c in range(NB) if c not in early_zero][::-1]
        not_loop = sb("not_loop", [P, TILES])
        spread_i = sb("spread_i", [P, 1], i32)
        iota_lo = sb("iota_lo", [P, P])
        iota_hi = sb("iota_hi", [P, MASKS])
        idx_slot = sb("idx_slot", [P, SLOTS * QUAD], i32)
        low_slot = sb("low_slot", [P, SLOTS * QUAD])

        X = sb("X", [P, NB, D])
        X1 = sb("X1", [P, NB, D])
        cat = sb("cat", [P, NB, 2 * D])
        turned_rows = sb("turned_rows", [P, 2, BANK])
        parts = sb("parts", [P, NB, PW], bf16)
        stat = sb("stat", [P, 8, NB])
        real = sb("real", [P, NB])
        rdeg = sb("rdeg", [P, NB])
        dinv = sb("dinv", [P, NB])
        ndinv = sb("ndinv", [P, NB])
        ident = sb("ident", [P, P])
        ones = sb("ones", [P, P])
        part = sb("part", [P, 8])
        outs = sb("outs", [P, NB])
        loops = sb("loops", [P, NB])
        eps5 = sb("eps5", [P, 1])
        eps3 = sb("eps3", [P, 1])
        zero = sb("zero", [P, 1])
        pick = sb("pick", [P, P], bf16)
        Wp = sb("Wp", [P, 6, D])
        Bp = sb("Bp", [P, 6, D])
        gam = sb("gam", [P, 3])
        bet = sb("bet", [P, 3])
        iota_key = sb("iota_key", [P, KEYS], mybir.dt.float16)
        iota_low = sb("iota_low", [P, P], mybir.dt.float16)
        all_but_last = flat[:, 0:(NB - 1) * (ACOLS + P)].rearrange("p (c n) -> p c n", n=ACOLS + P)[:, :, 0:P]
        loops_diagonal = X1[:, :, :].rearrange("p b d -> p (b d)").bitcast(bf16).rearrange("p (c n) -> p c n", n=P)
        diagonals = ((loops_diagonal[:, 0:NB - 1, :], all_but_last),
                     (loops_diagonal[:, NB - 1:NB, 0:ACOLS - (NB - 1) * P], adj[:, NB - 1:NB, (NB - 1) * P:ACOLS]))
        both = X1[:, :, :].rearrange("p b d -> p (b d)").bitcast(bf16)
        hot_key = both[:, 0:4 * KEYS].rearrange("p (s k) -> p s k", s=4)
        counts = both[:, 4 * KEYS:8 * KEYS].rearrange("p (s k) -> p s k", s=4)
        hot_low = turned_rows[:, :, :].rearrange("p a b -> p (a b)").bitcast(bf16).rearrange("p (s k) -> p s k", k=P)
        edge_keys = parts[:, :, :].rearrange("p b d -> p (b d)")[:, 0:6 * TILES].bitcast(f32)\
            .rearrange("p (k t) -> p k t", k=3)
        key = edge_keys[:, 0, :]
        src_low = edge_keys[:, 1, :]
        first_i = edge_keys[:, 2, :].bitcast(i32)

        agg_ps = ctx.enter_context(nc.psum_tensor("agg_ps", [P, 4 * BANK], f32))
        z_ps = ctx.enter_context(nc.psum_tensor("z_ps", [P, 2, BANK], f32))
        e_ps = ctx.enter_context(nc.psum_tensor("e_ps", [P, 2, BANK], f32))

        edges_in = sem("edges_in")
        loaded = sem("loaded")
        range_out = sem("range_out")
        range_in = sem("range_in")
        consts = sem("consts")
        flag_ready = sem("flag_ready")
        dve = sem("dve")
        hist_hot = sem("hist_hot")
        hist_done = sem("hist_done")
        early_due = sem("early_due")
        table_due = sem("table_due")
        table_in = sem("table_in")
        idx_in = [sem(f"idx_in{j}") for j in range(SLOTS)]
        idx_seen = sem("idx_seen")
        gathered = [sem(f"gathered{j}") for j in range(SLOTS)]
        masked_ready = sem("masked_ready")
        hot_ready = sem("hot_ready")
        msg_ready = sem("msg_ready")
        scattered = sem("scattered")
        cleared = sem("cleared")
        attr_in = [sem(f"attr_in{j}") for j in range(SLOTS)]
        z_ready = sem("z_ready")
        acted = sem("acted")
        e_ready = sem("e_ready")
        node_in = sem("node_in")
        turned = sem("turned")
        xt_ready = sem("xt_ready")
        square_in = sem("square_in")
        squared = sem("squared")
        power_in = sem("power_in")
        power_rooted = sem("power_rooted")
        rows_in = sem("rows_in")
        rows_turned = sem("rows_turned")
        rows_copied = sem("rows_copied")
        hid_ps_ready = sem("hid_ps_ready")
        hid_z_ready = sem("hid_z_ready")
        hid_ready = sem("hid_ready")
        rows_projected = sem("rows_projected")
        projected = sem("projected")
        sum_in = sem("sum_in")
        summed = sem("summed")
        root_in = sem("root_in")
        rooted = sem("rooted")
        out_due = sem("out_due")
        late = sem("late")
        kept = sem("kept")
        adj_free = sem("adj_free")
        adj_zero = sem("adj_zero")
        low_in = sem("low_in")
        lows_seen = sem("lows_seen")
        low_ready = sem("low_ready")
        key_ready = sem("key_ready")
        counted = sem("counted")
        counts_ready = sem("counts_ready")
        added = sem("added")
        diagonal_ready = sem("diagonal_ready")
        loops_off = sem("loops_off")
        hidden_weights_ready = sem("hidden_weights_ready")
        rest_in = sem("rest_in")
        cast = sem("cast")
        parts_ready = sem("parts_ready")
        nb_ready = sem("nb_ready")
        nb_taken = sem("nb_taken")
        cat_ready = sem("cat_ready")
        cat_turned = sem("cat_turned")
        cat_copied = sem("cat_copied")
        cat_out = sem("cat_out")
        cat_taken = sem("cat_taken")
        dense_root_in = sem("dense_root_in")
        dense_rooted = sem("dense_rooted")
        written = sem("written")

        NQ = -(-NB // QUAD)
        dims = lambda g: (g * QUAD, min(QUAD, NB - g * QUAD))
        weights = [
            (Wp[0:D, 0, :], w_self1), (Wp[D:P, 0, :], w_neigh1), (Wp[0:D, 1, :], w_self2), (Wp[D:P, 1, :], w_neigh2),
            (Wp[0:D, 2, :], w_r), (Wp[D:P, 2, :], w_l),
            (Wp[0:D, 3:6, :], w0_t.rearrange("i a b -> a i b")), (Wp[D:P, 3:6, :], w1_t.rearrange("i a b -> a i b")),
            (Bp[:, 0, :], b_1.partition_broadcast(P)), (Bp[:, 1, :], b_2.partition_broadcast(P)),
            (Bp[:, 2, :], b_m.partition_broadcast(P)),
            (Bp[:, 3:6, :], b_c.partition_broadcast(P)),
            (gam[:, :], gamma.partition_broadcast(P)), (bet[:, :], beta.partition_broadcast(P)),
        ]
        late_weights = [
            (W1[0:D, :, 0, :], w1.rearrange("l a b -> a l b")), (W1[D:P, :, 1, :], w1.rearrange("l a b -> a l b")),
            (B1[:, :], b1_t), (LGT[0:D, :], ln_g_t), (LGT[D:P, :], ln_g_t), (LBT[0:D, :], ln_b_t), (LBT[D:P, :], ln_b_t),
            (W2[:, :, :], w2.rearrange("l a b -> a l b")), (B2[:, :, :], b2.partition_broadcast(P)),
            (WE1[:, :, 0, :], we1.rearrange("l a b -> a l b")), (WE1[:, :, 1, :], we1.rearrange("l a b -> a l b")),
            (BE1[0:D, :], be1_t), (BE1[D:P, :], be1_t),
            (WE2[0:D, :, 0, :], we2.rearrange("l a b -> a l b")), (WE2[0:D, :, 1, :], we2.rearrange("l a b -> a l b")),
            (WE2[D:P, :, 0, :], we2.rearrange("l a b -> a l b")), (WE2[D:P, :, 1, :], we2.rearrange("l a b -> a l b")),
            (BE2[:, :, :], be2.partition_broadcast(P)),
            (RW[:, :], res_w.partition_broadcast(P)), (DS[:, :], dot_scale.partition_broadcast(P)),
            (LG[:, :, :], ln_g.partition_broadcast(P)), (LB[:, :, :], ln_b.partition_broadcast(P)),
        ]
        nodes = [
            (X[:, 0:NB - 1, :], x[0:(NB - 1) * P, :].rearrange("(b p) d -> p b d", p=P)),
            (X[0:LAST_BLOCK, NB - 1, :], x[(NB - 1) * P:NODES, :]),
        ]
        edge_ends = [(dstr_i[:, :, :], dst_r.rearrange("p (g e) -> p g e", g=4)), (src_i[:, :], src_t),
                     (dst_i[:, :], dst_t)]
        ALL_IN = 16 * (len(weights) + len(nodes))

        block = ctx.enter_context(nc.Block())

        def wait(eng, semaphore, value):
            if not isinstance(value, int) or value > 0:
                eng.wait_ge(semaphore, value)

        def rounds(eng, body, peel, end=ROUNDS):
            if peel:
                body(0)
            with eng.Fori(1 if peel else 0, end) as i:
                body(i)

        def branch(eng, program):
            eng.wait_ge(flag_ready, 1)
            flag = eng.value_load(spread_i[0:1, 0:1], min_val=0, max_val=1)
            with eng.If(flag == 0):
                program(1)
            with eng.Else():
                program(PAIRS)

        @block.sync
        def _(sp):
            for to, of in edge_ends:
                sp.dma_start(to, of).then_inc(edges_in, 16)
            sp.wait_ge(consts, 1)
            for to, of in nodes:
                sp.dma_start(to, of).then_inc(loaded, 16)
            sp.wait_ge(dve, 6)
            sp.dma_start(tile_range[0].rearrange("(p g) -> p g", g=4), low_r).then_inc(range_out, 16)
            sp.dma_start(tile_range[1].rearrange("(p g) -> p g", g=4), high_r).then_inc(range_out, 16)
            sp.wait_ge(range_out, 32)
            sp.dma_start(first_node, tile_range[0].partition_broadcast(P)).then_inc(range_in, 16)
            sp.dma_start(last_node, tile_range[1].partition_broadcast(P)).then_inc(range_in, 16)
            for to, of in weights:
                sp.dma_start(to, of).then_inc(loaded, 16)

            def program(wide):
                edge_tables = tables.rearrange("p k t -> p (k t)")
                if wide == 1:
                    sp.dma_start(saved_tables, edge_tables).then_inc(kept, 16)
                    sp.wait_ge(kept, 16)
                    sp.wait_ge(adj_free, 1)
                    sp.dma_start(edge_tables, saved_tables).then_inc(late, 16)
                for to, of in late_weights:
                    sp.dma_start(to, of).then_inc(late, 16)
                if wide == 1:
                    sp.wait_ge(late, 16 * (len(late_weights) + 1))
                skipped = DENSE if wide == 1 else 0

                def load_round(s, i):
                    l = s - DENSE + skipped
                    for j in range(SLOTS):
                        wait(sp, gathered[j], i * (16 * QUAD) + 16 * QUAD * ROUNDS * s)
                        sp.dma_start(idx_slot[:, j * QUAD:(j + 1) * QUAD],
                                     idx_all[:, bass.ds((i * SLOTS + j) * QUAD, QUAD)]).then_inc(idx_in[j], 16)
                        if l >= 0:
                            wait(sp, z_ready, i * SLOTS + (QUADS * l + j - SLOTS + 1))
                            sp.dma_start(attr[:, j, :], attr_t[:, bass.ds((i * SLOTS + j) * (QUAD * P), QUAD * P)])\
                              .then_inc(attr_in[j], 16)

                for s in range(STAGES - skipped):
                    load_round(s, 0)
                    rows_of = table.rearrange("(p b) d -> p b d", b=NB)
                    if s - DENSE + skipped >= 0:
                        sp.wait_ge(early_due, s - DENSE + skipped + 1)
                    else:
                        sp.wait_ge(table_due, s + 1)
                    sp.dma_start(rows_of[:, 0:EARLY, :], H[:, 0:EARLY, :]).then_inc(table_in, 16)
                    sp.wait_ge(table_due, s + 1)
                    sp.dma_start(rows_of[:, EARLY:NB, :], H[:, EARLY:NB, :]).then_inc(table_in, 16)
                    with sp.Fori(1, ROUNDS) as i:
                        load_round(s, i)
                sp.wait_ge(out_due, 1)
                sp.dma_start(out[0:(NB - 1) * P, :].rearrange("(b p) d -> p b d", p=P),
                             X[:, 0:NB - 1, :]).then_inc(written, 16)
                sp.dma_start(out[(NB - 1) * P:NODES, :], X[0:LAST_BLOCK, NB - 1, :]).then_inc(written, 16)
                sp.wait_ge(written, 32)

            branch(sp, program)

        @block.gpsimd
        def _(pool):
            nc.gpsimd.memset(X[:, NB - 1, :], 0.0).then_inc(consts, 1)
            nc.gpsimd.iota(iota_lo[:, :], [[1, P]], base=0, channel_multiplier=0,
                           allow_small_or_imprecise_dtypes=True).then_inc(consts, 1)
            nc.gpsimd.iota(iota_hi[:, :], [[1, MASKS]], base=0, channel_multiplier=0,
                           allow_small_or_imprecise_dtypes=True).then_inc(consts, 1)
            nc.gpsimd.memset(ident[:, :], 0.0).then_inc(consts, 1)
            nc.gpsimd.memset(ones[:, :], 1.0).then_inc(consts, 1)
            nc.gpsimd.memset(real[:, :], 1.0).then_inc(consts, 1)
            nc.gpsimd.memset(eps5[:, :], 1e-5).then_inc(consts, 1)
            nc.gpsimd.memset(eps3[:, :], 1e-3).then_inc(consts, 1)
            nc.gpsimd.memset(zero[:, :], 0.0).then_inc(consts, 1)
            nc.gpsimd.memset(pick[:, :], 0.0).then_inc(consts, 1)
            nc.gpsimd.iota(iota_low[:, :], [[1, P]], base=0, channel_multiplier=0,
                           allow_small_or_imprecise_dtypes=True).then_inc(consts, 1)
            nc.gpsimd.iota(iota_key[:, :], [[1, KEYS]], base=0, channel_multiplier=0,
                           allow_small_or_imprecise_dtypes=True).then_inc(consts, 1)
            pool.wait_ge(consts, 12)
            nc.gpsimd.affine_select(out=ident[:, :], in_=ident[:, :], compare_op=ALU.not_equal, fill=1.0, base=0,
                                    pattern=[[-1, P]], channel_multiplier=1).then_inc(consts, 1)
            nc.gpsimd.affine_select(out=real[:, NB - 1:NB], in_=real[:, NB - 1:NB], compare_op=ALU.is_gt, fill=0.0,
                                    base=LAST_BLOCK, pattern=[[0, 1]], channel_multiplier=-1).then_inc(consts, 1)
            for r in range(3):
                pool.wait_ge(consts, 14 + r)
                nc.gpsimd.memset(pick[32 * r:32 * r + 1, :], 1.0).then_inc(consts, 1)

            def program(wide):
                if wide == 1:
                    ring = SLOTS * QUAD

                    def lows(i):
                        wait(pool, low_ready, i * (ring - ring // SHARE))
                        nc.gpsimd.tensor_copy(low_slot[:, :], src_low[:, bass.ds(i * ring, ring)]).then_inc(low_in, 1)
                        pool.wait_ge(low_in, i + 1)
                        for j in range(ring):
                            if j % SHARE == SHARE - 1:
                                continue
                            if j % OUTS == 0:
                                wait(pool, counted, i * ring + (j - ring + OUTS))
                                pool.sem_inc(lows_seen, 1)
                            nc.gpsimd.tensor_scalar(hot_low[:, j, :], iota_low[:, :],
                                                    low_slot[:, j:j + 1], None, ALU.is_equal)\
                              .then_inc(low_ready, 1)

                    rounds(pool, lows, True)
                    pool.wait_ge(diagonal_ready, 1)
                    pool.wait_ge(nb_ready, 3 * NQ)
                    for of, at in diagonals:
                        nc.gpsimd.tensor_tensor(at, at, of, ALU.add).then_inc(loops_off, 1)
                for s in range(STAGES - (DENSE if wide == 1 else 0)):
                    pool.wait_ge(table_in, 32 * (s + 1))

                    def gathers(i):
                        for j in range(SLOTS):
                            wait(pool, masked_ready, i * (SLOTS * wide) + wide * (QUADS * s + j - SLOTS + 1))
                            pool.wait_ge(idx_in[j], i * 16 + 16 * (ROUNDS * s + 1))
                            pool.sem_inc(idx_seen, 1)
                            for k in range(QUAD):
                                at = j * QUAD + k
                                nc.gpsimd.indirect_dma_start(
                                    out=rows[:, j, k, :], out_offset=None, in_=table,
                                    in_offset=bass.IndirectOffsetOnAxis(ap=idx_slot[:, at:at + 1], axis=0),
                                ).then_inc(gathered[j], 16)

                    rounds(pool, gathers, s == 0)

            branch(pool, program)

        @block.scalar
        def _(act):
            def program(wide):
                def copy_turned(k):
                    for g in range(NQ):
                        b0, n = dims(g)
                        act.wait_ge(turned, NQ * k + g + 1)
                        nc.scalar.activation(XT[:, b0 * P:(b0 + n) * P], z_ps[:, g % 2, 0:n * P], ACT.Copy)\
                          .then_inc(xt_ready, 1)

                roots = [0]

                def root(eps, cols, row):
                    act.wait_ge(root_in, roots[0] + 1)
                    roots[0] += 1
                    t = stat[:, row, 0:cols]
                    nc.scalar.activation(t, t, ACT.Sqrt, bias=eps[:, :]).then_inc(rooted, 1)

                if wide == 1:
                    dense_blocks()
                else:
                    root(zero_bias, NB, 6)
                    root(eps5, NB, 1)
                    copy_turned(0)
                    copy_turned(1)
                    root(eps5, NB, 1)
                    copy_turned(2)
                    root(eps5, NB, 1)
                    for i in range(3):
                        copy_turned(3 + i)
                        act.wait_ge(root_in, roots[0] + 1)
                        roots[0] += 1
                        nc.scalar.activation(part[:, 4:5], part[:, 4:5], ACT.Sqrt, bias=eps3[:, :]).then_inc(rooted, 1)

                def copy_rows(l, k):
                    _, n = dims(2 * k)
                    high = P if n > 1 else D
                    to, of = XT[0:high, k * BANK:k * BANK + n * P], z_ps[0:high, k % 2, 0:n * P]
                    act.wait_ge(rows_turned, (UNITS + 1) // 2 * l + k + 1)
                    if l == 0:
                        nc.scalar.activation(to, of, ACT.Copy).then_inc(rows_copied, 1)
                    else:
                        nc.scalar.activation(to, of, ACT.Identity, bias=LBT[0:high, l - 1:l],
                                             scale=LGT[0:high, l - 1:l]).then_inc(rows_copied, 1)

                def bias_hidden(l, u):
                    _, n = dims(u)
                    act.wait_ge(hid_ps_ready, UNITS * l + u + 1)
                    wait(act, hid_ready, UNITS * l + u - 1)
                    nc.scalar.activation(hid_z[:, u % 2, 0:n * P], e_ps[:, u % 2, 0:n * P], ACT.Identity,
                                         bias=B1[:, l:l + 1]).then_inc(hid_z_ready, 1)

                def norm_rows(k):
                    def square(c):
                        b0, b1 = CHUNKS[c]
                        act.wait_ge(square_in, len(CHUNKS) * k + c + 1)
                        nc.scalar.activation(cat[:, b0:b1, 0:D], cat[:, b0:b1, D:2 * D], ACT.Square).then_inc(squared, 1)

                    def root_of(c):
                        b0, b1 = CHUNKS[c]
                        act.wait_ge(power_in, len(CHUNKS) * k + c + 1)
                        nc.scalar.activation(stat[:, 1, b0:b1], stat[:, 1, b0:b1], ACT.Sqrt, bias=eps5[:, :],
                                             scale=1.0 / D).then_inc(power_rooted, 1)

                    square(0)
                    root_of(0)
                    square(1)
                    if k < LAYERS:
                        copy_rows(k, 0)
                    root_of(1)
                    square(2)
                    if 0 < k < LAYERS:
                        bias_hidden(k, 0)
                    root_of(2)
                    if k == 0:
                        bias_hidden(k, 0)

                for l in range(LAYERS):
                    norm_rows(l)
                    for u in range(1, UNITS):
                        if u % 2 == 0:
                            copy_rows(l, u // 2)
                        bias_hidden(l, u)

                    def activate(i):
                        for j in range(SLOTS):
                            act.wait_ge(z_ready, i * SLOTS + (QUADS * l + j + 1))
                            wait(act, e_ready, i * SLOTS + (QUADS * l + j - 1))
                            nc.scalar.activation(act_e[:, j % 2, :], z_ps[:, j % 2, :], ACT.Relu,
                                                 bias=BE1[:, l:l + 1]).then_inc(acted, 1)

                    rounds(act, activate, l == 0)
                norm_rows(LAYERS)

            zero_bias = zero

            def zero_block(c):
                nc.scalar.activation(adj[:, c, :].bitcast(f32), zero[:, 0:1].to_broadcast([P, ACOLS // 2]), ACT.Copy)\
                  .then_inc(adj_zero, 1)

            act.wait_ge(consts, 12)
            for c in early_zero:
                zero_block(c)

            def dense_blocks():
                for c in late_zero[ZEROED:]:
                    if c * ACOLS < 10 * TILES:
                        act.wait_ge(kept, 16)
                    zero_block(c)

                def copy_counts(i):
                    for j in range(SLOTS):
                        act.wait_ge(counted, i * SLOTS + (j + 1))
                        wait(act, added, i * SLOTS + (j - SLOTS + 1))
                        nc.scalar.activation(counts[:, j, :], agg_ps[:, j * BANK:j * BANK + KEYS], ACT.Copy)\
                          .then_inc(counts_ready, 1)

                rounds(act, copy_counts, True, TILES // SLOTS)
                taken_roots = [0]

                def root(t, eps):
                    taken_roots[0] += 1
                    act.wait_ge(dense_root_in, taken_roots[0])
                    nc.scalar.activation(t, t, ACT.Sqrt, bias=eps[:, :]).then_inc(dense_rooted, 1)

                def copy_cat(s, g):
                    _, n = dims(g)
                    act.wait_ge(cat_turned, NQ * s + g + 1)
                    wait(act, cat_out, NQ * s + max(0, g - 1))
                    nc.scalar.activation(turned_rows[:, g % 2, 0:n * P], z_ps[:, g % 2, 0:n * P], ACT.Copy)\
                          .then_inc(cat_copied, 1)

                splits = [0]

                def split(scaled):
                    first = splits[0] * 6
                    splits[0] += 1
                    for k in range(3):
                        for h, b in enumerate(HALVES):
                            act.wait_ge(rest_in, first + 2 * k + h + 1)
                            of = cat[:, b, D:2 * D] if scaled or k else cat[:, b, 0:D]
                            nc.scalar.activation(parts[:, b, k * D:(k + 1) * D], of, ACT.Copy)\
                              .then_inc(parts_ready if k == 2 else cast, 1)

                root(stat[:, 1, :], eps5)
                split(False)
                for s in range(DENSE):
                    for it in range(1, NQ + 2):
                        if s == 2 and it == COUNTED:
                            root(stat[:, 6, :], zero)
                        if it <= NQ:
                            copy_cat(s, it - 1)
                        if s in (1, 2) and it >= 2 and it != NQ:
                            root(stat[:, 1, 0:dims(it - 2)[1] + (QUAD if it > NQ else 0)], eps5)
                    if s >= 3:
                        root(part[:, 4:5], eps3)
                    if s < DENSE - 1:
                        split(s >= 2)

            branch(act, program)

        @block.tensor
        def _(pe):
            def program(wide):
                def gathered_degrees():
                    with pe.Fori(0, QUADS // 2) as i:
                        for j in range(2):
                            pe.wait_ge(hist_hot, i * 2 + (j + 1))
                            for k in range(QUAD):
                                nc.tensor.matmul(z_ps[:, 0, 0:MASKS], onehot[:, j, k, :], hot_hi[:, j, 0, k, :],
                                                 start=False, stop=True, skip_group_check=True)
                                last = nc.tensor.matmul(z_ps[:, 1, 0:MASKS], onehot_src[:, j, k, :],
                                                        hot_hi[:, j, 1, k, :],
                                                        start=False, stop=True, skip_group_check=True)
                            last.then_inc(hist_done, 1)

                def count_edges(i):
                    ring = SLOTS * QUAD
                    for j in range(ring):
                        if j % SHARE == SHARE - 1:
                            pe.wait_ge(key_ready, i * ring + (j + 1))
                        else:
                            pe.wait_ge(low_ready, i * (ring - ring // SHARE) + (j - j // SHARE + 1))
                        pe.wait_ge(key_ready, i * ring + (j + 1))
                        wait(pe, counts_ready, i * ring + (j - SLOTS + 1))
                        nc.tensor.matmul(agg_ps[:, j % SLOTS * BANK:j % SLOTS * BANK + KEYS], hot_low[:, j, :],
                                         hot_key[:, j % 4, :], start=True, stop=True).then_inc(counted, 1)

                def dense_stage(s):
                    for g in range(NQ + 2):
                        if g < NQ:
                            b0, n = dims(g)
                            wait(pe, nb_taken, s * NQ + max(0, g - 1))
                            for b in range(n):
                                lo = (b0 + b) * P
                                m = min(P, ACOLS - lo)
                                for c in range(NB):
                                    if g == 0 and b == 0 and c in (0, HALF):
                                        pe.wait_ge(parts_ready, s * 2 + (1 if c == 0 else 2))
                                    at = g % 2 * 2 * BANK + b * (BANK // 2)
                                    last = nc.tensor.matmul(agg_ps[0:m, at:at + PW], adj[:, c, lo:lo + m],
                                                            parts[:, c, :], start=c == 0, stop=c == NB - 1)
                            last.then_inc(nb_ready, 1)
                        if 1 <= g <= NQ:
                            b0, n = dims(g - 1)
                            pe.wait_ge(cat_ready, s * NQ + g)
                            wait(pe, cat_copied, s * NQ + max(0, g - 2))
                            for b in range(n):
                                last = nc.tensor.transpose(z_ps[:, (g - 1) % 2, b * P:(b + 1) * P], cat[:, b0 + b, :],
                                                           ident[:, :])
                            last.then_inc(cat_turned, 1)
                        if g >= 2:
                            _, n = dims(g - 2)
                            pe.wait_ge(cat_copied, s * NQ + (g - 1))
                            wait(pe, cat_taken, s * NQ + max(0, g - 3))
                            for b in range(n):
                                last = nc.tensor.matmul(e_ps[:, g % 2, b * D:(b + 1) * D],
                                                        turned_rows[:, g % 2, b * P:(b + 1) * P], weight_of(s),
                                                        start=True, stop=True)
                            last.then_inc(cat_out, 1)

                def weight_of(s):
                    return Wp[:, bass.ds(s, 1), :].rearrange("p a d -> p (a d)")

                def mean_sums(first):
                    for r in range(2):
                        pe.wait_ge(sum_in, first + (r + 1))
                        nc.tensor.matmul(z_ps[:, 0, 0:1], ones[:, :], part[:, r:r + 1], start=True, stop=True)\
                          .then_inc(summed, 1)

                def turn(k, rows_of, width):
                    pe.wait_ge(node_in, k + 1)
                    for g in range(NQ):
                        b0, n = dims(g)
                        if g >= 2:
                            pe.wait_ge(xt_ready, NQ * k + g - 1)
                        for b in range(n):
                            last = nc.tensor.transpose(z_ps[0:width, g % 2, b * P:(b + 1) * P],
                                                       rows_of(b0 + b), ident[:, :])
                        last.then_inc(turned, 1)

                def scatter(s, i, j, at, source, ready, before):
                    pe.wait_ge(hot_ready, i * SLOTS + (QUADS * s + j + 1))
                    if wide == 1:
                        pe.wait_ge(ready, i * SLOTS + (before + j + 1))
                        for k in range(QUAD):
                            last = nc.tensor.matmul(agg_ps[:, bass.ds(at[j * QUAD + k], 2 * D)],
                                                    onehot[:, j % 2, k, :], source[:, j % 2, k, :, :],
                                                    start=False, stop=True, skip_group_check=True)
                        last.then_inc(scattered, 1)
                    else:
                        for w in range(wide):
                            pe.wait_ge(ready, i * (SLOTS * wide) + (wide * (before + j) + w + 1))
                            for k in range(QUAD):
                                last = nc.tensor.matmul(agg_ps[:, w * 2 * D:(w + 1) * 2 * D],
                                                        onehot[:, j % 2, k, :],
                                                        source[:, (j * wide + w) % 2, k, :, :],
                                                        start=False, stop=True, skip_group_check=True)
                            last.then_inc(scattered, 1)

                def windows(i):
                    if wide > 1:
                        return None
                    _, at = nc.values_load_multi_w_load_instructions(
                        window_at[0:1, bass.ds(i * SLOTS * QUAD, SLOTS * QUAD)], engines=[pe.engine],
                        min_val=0, max_val=4 * BANK - 2 * D, bass_reorder=False,
                        skip_runtime_bounds_check_because="it comes from a block, and no block lies further")
                    return at

                def project(k, lhs, weight, ready):
                    for g in range(NQ):
                        b0, n = dims(g)
                        ready(g)
                        for b in range(n):
                            last = nc.tensor.matmul(agg_ps[:, (b0 + b) * D:(b0 + b + 1) * D],
                                                    lhs(g, b), weight, start=False, stop=True, skip_group_check=True)
                    last.then_inc(projected, 1)

                def gathered_stages():
                    for s in range(DENSE):
                        pe.wait_ge(cleared, 2 * s + 1)
                        with pe.Fori(0, ROUNDS) as i:
                            at = windows(i)
                            for j in range(SLOTS):
                                scatter(s, i, j, at, masked, masked_ready, QUADS * s)
                        turn(s, lambda b: cat[:, b, :], P)
                        pe.wait_ge(cleared, 2 * s + 2)
                        project(s, lambda g, b: XT[:, (g * QUAD + b) * P:(g * QUAD + b + 1) * P], Wp[:, s, :],
                                lambda g: pe.wait_ge(xt_ready, NQ * s + g + 1))
                        if s >= 3:
                            mean_sums(2 * (s - 3))

                if wide == 1:
                    rounds(pe, count_edges, True)
                    dense_stage(0)
                    with pe.Fori(1, 3) as s:
                        dense_stage(s)
                    pe.wait_ge(loops_off, 2)
                    with pe.Fori(3, DENSE) as s:
                        dense_stage(s)
                        mean_sums(s * 2 - 6)
                else:
                    gathered_degrees()
                    gathered_stages()
                s0 = 0 if wide == 1 else DENSE
                for l in range(LAYERS):
                    s = s0 + l
                    def turn_rows(k):
                        wait(pe, rows_copied, (UNITS + 1) // 2 * l + k - 1)
                        pe.wait_ge(rows_in, len(CHUNKS) * l + min(k + 1, len(CHUNKS)))
                        for b in range(8 * k, min(8 * k + 8, NB), 2):
                            width = min(2, NB - b) * D
                            last = nc.tensor.transpose(z_ps[0:width, k % 2, (b // 2 - 4 * k) * P:(b // 2 - 4 * k + 1) * P],
                                                       rows_buf[:, b * D:b * D + width], ident[:, :])
                        last.then_inc(rows_turned, 1)

                    def hidden(u):
                        _, n = dims(u)
                        k, high = u // 2, (P if n > 1 else D)
                        pe.wait_ge(rows_copied, (UNITS + 1) // 2 * l + k + 1)
                        if u >= 2:
                            pe.wait_ge(hid_z_ready, UNITS * l + u - 1)
                        nc.tensor.matmul(e_ps[:, u % 2, 0:n * P], W1[0:high, l, u % 2, :],
                                         XT[0:high, k * BANK:k * BANK + n * P], start=True, stop=True)\
                          .then_inc(hid_ps_ready, 1)

                    def rows_out(u):
                        _, n = dims(u)
                        pe.wait_ge(hid_ready, UNITS * l + u + 1)
                        for k in range(n):
                            b = 8 * (u // 2) + u % 2 + 2 * k
                            last = nc.tensor.matmul(agg_ps[:, b * D:(b + 1) * D], hid[:, u % QUAD, k * P:(k + 1) * P],
                                                    W2[:, l, :], start=True, stop=True)
                        if u % 2 == 1 or u == UNITS - 1:
                            last.then_inc(rows_projected, 1)

                    turn_rows(0)
                    if l == 0:
                        pe.wait_ge(hidden_weights_ready, 1)
                    for u in range(UNITS):
                        hidden(u)
                        if u % 2 == 0 and u + 2 < UNITS + 1:
                            turn_rows(u // 2 + 1)
                        if u >= 2:
                            rows_out(u - 2)
                    rows_out(UNITS - 2)
                    rows_out(UNITS - 1)

                    base = QUADS * l
                    pe.wait_ge(cleared, s0 * 2 + l + 1)

                    def first_product(i, j):
                        i, j = i + j // SLOTS, j % SLOTS
                        pe.wait_ge(attr_in[j], 16 * (ROUNDS * l + i + 1))
                        wait(pe, acted, i * SLOTS + (base + j - 1))
                        nc.tensor.matmul(z_ps[:, j % 2, :], WE1[:, l, :, :], attr[:, j, :], start=True, stop=True)\
                          .then_inc(z_ready, 1)

                    def second_product(i, j):
                        i, j = i + j // SLOTS, j % SLOTS
                        pe.wait_ge(acted, i * SLOTS + (base + j + 1))
                        wait(pe, msg_ready, i * (SLOTS * wide) + wide * (base + j - 1))
                        nc.tensor.matmul(e_ps[:, j % 2, :], pick[:, :], bc(BE2s[:, l, :], 1, 2 * QUAD),
                                         start=True, stop=False, skip_group_check=True)
                        for k in range(QUAD):
                            last = nc.tensor.matmul(e_ps[:, j % 2, k * 2 * D:(k + 1) * 2 * D],
                                                    act_e[:, j % 2, k * P:(k + 1) * P], WE2[:, l, :, :],
                                                    start=False, stop=True, skip_group_check=True)
                        last.then_inc(e_ready, 1)

                    first_product(0, 0)
                    first_product(0, 1)
                    second_product(0, 0)

                    def products(i):
                        at = windows(i)
                        for j in range(SLOTS):
                            first_product(i, j + 2)
                            second_product(i, j + 1)
                            scatter(s, i, j, at, msg, msg_ready, base)

                    rounds(pe, products, l == 0, ROUNDS - 1)
                    at = windows(ROUNDS - 1)
                    for j in range(SLOTS):
                        if j + 2 < SLOTS:
                            first_product(ROUNDS - 1, j + 2)
                        if j + 1 < SLOTS:
                            second_product(ROUNDS - 1, j + 1)
                        scatter(s, ROUNDS - 1, j, at, msg, msg_ready, base)

            branch(pe, program)

        @block.vector
        def _(v):
            steps = [0]

            def link(ins):
                steps[0] += 1
                ins.then_inc(dve, 1)
                v.wait_ge(dve, steps[0])

            V = nc.vector
            link(V.memset(agg_ps[:, :], 0.0))
            link(V.memset(z_ps[:, :, :], 0.0))
            link(V.memset(part[:, :], 0.0))
            v.wait_ge(edges_in, 16 * len(edge_ends))
            link(V.tensor_copy(dstr_f[:, :, :], dstr_i[:, :, :]))
            link(V.tensor_reduce(low_r[:, :], dstr_f[:, :, :], AX.X, ALU.min))
            link(V.tensor_reduce(high_r[:, :], dstr_f[:, :, :], AX.X, ALU.max))
            for i_t, f_t, lo, hi in ((src_i, src_f, src_lo, src_hi), (dst_i, dst_f, dst_lo, dst_hi)):
                link(V.tensor_copy(f_t[:, :], i_t[:, :]))
                link(V.tensor_scalar(tmp_i[:, :], i_t[:, :], 7, None, ALU.arith_shift_right))
                link(V.tensor_copy(hi[:, :], tmp_i[:, :]))
                link(V.scalar_tensor_tensor(lo[:, :], hi[:, :], -float(P), f_t[:, :], ALU.mult, ALU.add))
            link(V.tensor_tensor(not_loop[:, :], src_f[:, :], dst_f[:, :], ALU.not_equal))
            link(V.tensor_scalar(cmp[:, :], src_hi[:, :], 1.0, None, ALU.add))
            link(V.tensor_tensor(cmp[:, :], cmp[:, :], not_loop[:, :], ALU.mult))
            link(V.tensor_scalar(out_hi[:, :], cmp[:, :], -1.0, None, ALU.add))
            link(V.tensor_copy(src_low[:, :], src_lo[:, :]))
            link(V.scalar_tensor_tensor(cmp[:, :], src_lo[:, :], float(NB), src_hi[:, :], ALU.mult, ALU.add))
            link(V.tensor_copy(idx_all[:, :], cmp[:, :]))
            v.wait_ge(range_in, 32)
            link(V.tensor_copy(first_i[:, :], first_node[:, :]))
            link(V.tensor_scalar(tmp_i[:, :], first_i[:, :], 7, None, ALU.arith_shift_right))
            link(V.tensor_copy(first_block[:, :], tmp_i[:, :]))
            link(V.scalar_tensor_tensor(key[:, :], src_hi[:, :], float(SPAN), dst_f[:, :], ALU.mult, ALU.add))
            link(V.tensor_tensor(key[:, :], key[:, :], first_node[:, :], ALU.subtract))
            link(V.tensor_tensor(near[:, :, 0], dst_hi[:, :], first_block[:, :], ALU.is_equal))
            link(V.tensor_scalar(cmp[:, :], first_block[:, :], 1.0, None, ALU.add))
            link(V.tensor_tensor(near[:, :, 1], dst_hi[:, :], cmp[:, :], ALU.is_equal))
            link(V.tensor_scalar(bank_of[:, :], first_block[:, :], 7.0, None, ALU.is_ge))
            for edge in (14.0, 21.0):
                link(V.tensor_scalar(cmp[:, :], first_block[:, :], edge, None, ALU.is_ge))
                link(V.tensor_tensor(bank_of[:, :], bank_of[:, :], cmp[:, :], ALU.add))
            link(V.tensor_tensor(window_f[:, :], first_block[:, :], bank_of[:, :], ALU.add))
            link(V.tensor_scalar(window_f[:, :], window_f[:, :], float(D), None, ALU.mult))
            link(V.tensor_copy(window_at[:, :], window_f[:, :]))
            link(V.tensor_tensor(cmp[:, :], last_node[:, :], first_node[:, :], ALU.subtract))
            link(V.tensor_scalar(window_f[:, :], cmp[:, :], float(SPAN), None, ALU.is_ge))
            link(V.tensor_reduce(spread[:, 0:1], window_f[:, :], AX.X, ALU.max))
            link(V.tensor_scalar(window_f[:, :], cmp[:, :], 1.0, None, ALU.is_lt))
            link(V.tensor_reduce(spread[:, 1:2], window_f[:, :], AX.X, ALU.max))
            link(V.tensor_tensor(window_f[:, 0:TILES - 1], last_node[:, 0:TILES - 1], first_node[:, 1:TILES], ALU.is_gt))
            link(V.tensor_reduce(spread[:, 2:3], window_f[:, 0:TILES - 1], AX.X, ALU.max))
            link(V.tensor_reduce(spread[:, 3:4], spread[:, 0:3], AX.X, ALU.max))
            v.wait_ge(consts, 17)
            v.wait_ge(adj_zero, len(early_zero))
            V.tensor_copy(spread_i[:, :], spread[:, 3:4]).then_inc(flag_ready, 1)

            began = steps[0]

            def program(wide):
                steps[0] = began
                roots = [0]
                dense = [wide == 1]

                def root(ins):
                    roots[0] += 1
                    ins.then_inc(dense_root_in if dense[0] else root_in, 1)
                    v.wait_ge(dense_rooted if dense[0] else rooted, roots[0])

                given = {}

                def give(ins, semaphore):
                    given[semaphore.name] = given.get(semaphore.name, 0) + 1
                    ins.then_inc(semaphore, 1)
                    v.wait_ge(semaphore, given[semaphore.name])

                def hidden_weights():
                    v.wait_ge(late, 16 * (len(late_weights) + (1 if wide == 1 else 0)))
                    link(V.memset(W1[0:D, :, 1, :], 0.0))
                    link(V.memset(W1[D:P, :, 0, :], 0.0))
                    v.sem_inc(hidden_weights_ready, 1)

                def edge_weights():
                    link(V.tensor_scalar(WE1[:, :, 1, :], WE1[:, :, 1, :], -1.0, None, ALU.mult))
                    link(V.tensor_scalar(BE1[D:P, :], BE1[D:P, :], -1.0, None, ALU.mult))
                    link(V.tensor_scalar(WE2[D:P, :, :, :], WE2[D:P, :, :, :], -0.1, None, ALU.mult))
                    link(V.memset(BE2s[:, :, :], 0.0))
                    link(V.tensor_copy(BE2p[:, 0, :, :], BE2[:, :, :]))
                    link(V.tensor_tensor(BE2r[:, :, :], BE2[:, :, :], BE2p[:, 0, :, :], ALU.subtract))
                    link(V.tensor_copy(BE2p[:, 1, :, :], BE2r[:, :, :]))
                    link(V.tensor_tensor(BE2r[:, :, :], BE2r[:, :, :], BE2p[:, 1, :, :], ALU.subtract))
                    link(V.tensor_copy(BE2p[:, 2, :, :], BE2r[:, :, :]))
                    for r in range(3):
                        link(V.tensor_copy(BE2s[32 * r:32 * r + 1, :, :], BE2p[32 * r:32 * r + 1, r, :, :]))
                    link(V.tensor_tensor(RW[:, :], RW[:, :], DS[:, :], ALU.mult))

                def out_degrees(counted_out):
                    link(V.tensor_scalar(stat[:, 7, :], counted_out, 0.0, None, ALU.is_gt))
                    root(V.tensor_scalar(stat[:, 6, :], counted_out, 1.0, None, ALU.max))
                    link(V.reciprocal(stat[:, 6, :], stat[:, 6, :]))
                    link(V.tensor_tensor(dinv[:, :], stat[:, 6, :], stat[:, 7, :], ALU.mult))
                    link(V.tensor_scalar(ndinv[:, :], dinv[:, :], -1.0, None, ALU.mult))

                def gathered_degrees():
                    for w in range(2 * wide):
                        link(V.tensor_scalar(masks[:, :, w], dst_hi[:, :], float(w), None, ALU.is_equal))

                    def hist(i):
                        for j in range(2):
                            wait(v, hist_done, i * 2 + (j - 1))
                            t = bass.ds((i * 2 + j) * QUAD, QUAD)
                            for hot, lo in ((onehot, dst_lo), (onehot_src, src_lo)):
                                V.tensor_tensor(hot[:, j, :, :], bc(iota_lo[:, :], 1, QUAD), bc(lo[:, t], 2, P),
                                                ALU.is_equal)
                            V.tensor_tensor(hot_hi[:, j, 0, :, :], bc(iota_hi[:, :], 1, QUAD), bc(dst_hi[:, t], 2, MASKS),
                                            ALU.is_equal)
                            V.tensor_tensor(hot_hi[:, j, 1, :, :], bc(iota_hi[:, :], 1, QUAD), bc(out_hi[:, t], 2, MASKS),
                                            ALU.is_equal).then_inc(hist_hot, 1)

                    rounds(v, hist, True, QUADS // 2)
                    v.wait_ge(hist_done, QUADS)
                    link(V.tensor_scalar(stat[:, 0, :], z_ps[:, 0, 0:NB], 1.0, None, ALU.max))
                    link(V.reciprocal(rdeg[:, :], stat[:, 0, :]))
                    out_degrees(z_ps[:, 1, 0:NB])

                def count_edges():
                    ring, ahead = SLOTS * QUAD, 3
                    for c in late_zero[:ZEROED]:
                        if c * ACOLS < 10 * TILES:
                            v.wait_ge(kept, 16)
                        V.memset(adj[:, c, :].bitcast(f32), 0.0).then_inc(adj_zero, 1)

                    def hot_keys(i, j):
                        if j % SHARE == SHARE - 1:
                            V.tensor_scalar(hot_low[:, j % ring, :], iota_low[:, :], src_low[:, bass.ds(i * ring + j, 1)],
                                            None, ALU.is_equal)
                        V.tensor_scalar(hot_key[:, j % 4, :], iota_key[:, :], key[:, bass.ds(i * ring + j, 1)], None,
                                        ALU.is_equal).then_inc(key_ready, 1)

                    for j in range(ahead):
                        hot_keys(0, j)
                    v.wait_ge(adj_zero, NB)

                    def tiles(i, last=False):
                        _, first = nc.values_load_multi_w_load_instructions(
                            first_i[0:1, bass.ds(i * ring, ring)], engines=[v.engine], min_val=0, max_val=NODES - 1,
                            bass_reorder=False,
                            skip_runtime_bounds_check_because="the narrow program's tiles begin at real nodes")
                        for j in range(ring):
                            if not last or j + ahead < ring:
                                wait(v, counted, i * ring + (j + ahead - 3))
                                hot_keys(i, j + ahead)
                            if j % 2 == 0:
                                v.wait_ge(counts_ready, i * ring + (j + 2))
                            wait(v, added, i * ring + j)
                            to = adj[:, :, bass.ds(first[j], SPAN)]
                            V.tensor_tensor(to, to, counts[:, j % SLOTS, :].rearrange("p (c n) -> p c n", n=SPAN),
                                            ALU.add).then_inc(added, 1)

                    rounds(v, tiles, True, ROUNDS - 1)
                    tiles(ROUNDS - 1, last=True)
                    v.wait_ge(added, TILES)
                    v.wait_ge(loaded, ALL_IN)

                def per_node(t):
                    return bc(t, 2, D)

                def norm(to, of, centred, relu, last=None):
                    n = to.shape[1]
                    mean, power = stat[:, 0, 0:n], stat[:, 1, 0:n]
                    link(V.tensor_reduce(mean, of, AX.X, ALU.add))
                    link(V.tensor_scalar(mean, mean, 1.0 / D, None, ALU.mult))
                    link(V.tensor_tensor(centred, of, per_node(mean), ALU.subtract))
                    link(V.tensor_tensor(to, centred, centred, ALU.mult))
                    link(V.tensor_reduce(power, to, AX.X, ALU.add))
                    root(V.tensor_scalar(power, power, 1.0 / D, None, ALU.mult))
                    link(V.reciprocal(power, power))
                    if relu:
                        link(V.tensor_scalar(centred, centred, 0.0, None, ALU.max))
                    ins = V.tensor_tensor(to, centred, per_node(power), ALU.mult)
                    give(ins, last) if last is not None else link(ins)

                own, neighbours = cat[:, :, 0:D], cat[:, :, D:2 * D]

                splits = [0]

                def split(scaled):
                    first = splits[0] * 6
                    splits[0] += 1
                    for b in HALVES:
                        if scaled:
                            V.tensor_tensor(neighbours[:, b, :], own[:, b, :], per_node(dinv[:, b]), ALU.mult)\
                             .then_inc(rest_in, 1)
                        else:
                            v.sem_inc(rest_in, 1)
                    for k in range(2):
                        for h, b in enumerate(HALVES):
                            of = neighbours if scaled or k else own
                            v.wait_ge(rest_in, first + 2 * k + h + 1)
                            v.wait_ge(cast, (first // 3 * 2) + 2 * k + h + 1)
                            V.tensor_tensor(neighbours[:, b, :], of[:, b, :], parts[:, b, k * D:(k + 1) * D],
                                            ALU.subtract).then_inc(rest_in, 1)

                def dense_stages():
                    link(V.memset(parts[:, :, 3 * D:PW], 1.0))
                    norm(own, X[:, :, :], neighbours, True)
                    split(False)
                    for at, of in diagonals:
                        link(V.scalar_tensor_tensor(at, of, -1.0, bc(ident[:, :], 1, NB)[:, 0:at.shape[1], 0:at.shape[2]],
                                                    ALU.mult, ALU.mult))
                    link(V.tensor_reduce(loops[:, 0:NB - 1], loops_diagonal[:, 0:NB - 1, :], AX.X, ALU.add))
                    link(V.tensor_reduce(loops[:, NB - 1:NB], loops_diagonal[:, NB - 1:NB, 0:ACOLS - (NB - 1) * P],
                                         AX.X, ALU.add))
                    to_count = list(range(NB))
                    for s in range(DENSE):
                        for it in range(NQ + 2):
                            if s == 2 and it == COUNTED:
                                link(V.tensor_tensor(outs[:, :], outs[:, :], loops[:, :], ALU.add))
                                out_degrees(outs[:, :])
                                v.sem_inc(diagonal_ready, 1)
                            if it < NQ:
                                neighbours_sum(s, it)
                            if it == NQ and s == DENSE - 1:
                                v.wait_ge(nb_ready, NQ * DENSE)
                                v.sem_inc(adj_free, 1)
                            if it >= 2:
                                after_projection(s, it - 2)
                            for _ in range(0 if s > 2 or it >= COUNTED + (s == 0) else 2 if s == 0 and it < COUNTED else 1):
                                if to_count:
                                    c = to_count.pop()
                                    link(V.tensor_reduce(outs[:, c:c + 1], adj[:, c, :], AX.X, ALU.add))
                        if s >= 3:
                            norm_all(s - 3, own, neighbours)
                            if s == 4:
                                link(V.tensor_scalar(own, own, 0.0, None, ALU.max))
                        if s < DENSE - 1:
                            split(s >= 2)
                        if s == 3:
                            link(V.tensor_copy(X1[:, :, :], own))

                def neighbours_sum(s, g):
                    b0, n = dims(g)
                    b = slice(b0, b0 + n)
                    at = g % 2 * 2 * BANK
                    sums = agg_ps[:, at:at + n * (BANK // 2)].rearrange("p (b w) -> p b w", w=BANK // 2)
                    v.wait_ge(nb_ready, NQ * s + g + 1)
                    if s == 0:
                        link(V.tensor_scalar(stat[:, 0, b], sums[:, :, 3 * D], 1.0, None, ALU.max))
                        link(V.reciprocal(rdeg[:, b], stat[:, 0, b]))
                    give(V.tensor_reduce(neighbours[:, b, :],
                                         sums[:, :, 0:3 * D].rearrange("p b (k d) -> p b d k", k=3), AX.X, ALU.add),
                         nb_taken)
                    give(V.tensor_tensor(neighbours[:, b, :], neighbours[:, b, :],
                                         per_node((rdeg if s < 3 else ndinv)[:, b]), ALU.mult), cat_ready)

                def after_projection(s, g):
                    b0, n = dims(g)
                    b = slice(b0, b0 + n)
                    h, scratch = own[:, b, :], neighbours[:, b, :]
                    v.wait_ge(cat_out, NQ * s + g + 1)
                    give(V.tensor_tensor(h if s in (0, 3, 4, 5) else scratch,
                                         e_ps[:, g % 2, 0:n * D].rearrange("p (b d) -> p b d", d=D),
                                         bc(Bp[:, s, :], 1, n), ALU.add), cat_taken)
                    if s in (1, 2):
                        if s == 2:
                            link(V.tensor_scalar(scratch, scratch, 0.0, None, ALU.max))
                        link(V.tensor_tensor(X[:, b, :], X[:, b, :], scratch, ALU.add))
                        if g != NQ - 2:
                            b = slice(b0 if g < NQ - 1 else b0 - QUAD, b0 + n)
                            norm(own[:, b, :], X[:, b, :], neighbours[:, b, :], True)
                    if s >= 3:
                        if g == NQ - 1:
                            link(V.tensor_tensor(own[:, NB - 1:NB, :], own[:, NB - 1:NB, :],
                                                 per_node(real[:, NB - 1:NB]), ALU.mult))
                        link(V.tensor_reduce(stat[:, 2, b], h, AX.X, ALU.add))

                def norm_all(i, to, scratch):
                    give(V.tensor_reduce(part[:, 0:1], stat[:, 2, :], AX.X, ALU.add), sum_in)
                    v.wait_ge(summed, 2 * i + 1)
                    link(V.tensor_scalar(part[:, 2:3], z_ps[:, 0, 0:1], 1.0 / (NODES * D), None, ALU.mult))
                    link(V.tensor_scalar(to, to, part[:, 2:3], None, ALU.subtract))
                    link(V.tensor_tensor(to[:, NB - 1:NB, :], to[:, NB - 1:NB, :], per_node(real[:, NB - 1:NB]), ALU.mult))
                    link(V.tensor_tensor(scratch, to, to, ALU.mult))
                    link(V.tensor_reduce(stat[:, 2, :], scratch, AX.X, ALU.add))
                    give(V.tensor_reduce(part[:, 1:2], stat[:, 2, :], AX.X, ALU.add), sum_in)
                    v.wait_ge(summed, 2 * i + 2)
                    root(V.tensor_scalar(part[:, 4:5], z_ps[:, 0, 0:1], 1.0 / (NODES * D), None, ALU.mult))
                    link(V.reciprocal(part[:, 3:4], part[:, 4:5]))
                    link(V.tensor_tensor(part[:, 3:4], part[:, 3:4], gam[:, i:i + 1], ALU.mult))
                    link(V.tensor_scalar(to, to, part[:, 3:4], bet[:, i:i + 1], ALU.mult, ALU.add))

                def agg_view():
                    if wide > 1:
                        return [(0, NB, agg_ps[:, 0:NB * D].rearrange("p (b d) -> p b d", d=D))]
                    got = []
                    for k in range(4):
                        n = min(7, NB - 7 * k)
                        got.append((7 * k, n, agg_ps[:, k * BANK:k * BANK + n * D].rearrange("p (b d) -> p b d", d=D)))
                    return got

                def edges(s, l):

                    def quads(i):
                        for j in range(SLOTS):
                            t = bass.ds((i * SLOTS + j) * QUAD, QUAD)
                            wait(v, scattered, i * (SLOTS * wide) + wide * (QUADS * s + j - 1))
                            V.tensor_tensor(onehot[:, j % 2, :, :], bc(iota_lo[:, :], 1, QUAD), bc(dst_lo[:, t], 2, P),
                                            ALU.is_equal).then_inc(hot_ready, 1)
                            v.wait_ge(gathered[j], i * (16 * QUAD) + 16 * QUAD * (ROUNDS * s + 1))
                            for w in range(wide):
                                at = (j * wide + w) % 2
                                units = i * (SLOTS * wide)
                                u = wide * (QUADS * s + j) + w
                                ue = wide * (QUADS * l + j) + w
                                if l < 0:
                                    wait(v, scattered, units + (u - 1))
                                else:
                                    wait(v, msg_ready, units + (ue - 1))
                                V.tensor_tensor(masked[:, at, :, :, :], bc(rows[:, j, :, :], 2, 2),
                                                bc(by_block[:, t, 2 * w:2 * w + 2], 3, D), ALU.mult)\
                                 .then_inc(masked_ready, 1)
                                if l < 0:
                                    continue
                                if w == 0:
                                    v.wait_ge(e_ready, i * SLOTS + (QUADS * l + j + 1))
                                v.wait_ge(masked_ready, units + (u + 1))
                                wait(v, scattered, units + (u - 1))
                                V.tensor_tensor(msg[:, at, :, :, :], masked[:, at, :, :, :],
                                                e_ps[:, j % 2, :].rearrange("p (k w d) -> p k w d", k=QUAD, w=2),
                                                ALU.mult).then_inc(msg_ready, 1)

                    rounds(v, quads, s == 0 or l == 0)
                    v.wait_ge(scattered, wide * QUADS * (s + 1))

                by_block = near if wide == 1 else masks

                def clear():
                    give(V.memset(agg_ps[:, :], 0.0), cleared)

                def take_agg(to):
                    for b0, n, view in agg_view():
                        link(V.tensor_copy(to[:, b0:b0 + n, :], view))
                    if wide == 1:
                        for k in range(3):
                            b = 7 * (k + 1)
                            link(V.tensor_tensor(to[:, b, :], to[:, b, :],
                                                 agg_ps[:, k * BANK + 7 * D:k * BANK + 8 * D], ALU.add))

                def projection(s):
                    v.wait_ge(projected, s + 1)
                    return agg_ps[:, 0:NB * D].rearrange("p (b d) -> p b d", d=D)

                def gathered_stages():
                    norm(H[:, :, :], X[:, :, :], S0[:, :, :], True, table_due)
                    for s in range(3):
                        clear()
                        edges(s, -1)
                        link(V.tensor_copy(cat[:, :, 0:D], H[:, :, :]))
                        take_agg(S0)
                        give(V.tensor_tensor(cat[:, :, D:2 * D], S0[:, :, :], per_node(rdeg[:, :]), ALU.mult), node_in)
                        clear()
                        y = projection(s)
                        ins = V.tensor_tensor(H[:, :, :], y, bc(Bp[:, s, :], 1, NB), ALU.add)
                        give(ins, table_due) if s == 0 else link(ins)
                        if s == 2:
                            link(V.tensor_scalar(H[:, :, :], H[:, :, :], 0.0, None, ALU.max))
                        if s:
                            link(V.tensor_tensor(X[:, :, :], X[:, :, :], H[:, :, :], ALU.add))
                            norm(H[:, :, :], X[:, :, :], S0[:, :, :], True, table_due if s == 1 else None)

                    for w in range(2 * wide):
                        link(V.tensor_copy(cmp[:, :], masks[:, :, w]))
                        link(V.tensor_tensor(masks[:, :, w], cmp[:, :], not_loop[:, :], ALU.mult))
                    link(V.tensor_copy(cat[:, :, 0:D], H[:, :, :]))
                    for i in range(3):
                        s = 3 + i
                        give(V.tensor_tensor(H[:, :, :], cat[:, :, 0:D], per_node(dinv[:, :]), ALU.mult), table_due)
                        clear()
                        edges(s, -1)
                        take_agg(S0)
                        give(V.tensor_tensor(cat[:, :, D:2 * D], S0[:, :, :], per_node(ndinv[:, :]), ALU.mult), node_in)
                        clear()
                        y = projection(s)
                        link(V.tensor_tensor(own, y, bc(Bp[:, s, :], 1, NB), ALU.add))
                        link(V.tensor_tensor(own, own, per_node(real[:, :]), ALU.mult))
                        link(V.tensor_reduce(stat[:, 2, :], own, AX.X, ALU.add))
                        norm_all(i, own, neighbours)
                        if i == 0:
                            link(V.tensor_copy(X1[:, :, :], cat[:, :, 0:D]))
                        if i == 1:
                            link(V.tensor_scalar(cat[:, :, 0:D], cat[:, :, 0:D], 0.0, None, ALU.max))

                if wide == 1:
                    count_edges()
                    dense_stages()
                else:
                    v.wait_ge(loaded, ALL_IN)
                    hidden_weights()
                    gathered_degrees()
                    gathered_stages()
                link(V.tensor_tensor(neighbours, X1[:, :, :], own, ALU.add))
                link(V.tensor_scalar(neighbours, neighbours, 0.5, 0.0, ALU.mult, ALU.max))
                link(V.tensor_tensor(X[:, :, :], X[:, :, :], neighbours, ALU.add))
                normed = rows_buf[:, :].rearrange("p (b d) -> p b d", d=D)

                def take_rows(l, j):
                    scale = RW[:, l:l + 1]
                    if wide > 1:
                        b = slice(*CHUNKS[j])
                        sums = agg_ps[:, b.start * D:b.stop * D].rearrange("p (b d) -> p b d", d=D)
                        link(V.scalar_tensor_tensor(H[:, b, :], sums, scale, X1[:, b, :], ALU.mult, ALU.add))
                        return
                    for k in ((0, 1), (2,), (3,))[j]:
                        b0, n, view = agg_view()[k]
                        link(V.scalar_tensor_tensor(H[:, b0:b0 + n, :], view, scale, X1[:, b0:b0 + n, :],
                                                    ALU.mult, ALU.add))
                        if k:
                            before = agg_ps[:, (k - 1) * BANK + 7 * D:k * BANK]
                            link(V.scalar_tensor_tensor(H[:, b0, :], before, scale, H[:, b0, :], ALU.mult, ALU.add))

                def leaky(l, u):
                    _, n = dims(u)
                    v.wait_ge(hid_z_ready, UNITS * l + u + 1)
                    V.scalar_tensor_tensor(hid[:, u % QUAD, 0:n * P], hid_z[:, u % 2, 0:n * P], 0.1,
                                           hid_z[:, u % 2, 0:n * P], ALU.mult, ALU.max).then_inc(hid_ready, 1)

                def norm_rows(k, of, relu, take):
                    cut = [slice(b0, b1) for b0, b1 in CHUNKS]

                    def total(j):
                        take(j)
                        link(V.tensor_reduce(stat[:, 0, cut[j]], of[:, cut[j], :], AX.X, ALU.add))

                    def centre(j):
                        c = cut[j]
                        V.scalar_tensor_tensor(neighbours[:, c, :], per_node(stat[:, 0, c]), -1.0 / D, of[:, c, :],
                                               ALU.mult, ALU.add).then_inc(square_in, 1)

                    def power(j):
                        c = cut[j]
                        v.wait_ge(squared, len(cut) * k + j + 1)
                        V.tensor_reduce(stat[:, 1, c], own[:, c, :], AX.X, ALU.add).then_inc(power_in, 1)
                        if relu:
                            link(V.tensor_scalar(neighbours[:, c, :], neighbours[:, c, :], 0.0, None, ALU.max))

                    def scale(j):
                        c = cut[j]
                        v.wait_ge(power_rooted, len(cut) * k + j + 1)
                        link(V.reciprocal(stat[:, 1, c], stat[:, 1, c]))
                        V.tensor_tensor(normed[:, c, :], neighbours[:, c, :], per_node(stat[:, 1, c]),
                                        ALU.mult).then_inc(rows_in, 1)

                    total(0)
                    centre(0)
                    total(1)
                    power(0)
                    centre(1)
                    scale(0)
                    total(2)
                    power(1)
                    centre(2)
                    scale(1)
                    if k < LAYERS and not relu:
                        leaky(k, 0)
                    power(2)
                    scale(2)

                norm_rows(0, X[:, :, :], True, lambda j: None)
                if wide == 1:
                    hidden_weights()


                def rows_done(l, k):
                    b = slice(8 * k, min(8 * k + 8, NB))
                    v.wait_ge(rows_projected, (UNITS + 1) // 2 * l + k + 1)
                    return V.tensor_tensor(H[:, b, :], agg_ps[:, b.start * D:b.stop * D].rearrange("p (b d) -> p b d", d=D),
                                           bc(B2[:, l, :], 1, b.stop - b.start), ALU.add)

                for l in range(LAYERS):
                    s = l if wide == 1 else DENSE + l
                    for u in range(1 if l else 0, UNITS):
                        leaky(l, u)
                        if u == 4:
                            rows_done(l, 0)
                    rows_done(l, 1).then_inc(early_due, 1)
                    rows_done(l, 2)
                    give(rows_done(l, 3), table_due)
                    if l == 0:
                        edge_weights()
                    clear()
                    v.wait_ge(rows_in, len(CHUNKS) * (l + 1))
                    if l == 0:
                        link(V.tensor_copy(X1[:, :, :], normed))
                    else:
                        link(V.tensor_tensor(X1[:, :, :], normed, bc(LG[:, l - 1, :], 1, NB), ALU.mult))
                        link(V.tensor_tensor(X1[:, :, :], X1[:, :, :], bc(LB[:, l - 1, :], 1, NB), ALU.add))
                    if l == 0 and wide > 1:
                        for w in range(2 * wide):
                            link(V.tensor_scalar(masks[:, :, w], dst_hi[:, :], float(w), None, ALU.is_equal))
                    edges(s, l)
                    norm_rows(l + 1, H[:, :, :], False, lambda j: take_rows(l, j))
                v.wait_ge(rows_in, len(CHUNKS) * (LAYERS + 1))
                link(V.tensor_tensor(X1[:, :, :], normed, bc(LG[:, LAYERS - 1, :], 1, NB), ALU.mult))
                link(V.tensor_tensor(X1[:, :, :], X1[:, :, :], bc(LB[:, LAYERS - 1, :], 1, NB), ALU.add))
                V.tensor_tensor(X[:, :, :], X[:, :, :], X1[:, :, :], ALU.add).then_inc(out_due, 1)

            branch(v, program)


_OUTS = [((3125, 64), "float32")]


def kernel(**inputs):
    import numpy as np
    import concourse.bacc as bacc
    from concourse import mybir as mb
    from concourse.bass_utils import run_bass_kernel_spmd as run

    a = {k: np.asarray(v) for k, v in inputs.items()}
    pad = EPAD - EDGES
    src = np.concatenate([a["src"].astype(np.int32), np.full(pad, NODES, np.int32)])
    dst = np.concatenate([a["dst"].astype(np.int32), np.full(pad, NODES, np.int32)])
    attr_t = np.zeros((ED, EPAD), np.float32)
    attr_t[:, :EDGES] = a["edge_attr_32"].T
    arrays = {
        "x": a["x"], "src_t": src.reshape(TILES, P).T, "dst_t": dst.reshape(TILES, P).T,
        "dst_r": dst.reshape(ROWS, 4 * P), "attr_t": attr_t,
        "w_self1": a["L0_gnn_W_self1"], "w_neigh1": a["L0_gnn_W_neigh1"], "b_1": a["L0_gnn_b1"],
        "w_self2": a["L0_gnn_W_self2"], "w_neigh2": a["L0_gnn_W_neigh2"], "b_2": a["L0_gnn_b2"],
        "w_l": a["L1_gnn_W_l"], "w_r": a["L1_gnn_W_r"], "b_m": a["L1_gnn_b"],
        "w0_t": a["L2_gnn_W0"].transpose(0, 2, 1), "w1_t": a["L2_gnn_W1"].transpose(0, 2, 1),
        "b_c": a["L2_gnn_b"], "gamma": a["L2_gnn_gamma"], "beta": a["L2_gnn_beta"],
        "w1": a["L3_gnn_W1"], "b1_t": a["L3_gnn_b1"].T, "w2": a["L3_gnn_W2"], "b2": a["L3_gnn_b2"],
        "we1": a["L3_gnn_We1"], "be1_t": a["L3_gnn_be1"].T, "we2": a["L3_gnn_We2"], "be2": a["L3_gnn_be2"],
        "res_w": a["L3_gnn_res_w"], "dot_scale": a["L3_gnn_dot_scale"], "ln_g": a["L3_gnn_ln_g"],
        "ln_b": a["L3_gnn_ln_b"], "ln_g_t": a["L3_gnn_ln_g"].T, "ln_b_t": a["L3_gnn_ln_b"].T,
    }
    nc = bacc.Bacc("TRN2", target_bir_lowering=False, num_devices=1)
    args = []
    for name, v in arrays.items():
        arrays[name] = v = np.ascontiguousarray(v)
        args.append(nc.dram_tensor(name, v.shape, mb.dt.from_np(v.dtype), kind="ExternalInput").ap())
    for i, (shape, dtype) in enumerate(_OUTS):
        args.append(nc.dram_tensor(f"out_{i}", shape, mb.dt.from_np(np.dtype(dtype)), kind="ExternalOutput").ap())
    gnn_program(nc, *args)
    got = run(nc, [arrays], core_ids=[0])
    return got.results[0]["out_0"]
```
